# Optimizing a Trainium2 kernel written in Bass

```python
import numpy as np
import jax
import jax.numpy as jnp

def _softmax(x, axis=-1):
    return jax.nn.softmax(x, axis=axis)

def _gelu(x):
    return jax.nn.gelu(x, approximate=True)

def _silu(x):
    return jax.nn.silu(x)

def _sigmoid(x):
    return jax.nn.sigmoid(x)

def _layernorm(x, axis=-1, eps=1e-05):
    m = jnp.mean(x, axis=axis, keepdims=True)
    v = jnp.var(x, axis=axis, keepdims=True)
    return (x - m) / jnp.sqrt(v + eps)

def _scatter_add(tgt, idx, src, axis=0):
    return tgt.at[idx].add(src)

def _segment_sum(src, seg, n):
    return jax.ops.segment_sum(src, seg, n)
kernel_name = 'mk_recurrent_d1_jaxref_r4_b70172'

def setup_inputs(seed: int=0):
    np.random.seed(seed)
    _w = jnp.asarray

    def _L0_attn_setup():
        import jax, jax.numpy as jnp
        import numpy as np
        NUM_HEADS = 16
        key = jax.random.key(seed)
        ks = jax.random.split(key, 11)
        B, S, D = (4, 256, 256)
        M = 128
        hd = D // NUM_HEADS
        s = 0.02
        return {'x': jax.random.normal(ks[0], (B, S, D), jnp.float32), 'Wq': jax.random.normal(ks[1], (D, D), jnp.float32) * s, 'bq': jax.random.normal(ks[2], (D,), jnp.float32) * s, 'Wk': jax.random.normal(ks[3], (D, D), jnp.float32) * s, 'bk': jax.random.normal(ks[4], (D,), jnp.float32) * s, 'Wv': jax.random.normal(ks[5], (D, D), jnp.float32) * s, 'bv': jax.random.normal(ks[6], (D,), jnp.float32) * s, 'Wo': jax.random.normal(ks[7], (D, D), jnp.float32) * s, 'bo': jax.random.normal(ks[8], (D,), jnp.float32) * s, 'rel_k': jax.random.normal(ks[9], (2 * M + 1, hd), jnp.float32), 'rel_v': jax.random.normal(ks[10], (2 * M + 1, hd), jnp.float32)}
    _L0_attn_in = _L0_attn_setup()

    def _L0_ffn_setup():
        import jax, jax.numpy as jnp
        import numpy as np
        D = 256
        H = 1024
        E = 8
        B, N = (2, 512)
        key = jax.random.key(seed)
        ks = jax.random.split(key, 5)
        x = jax.random.normal(ks[0], (B, N, D), dtype=jnp.float32)
        W1 = jax.random.normal(ks[1], (E, D, H), dtype=jnp.float32) / np.sqrt(D)
        W2 = jax.random.normal(ks[2], (E, H, D), dtype=jnp.float32) / np.sqrt(H)
        Wg = jax.random.normal(ks[3], (D, E), dtype=jnp.float32) / np.sqrt(D)
        bg = jax.random.normal(ks[4], (E,), dtype=jnp.float32) * 0.01
        return {'x': x, 'W1': W1, 'W2': W2, 'Wg': Wg, 'bg': bg}
    _L0_ffn_in = _L0_ffn_setup()
    _d = {'L0_attn_x': _L0_attn_in['x'], 'L0_attn_Wq': _L0_attn_in['Wq'], 'L0_attn_bq': _L0_attn_in['bq'], 'L0_attn_Wk': _L0_attn_in['Wk'], 'L0_attn_bk': _L0_attn_in['bk'], 'L0_attn_Wv': _L0_attn_in['Wv'], 'L0_attn_bv': _L0_attn_in['bv'], 'L0_attn_Wo': _L0_attn_in['Wo'], 'L0_attn_bo': _L0_attn_in['bo'], 'L0_attn_rel_k': _L0_attn_in['rel_k'], 'L0_attn_rel_v': _L0_attn_in['rel_v'], 'L0_ffn_W1': _L0_ffn_in['W1'], 'L0_ffn_W2': _L0_ffn_in['W2'], 'L0_ffn_Wg': _L0_ffn_in['Wg'], 'L0_ffn_bg': _L0_ffn_in['bg']}
    _x0 = _d['L0_attn_x']
    _d['L0_attn_x'] = jax.random.normal(jax.random.fold_in(jax.random.key(seed), 1), (2, 2048, 256), dtype=_x0.dtype)
    del _x0
    return _d

def reference(L0_attn_x, L0_attn_Wq, L0_attn_bq, L0_attn_Wk, L0_attn_bk, L0_attn_Wv, L0_attn_bv, L0_attn_Wo, L0_attn_bo, L0_attn_rel_k, L0_attn_rel_v, L0_ffn_W1, L0_ffn_W2, L0_ffn_Wg, L0_ffn_bg):

    def _L0_attn_ref(x, Wq, bq, Wk, bk, Wv, bv, Wo, bo, rel_k, rel_v):
        import jax, jax.numpy as jnp
        import numpy as np
        NUM_HEADS = 16
        B, S, D = x.shape
        H = NUM_HEADS
        hd = D // H
        M = (rel_k.shape[0] - 1) // 2

        def proj(W, b):
            return (x @ W.T + b).reshape(B, S, H, hd).transpose(0, 2, 1, 3)
        q = proj(Wq, bq)
        k = proj(Wk, bk)
        v = proj(Wv, bv)
        r = jnp.arange(S)
        idx = jnp.clip(r[None, :] - r[:, None], -M, M) + M
        rpk = rel_k[idx]
        rpv = rel_v[idx]
        content = jnp.einsum('bhqd,bhkd->bhqk', q, k)
        relative = jnp.einsum('bhqd,qkd->bhqk', q, rpk)
        scores = (content + relative) / jnp.sqrt(jnp.float32(hd))
        w = jax.nn.softmax(scores, axis=-1)
        out = jnp.einsum('bhqk,bhkd->bhqd', w, v) + jnp.einsum('bhqk,qkd->bhqd', w, rpv)
        out = out.transpose(0, 2, 1, 3).reshape(B, S, D)
        return out @ Wo.T + bo

    def _L0_ffn_ref(x, W1, W2, Wg, bg):
        import jax, jax.numpy as jnp
        import numpy as np
        D = 256
        H = 1024
        E = 8
        B, N = (2, 512)
        b, n, d = x.shape
        e = Wg.shape[1]
        xf = x.reshape(b * n, d)
        logits = xf @ Wg + bg
        one_hot = jax.nn.one_hot(jnp.argmax(logits, axis=-1), e, dtype=x.dtype)
        h = jax.nn.gelu(jnp.einsum('td,edh->eth', xf, W1), approximate=True)
        y = jnp.einsum('eth,ehd->etd', h, W2)
        out = jnp.einsum('etd,te->td', y, one_hot)
        return out.reshape(b, n, d)
    x = L0_attn_x
    xn = _layernorm(x, axis=-1)
    s = _L0_attn_ref(xn, L0_attn_Wq, L0_attn_bq, L0_attn_Wk, L0_attn_bk, L0_attn_Wv, L0_attn_bv, L0_attn_Wo, L0_attn_bo, L0_attn_rel_k, L0_attn_rel_v)
    g = _silu(_L0_ffn_ref(xn, L0_ffn_W1, L0_ffn_W2, L0_ffn_Wg, L0_ffn_bg))
    x = x + s * g
    return x

_drawn_inputs = setup_inputs


def setup_inputs(seed=0):
    import zlib

    import numpy as np

    out = dict(_drawn_inputs(seed))
    spreads = {}
    factors = {'L0_attn_Wq': 4.998,
     'L0_attn_bq': 8.0,
     'L0_attn_Wk': 8.0,
     'L0_attn_bk': 64.0,
     'L0_attn_Wv': 8.0,
     'L0_attn_bv': 25.07,
     'L0_attn_bo': 7.984,
     'L0_attn_rel_k': 4.4,
     'L0_ffn_bg': 7.518}
    for name, (base, spread) in spreads.items():
        noise = np.random.default_rng([zlib.crc32(name.encode()), seed]).standard_normal(out[name].shape)
        drawn = base * np.exp(spread * noise) if base else spread * noise
        out[name] = jnp.asarray(drawn.astype(out[name].dtype))
    for name, factor in factors.items():
        out[name] = (out[name] * factor).astype(out[name].dtype)
    return out
```

```python
from contextlib import ExitStack

import concourse.bass as bass
from concourse import mybir

F32 = mybir.dt.float32
BF16 = mybir.dt.bfloat16
I32 = mybir.dt.int32
ALU = mybir.AluOpType
ACT = mybir.ActivationFunctionType
AX_X = mybir.AxisListType.X

P = 128
B, S, D = 2, 2048, 256
HEADS, HD = 16, 16
NBH = HEADS * B
NB = S // P
TILES = B * S // P
DC = D // P
M = 128
NE, FF = 8, 1024
FC = FF // P
XT = TILES + NE
EPS = 1e-5
SCALE = HD ** -0.5
LOWEST = -3.0e38

QTERM = (0, 0, 0, 1, 1, 2)
KTERM = (0, 1, 2, 0, 1, 0)
ROWS = len(QTERM) * HD
SHIFTS = 6
ALLROWS = ROWS + SHIFTS

BAND = 3 * P
WIN = 4 * P
NEARW = 2 * M
CH = 4
CW = S // CH

LAG_R = 14
LAG_T = 18


def order(s):
    return s // CH + CH * (s % CH)


def band_blocks(i):
    return [j for j in (i - 1, i, i + 1) if 0 <= j < NB]


def runs(blocks):
    out = []
    for b in blocks:
        if out and out[-1][0] + out[-1][1] == b:
            out[-1][1] += 1
        else:
            out.append([b, 1])
    return out


def wait(eng, sem, value):
    if not (isinstance(value, int) and value <= 0):
        eng.wait_ge(sem, value)


def chain(eng, sem):
    count = [0]

    def link(ins):
        count[0] += 1
        ins.then_inc(sem, 1)
        eng.wait_ge(sem, count[0])

    return link


def project(nc, io, dram, con, x_all, lg_all):
    with ExitStack() as ctx:
        def sb(name, shape, dt):
            return ctx.enter_context(nc.sbuf_tensor(name, shape, dt))

        def sem(name):
            return ctx.enter_context(nc.semaphore(name))

        wq = sb("wq", [P, DC, D], F32)
        wk = sb("wk", [P, DC, D], F32)
        wvg = sb("wvg", [P, DC, D + NE], F32)
        bqk = sb("bqk", [P, 2, DC], F32)
        bvg = sb("bvg", [P, D + NE], F32)
        stats = sb("stats", [P, TILES, 6], F32)
        mean = sb("mean", [P, TILES], F32)
        var = sb("var", [P, TILES], F32)
        std = sb("std", [P, TILES], F32)
        rstd = sb("rstd", [P, TILES], F32)
        tmp = sb("tmp", [P, TILES], F32)
        xr = [sb(f"xr{h}", [P, 4, D], F32) for h in range(2)]
        xT = [sb(f"xT{h}", [P, DC, 4 * P], F32) for h in range(2)]
        qf = [sb(f"qf{u}", [P, 4 * P], F32) for u in range(4)]
        terms = [sb(f"terms{u}", [P, 3, 4 * P], BF16) for u in range(4)]
        v_all = sb("v_all", [P, HEADS, TILES, HD], F32)
        rkT = sb("rkT", [HD, 2 * M + 1], F32)
        rk_ext = sb("rk_ext", [HD, WIN], F32)
        rk_terms = sb("rk_terms", [HD, 3, WIN], BF16)
        zeros = sb("zeros", [P, D], F32)

        tp = [ctx.enter_context(nc.psum_tensor(f"tp{i}", [P, 512], F32)) for i in range(2)]
        pq = [ctx.enter_context(nc.psum_tensor(f"pq{i}", [P, 512], F32)) for i in range(2)]
        pv = [ctx.enter_context(nc.psum_tensor(f"pv{i}", [P, 512], F32)) for i in range(2)]

        x_in = [sem(f"x_in{i}") for i in range(4)]
        w_in = sem("w_in")
        rk_in = sem("rk_in")
        rk_split = sem("rk_split")
        rk_out = sem("rk_out")
        ident_set = sem("ident_set")
        zero_set = sem("zero_set")
        pads_out = sem("pads_out")
        stats_done = sem("stats_done")
        var_ready = sem("var_ready")
        std_ready = sem("std_ready")
        norm_link = sem("norm_link")
        xn_ready = sem("xn_ready")
        tr_mm = sem("tr_mm")
        xT_evac = sem("xT_evac")
        qk_mm = sem("qk_mm")
        qk_evac = sem("qk_evac")
        split_link = sem("split_link")
        split_done = sem("split_done")
        stacked = [sem(f"stacked{u}") for u in range(4)]
        vg_mm = sem("vg_mm")
        vg_evac = sem("vg_evac")
        v_out = sem("v_out")

        x_v = io["x"].rearrange("b (t p) d -> p (b t) d", p=P)
        QT = TILES // 4
        CHUNKS = TILES // 4
        HALF = HEADS // DC

        with nc.Block() as block:

            @block.sync
            def _(sp):
                for q in range(4):
                    sp.dma_start(x_all[:, q * QT:(q + 1) * QT, :], x_v[:, q * QT:(q + 1) * QT, :]).then_inc(x_in[q], 16)
                for t, name in ((wq, "wqT"), (wk, "wkT")):
                    sp.dma_start(t[:, :, :], io[name].rearrange("(c p) n -> p c n", p=P)).then_inc(w_in, 16)
                sp.dma_start(wvg[:, :, 0:D], io["wvT"].rearrange("(c p) n -> p c n", p=P)).then_inc(w_in, 16)
                sp.dma_start(wvg[:, :, D:D + NE], io["wg"].rearrange("(c p) n -> p c n", p=P)).then_inc(w_in, 16)
                for k, name in enumerate(("bq", "bk")):
                    sp.dma_start(bqk[:, k, :], io[name]).then_inc(w_in, 16)
                sp.dma_start(bvg[:, 0:D], io["bv"].partition_broadcast(P)).then_inc(w_in, 16)
                sp.dma_start(bvg[:, D:D + NE], io["bg"].partition_broadcast(P)).then_inc(w_in, 16)
                sp.dma_start(rkT[:, :], io["rel_kT"]).then_inc(rk_in, 16)
                sp.wait_ge(zero_set, 1)
                for t in range(XT):
                    sp.dma_start(dram["xs"][t * P:(t + 1) * P, :], zeros[:, :]).then_inc(pads_out, 16)
                sp.wait_ge(rk_split, 3)
                for slot in range(len(KTERM)):
                    sp.dma_start(con["rel_k"][slot * HD:(slot + 1) * HD, :], rk_terms[:, KTERM[slot], :]).then_inc(rk_out, 16)

                with sp.Fori(0, CHUNKS // 2) as pair_i:
                    c0 = pair_i * 2
                    for half in range(2):
                        for u in range(4):
                            sp.wait_ge(split_done, c0 * 4 + half * 4 + u + 1)
                            tab = dram["q_stack"] if u < 2 else dram["k_stack"]
                            which = QTERM if u < 2 else KTERM
                            for slot in range(len(which)):
                                dst = tab[HALF * (u % 2):HALF * (u % 2 + 1), slot * HD:(slot + 1) * HD, bass.ds(c0 * 4 * P + half * 4 * P, 4 * P)]
                                sp.dma_start(dst, terms[u][:, which[slot], :]).then_inc(stacked[u], 16)
                for u in range(4):
                    sp.wait_ge(stacked[u], 16 * 6 * CHUNKS)
                sp.wait_ge(vg_evac, TILES)
                for n in range(NBH):
                    sp.dma_start(dram["v"][n], v_all[:, n // 2, NB * (n % 2):NB * (n % 2 + 1), :]).then_inc(v_out, 16)
                sp.wait_ge(v_out, 16 * NBH)
                sp.wait_ge(pads_out, 16 * XT)
                sp.wait_ge(rk_out, 16 * len(KTERM))

            @block.gpsimd
            def _(pool):
                pool.memset(zeros[:, :], 0.0).then_inc(zero_set, 1)
                pool.memset(con["ident"][:, :], 0.0).then_inc(ident_set, 1)
                pool.memset(con["ident_bf"][:, :], 0.0).then_inc(ident_set, 1)
                pool.wait_ge(ident_set, 2)
                for m in (con["ident"], con["ident_bf"]):
                    pool.affine_select(out=m[:, :], in_=m[:, :], compare_op=ALU.not_equal, fill=1.0, base=0,
                                       pattern=[[-1, P]], channel_multiplier=1).then_inc(ident_set, 1)

            @block.vector
            def _(dve):
                link = chain(dve, norm_link)
                dve.wait_ge(rk_in, 16)
                nc.vector.tensor_copy(rk_ext[:, P:P + 2 * M + 1], rkT[:, :])
                nc.vector.tensor_copy(rk_ext[:, 0:P], rkT[:, 0:1].to_broadcast([HD, P]))
                link(nc.vector.tensor_copy(rk_ext[:, P + 2 * M + 1:WIN], rkT[:, 2 * M:2 * M + 1].to_broadcast([HD, WIN - P - 2 * M - 1])))
                nc.vector.tensor_copy(rk_terms[:, 0, :], rk_ext[:, :]).then_inc(rk_split, 1)
                dve.wait_ge(rk_split, 1)
                link(nc.vector.tensor_tensor(rk_ext[:, :], rk_ext[:, :], rk_terms[:, 0, :], ALU.subtract))
                nc.vector.tensor_copy(rk_terms[:, 1, :], rk_ext[:, :]).then_inc(rk_split, 1)
                dve.wait_ge(rk_split, 2)
                nc.vector.tensor_tensor(rk_terms[:, 2, :], rk_ext[:, :], rk_terms[:, 1, :], ALU.subtract).then_inc(rk_split, 1)

                for q in range(4):
                    dve.wait_ge(x_in[q], 16)
                    with dve.Fori(0, QT) as t:
                        nc.vector.bn_stats(stats[:, t + q * QT, :], x_all[:, t + q * QT, :]).then_inc(stats_done, 1)
                dve.wait_ge(stats_done, TILES)
                me, mo = stats[:, :, 1], stats[:, :, 4]
                nc.vector.tensor_tensor(mean[:, :], me, mo, ALU.add)
                nc.vector.tensor_tensor(tmp[:, :], me, mo, ALU.subtract)
                link(nc.vector.tensor_tensor(var[:, :], stats[:, :, 2], stats[:, :, 5], ALU.add))
                nc.vector.tensor_scalar(mean[:, :], mean[:, :], 0.5, None, ALU.mult)
                nc.vector.tensor_scalar(var[:, :], var[:, :], 1.0 / D, EPS, ALU.mult, ALU.add)
                link(nc.vector.tensor_scalar(tmp[:, :], tmp[:, :], 0.5, None, ALU.mult))
                link(nc.vector.tensor_tensor(tmp[:, :], tmp[:, :], tmp[:, :], ALU.mult))
                nc.vector.tensor_tensor(var[:, :], var[:, :], tmp[:, :], ALU.add).then_inc(var_ready, 1)
                dve.wait_ge(std_ready, 1)
                link(nc.vector.reciprocal(rstd[:, :], std[:, :]))
                link(nc.vector.tensor_tensor(tmp[:, :], rstd[:, :], rstd[:, :], ALU.mult))
                link(nc.vector.tensor_tensor(tmp[:, :], tmp[:, :], var[:, :], ALU.mult))
                link(nc.vector.tensor_scalar(tmp[:, :], tmp[:, :], -0.5, 1.5, ALU.mult, ALU.add))
                link(nc.vector.tensor_tensor(rstd[:, :], rstd[:, :], tmp[:, :], ALU.mult))
                dve.wait_ge(w_in, 16 * 8)

                def chunk(c, half, c_first):
                    for k in range(4):
                        if k == 0 and not c_first:
                            dve.wait_ge(tr_mm, c * 4 - 4)
                        t = c * 4 + k
                        nc.vector.tensor_scalar(xr[half][:, k, :], x_all[:, t, :], mean[:, bass.ds(t, 1)], rstd[:, bass.ds(t, 1)],
                                                ALU.subtract, ALU.mult).then_inc(xn_ready, 1)
                        nc.vector.tensor_scalar(x_all[:, t, :], x_all[:, t, :], mean[:, bass.ds(t, 1)], rstd[:, bass.ds(t, 1)],
                                                ALU.subtract, ALU.mult)
                    for u in range(4):
                        n = c * 4 + u
                        dve.wait_ge(qk_evac, n + 1)
                        nc.vector.tensor_tensor(qf[u][:, :], qf[u][:, :], terms[u][:, 0, :], ALU.subtract).then_inc(split_link, 1)
                        dve.wait_ge(split_link, n * 2 + 1)
                        nc.vector.tensor_copy(terms[u][:, 1, :], qf[u][:, :]).then_inc(split_link, 1)
                        dve.wait_ge(split_link, n * 2 + 2)
                        nc.vector.tensor_tensor(terms[u][:, 2, :], qf[u][:, :], terms[u][:, 1, :], ALU.subtract).then_inc(split_done, 1)
                    for k in range(4):
                        t = c * 4 + k
                        dve.wait_ge(vg_mm, t + 1)
                        nc.vector.tensor_tensor(v_all[:, :, bass.ds(t, 1), :].rearrange("p h t d -> p h (t d)"),
                                                pv[k % 2][:, 0:D].rearrange("p (h d) -> p h d", h=HEADS),
                                                bvg[:, 0:D].rearrange("p (h d) -> p h d", h=HEADS), ALU.add)
                        nc.vector.tensor_tensor(lg_all[:, bass.ds(t, 1), :].rearrange("p t e -> p (t e)"), pv[k % 2][:, D:D + NE],
                                                bvg[:, D:D + NE], ALU.add).then_inc(vg_evac, 1)

                chunk(0, 0, True)
                chunk(1, 1, True)
                with dve.Fori(1, CHUNKS // 2) as pair_i:
                    c0 = pair_i * 2
                    chunk(c0, 0, False)
                    chunk(c0 + 1, 1, False)

            @block.scalar
            def _(act):
                act.wait_ge(var_ready, 1)
                nc.scalar.activation(std[:, :], var[:, :], ACT.Sqrt).then_inc(std_ready, 1)
                act.wait_ge(w_in, 16 * 8)

                def chunk(c, half, c_first):
                    for k in range(4):
                        if k == 0 and not c_first:
                            act.wait_ge(vg_mm, c * 4 - 4)
                        act.wait_ge(tr_mm, c * 4 + k + 1)
                        nc.scalar.activation(xT[half][:, :, k * P:(k + 1) * P], tp[k % 2][:, 0:D].rearrange("p (c m) -> p c m", c=DC),
                                             ACT.Copy).then_inc(xT_evac, 1)
                    for u in range(4):
                        act.wait_ge(qk_mm, c * 4 + u + 1)
                        if not (isinstance(c, int) and c == 0):
                            act.wait_ge(stacked[u], c * 96)
                        bias = bqk[:, u // 2, u % 2:u % 2 + 1]
                        nc.scalar.activation(qf[u][:, :], pq[u % 2][:, :], ACT.Identity, bias=bias)
                        nc.scalar.activation(terms[u][:, 0, :], pq[u % 2][:, :], ACT.Identity, bias=bias).then_inc(qk_evac, 1)

                chunk(0, 0, True)
                chunk(1, 1, True)
                with act.Fori(1, CHUNKS // 2) as pair_i:
                    c0 = pair_i * 2
                    chunk(c0, 0, False)
                    chunk(c0 + 1, 1, False)

            @block.tensor
            def _(pe):
                pe.wait_ge(ident_set, 4)
                pe.wait_ge(w_in, 16 * 8)

                def chunk(c, half, c_first):
                    for k in range(4):
                        pe.wait_ge(xn_ready, c * 4 + k + 1)
                        wait(pe, xT_evac, c * 4 + k - 1)
                        for d in range(DC):
                            mm = nc.tensor.transpose(tp[k % 2][:, d * P:(d + 1) * P], xr[half][:, k, d * P:(d + 1) * P], con["ident"][:, :])
                        mm.then_inc(tr_mm, 1)
                    pe.wait_ge(xT_evac, c * 4 + 4)
                    for u in range(4):
                        w = wq if u < 2 else wk
                        wait(pe, qk_evac, c * 4 + u - 1)
                        for d in range(DC):
                            mm = nc.tensor.matmul(pq[u % 2][:, :], w[:, d, (u % 2) * P:(u % 2 + 1) * P], xT[half][:, d, :],
                                                  start=(d == 0), stop=(d == DC - 1))
                        mm.then_inc(qk_mm, 1)
                    for k in range(4):
                        wait(pe, vg_evac, c * 4 + k - 1)
                        for d in range(DC):
                            mm = nc.tensor.matmul(pv[k % 2][:, 0:D + NE], xT[half][:, d, k * P:(k + 1) * P], wvg[:, d, :],
                                                  start=(d == 0), stop=(d == DC - 1))
                        mm.then_inc(vg_mm, 1)

                chunk(0, 0, True)
                chunk(1, 1, True)
                with pe.Fori(1, CHUNKS // 2) as pair_i:
                    c0 = pair_i * 2
                    chunk(c0, 0, False)
                    chunk(c0 + 1, 1, False)


def route(nc, dram, con, x_all, lg_all, pos_i, expert_i):
    with ExitStack() as ctx:
        def sb(name, shape, dt):
            return ctx.enter_context(nc.sbuf_tensor(name, shape, dt))

        def sem(name):
            return ctx.enter_context(nc.semaphore(name))

        iota_i = sb("iota_i", [P, XT], I32)
        iota_f = sb("iota_f", [P, XT], F32)
        iota_e = sb("iota_e", [P, NE], F32)
        iota_c = sb("iota_c", [P, TILES], F32)
        before = sb("before", [P, P], BF16)
        ones = sb("ones", [P, P], BF16)
        top = sb("top", [P, TILES], F32)
        eq = sb("eq", [P, TILES, NE], F32)
        pick = sb("pick", [P, TILES], F32)
        oh = sb("oh", [P, TILES, NE], BF16)
        tot = sb("tot", [P, TILES, NE], F32)
        cum = [sb(f"cum{i}", [P, TILES, NE], F32) for i in range(2)]
        base = sb("base", [P, TILES, NE], F32)
        more = sb("more", [P, NE, TILES], F32)
        nt = sb("nt", [P, NE], F32)
        end = [sb(f"end{i}", [P, NE], F32) for i in range(2)]
        first = sb("first", [P, NE], F32)
        posf = sb("posf", [P, TILES], F32)
        past = sb("past", [P, XT, NE], F32)
        expf = sb("expf", [P, XT], F32)
        pr = ctx.enter_context(nc.psum_tensor("pr", [P, 2, TILES * NE], F32))

        iota_set = sem("iota_set")
        tri_set = sem("tri_set")
        link_sem = sem("route_link")
        oh_ready = sem("oh_ready")
        counts_mm = sem("counts_mm")
        pos_ready = sem("pos_ready")
        sorted_out = sem("sorted_out")

        with nc.Block() as block:

            @block.gpsimd
            def _(pool):
                pool.iota(iota_i[:, :], pattern=[[1, XT]], base=0, channel_multiplier=0).then_inc(iota_set, 1)
                pool.memset(ones[:, :], 1.0).then_inc(tri_set, 1)
                pool.memset(before[:, :], 1.0).then_inc(tri_set, 1)
                pool.wait_ge(tri_set, 2)
                pool.affine_select(out=before[:, :], in_=before[:, :], compare_op=ALU.is_gt, fill=0.0, base=0,
                                   pattern=[[1, P]], channel_multiplier=-1).then_inc(tri_set, 1)
                pool.wait_ge(pos_ready, 1)
                for t in range(TILES):
                    pool.indirect_dma_start(out=dram["xs"][:, :], out_offset=bass.IndirectOffsetOnAxis(ap=pos_i[:, t:t + 1], axis=0),
                                            in_=x_all[:, t, :], in_offset=None).then_inc(sorted_out, 16)
                pool.wait_ge(sorted_out, 16 * TILES)

            @block.tensor
            def _(pe):
                pe.wait_ge(tri_set, 3)
                pe.wait_ge(oh_ready, 1)
                ohv = oh[:, :, :].rearrange("p t e -> p (t e)")
                nc.tensor.matmul(pr[:, 0, :], before[:, :], ohv, start=True, stop=True)
                nc.tensor.matmul(pr[:, 1, :], ones[:, :], ohv, start=True, stop=True).then_inc(counts_mm, 1)

            @block.vector
            def _(dve):
                link = chain(dve, link_sem)
                v = nc.vector

                def over(ap, shape, axis):
                    return ap.unsqueeze(axis).to_broadcast(shape)

                TE = [P, TILES, NE]
                dve.wait_ge(iota_set, 1)
                link(v.tensor_copy(iota_f[:, :], iota_i[:, :]))
                v.tensor_scalar(iota_e[:, :], iota_f[:, 0:NE], -float(NE), None, ALU.add)
                v.tensor_scalar(iota_c[:, :], iota_f[:, 0:TILES], float(P), None, ALU.mult)
                link(v.tensor_reduce(top[:, :], lg_all[:, :, :], AX_X, ALU.max))
                link(v.tensor_tensor(eq[:, :, :], lg_all[:, :, :], over(top[:, :], TE, 2), ALU.is_ge))
                link(v.tensor_tensor(eq[:, :, :], eq[:, :, :], over(iota_e[:, :], TE, 1), ALU.mult))
                link(v.tensor_reduce(pick[:, :], eq[:, :, :], AX_X, ALU.min))
                v.tensor_tensor(oh[:, :, :], over(iota_e[:, :], TE, 1), over(pick[:, :], TE, 2), ALU.is_equal).then_inc(oh_ready, 1)
                dve.wait_ge(counts_mm, 1)
                v.tensor_copy(cum[0][:, :, :], pr[:, 1, :].rearrange("p (t e) -> p t e", e=NE))
                link(v.tensor_copy(tot[:, :, :], pr[:, 1, :].rearrange("p (t e) -> p t e", e=NE)))
                a = 0
                k = 1
                while k < TILES:
                    v.tensor_copy(cum[1 - a][:, 0:k, :], cum[a][:, 0:k, :])
                    link(v.tensor_tensor(cum[1 - a][:, k:, :], cum[a][:, k:, :], cum[a][:, 0:TILES - k, :], ALU.add))
                    a, k = 1 - a, 2 * k
                ET = [P, NE, TILES]
                link(v.tensor_tensor(more[:, :, :], over(cum[a][:, TILES - 1, :], ET, 2), over(iota_c[:, :], ET, 1), ALU.is_gt))
                link(v.tensor_reduce(nt[:, :], more[:, :, :], AX_X, ALU.add))
                link(v.tensor_copy(end[0][:, :], nt[:, :]))
                b, k = 0, 1
                while k < NE:
                    v.tensor_copy(end[1 - b][:, 0:k], end[b][:, 0:k])
                    link(v.tensor_tensor(end[1 - b][:, k:], end[b][:, k:], end[b][:, 0:NE - k], ALU.add))
                    b, k = 1 - b, 2 * k
                link(v.tensor_tensor(first[:, :], end[b][:, :], nt[:, :], ALU.subtract))
                link(v.tensor_scalar(first[:, :], first[:, :], float(P), None, ALU.mult))
                link(v.tensor_tensor(base[:, :, :], cum[a][:, :, :], tot[:, :, :], ALU.subtract))
                link(v.tensor_tensor(base[:, :, :], base[:, :, :], pr[:, 0, :].rearrange("p (t e) -> p t e", e=NE), ALU.add))
                link(v.tensor_tensor(base[:, :, :], base[:, :, :], over(first[:, :], TE, 1), ALU.add))
                link(v.tensor_tensor(base[:, :, :], base[:, :, :], oh[:, :, :], ALU.mult))
                link(v.tensor_reduce(posf[:, :], base[:, :, :], AX_X, ALU.add))
                v.tensor_copy(pos_i[:, :], posf[:, :]).then_inc(pos_ready, 1)
                XE = [P, XT, NE]
                link(v.tensor_tensor(past[:, :, :], over(iota_f[:, :], XE, 2), over(end[b][:, :], XE, 1), ALU.is_ge))
                link(v.tensor_reduce(expf[:, :], past[:, :, :], AX_X, ALU.add))
                link(v.tensor_scalar(expf[:, :], expf[:, :], float(NE - 1), None, ALU.min))
                v.tensor_copy(expert_i[:, :], expf[:, :]).then_inc(pos_ready, 1)


def attend(nc, io, dram, con, attn):
    with ExitStack() as ctx:
        def sb(name, shape, dt):
            return ctx.enter_context(nc.sbuf_tensor(name, shape, dt))

        def sem(name):
            return ctx.enter_context(nc.semaphore(name))

        def two(name, shape, dt):
            return [sb(f"{name}{i}", shape, dt) for i in range(2)]

        q_front = two("q_front", [ROWS, S], BF16)
        k_front = two("k_front", [ROWS, S], BF16)
        q_back = two("q_back", [ALLROWS, S], BF16)
        k_left = two("k_left", [ALLROWS, S], BF16)
        k_right = two("k_right", [ALLROWS, S], BF16)
        rel = two("rel", [P, CH, WIN], F32)
        band = two("band", [P, NB, BAND], F32)
        pwin = two("pwin", [P, CH, NEARW], F32)
        band_T = two("band_T", [P, CH, BAND], F32)
        pwin_T = two("pwin_T", [P, CH, NEARW], F32)
        clip_T = sb("clip_T", [P, CH, 2, P], F32)
        clip_mask = sb("clip_mask", [P, 2, P], F32)
        far_T = two("far_T", [P, CH, CW], F32)
        v_raw = sb("v_raw", [P, NB, HD], F32)
        v_far = [two(f"v_far{k}", [P, NB, 32], F32) for k in range(2)]
        v_near = two("v_near", [P, NB, 32], F32)
        rv_ends = sb("rv_ends", [P, 2, HD], F32)
        rv_win = sb("rv_win", [P, CH, 32], F32)
        part = two("part", [P, NB, 3, CH], F32)
        lm = sb("lm", [P, CH, 3], F32)
        rmax = two("rmax", [P, NB], F32)
        negm = two("negm", [P, NB], F32)
        rel_ends = two("rel_ends", [P, NB, 3], F32)
        sh = sb("sh", [P, CH, 2], F32)
        shb = two("shb", [P, CH, SHIFTS], BF16)
        outT = sb("outT", [P, CW], F32)
        rden = sb("rden", [P, NB], F32)
        zero = sb("zero", [P, CH, 2], F32)
        neg_scale = sb("neg_scale", [P, 1], F32)

        ps1 = [ctx.enter_context(nc.psum_tensor(f"ps1_{i}", [P, 512], F32)) for i in range(2)]
        pst = [ctx.enter_context(nc.psum_tensor(f"pst{i}", [P, 512], F32)) for i in range(2)]
        pout = ctx.enter_context(nc.psum_tensor("pout", [P, 512], F32))
        prel = ctx.enter_context(nc.psum_tensor("prel", [P, 512], F32))
        pband = ctx.enter_context(nc.psum_tensor("pband", [P, 512], F32))
        psmall = ctx.enter_context(nc.psum_tensor("psmall", [P, 512], F32))
        pnear = psmall[:, 0:NEARW]
        prow = psmall[0:SHIFTS, NEARW:512].bitcast(BF16)

        const_in = sem("const_in")
        const_set = sem("const_set")
        shift_set = sem("shift_set")
        qf_in = [sem(f"qf_in{i}") for i in range(2)]
        kf_in = [sem(f"kf_in{i}") for i in range(2)]
        back_in = [sem(f"back_in{i}") for i in range(2)]
        v_in = sem("v_in")
        v_built = sem("v_built")
        s1_mm = sem("s1_mm")
        s1_used = sem("s1_used")
        r_mm = sem("r_mm")
        r_evac = sem("r_evac")
        ends_done = sem("ends_done")
        rel_out = [sem(f"rel_out{r}") for r in range(4)]
        rel_in = [[sem(f"rel_in{p}{r}") for r in range(4)] for p in range(2)]
        max_link = sem("max_link")
        rmax_ready = sem("rmax_ready")
        negm_ready = sem("negm_ready")
        shift_link = sem("shift_link")
        shift_ready = sem("shift_ready")
        rows_tp = sem("rows_tp")
        rows_copied = sem("rows_copied")
        band_exp = sem("band_exp")
        prob_out = [sem(f"prob_out{r}") for r in range(4)]
        win_in = [sem(f"win_in{i}") for i in range(2)]
        st_mm = sem("st_mm")
        exp_done = sem("exp_done")
        pv_done = sem("pv_done")
        bandT_mm = sem("bandT_mm")
        bandT_evac = sem("bandT_evac")
        winT_mm = sem("winT_mm")
        winT_evac = sem("winT_evac")
        clip_ready = sem("clip_ready")
        clip_used = sem("clip_used")
        band_pv = sem("band_pv")
        out_evac = sem("out_evac")
        back_mm = sem("back_mm")
        den_ready = sem("den_ready")
        norm_done = sem("norm_done")

        class Step:

            def __init__(self, hb, off):
                self.dn, self.s = divmod(off, NB)
                self.hb = hb
                self.par = self.dn % 2
                self.head = hb + self.dn // 2
                self.n = hb * 2 + self.dn
                self.r, self.g = divmod(self.s, CH)
                self.valid = not isinstance(hb, int) or 0 <= self.n < NBH

            def count(self, per, more):
                return self.sum(2 * per, self.dn * per + more)

            def count2(self, per, more):
                return self.sum(per, self.dn // 2 * per + more)

            def sum(self, per, more):
                return self.hb * per + more if more else (self.hb - 1) * per + per

        def loop(eng, step):
            for off in range(-NB, 2 * NB):
                step(0, off)
            with eng.Fori(1, HEADS - 1) as hb:
                for off in range(2 * NB):
                    step(hb, off)
            for off in range(2 * NB + LAG_T + 3):
                step(HEADS - 1, off)

        def far_pieces(j, g):
            blocks = range(CH * g, CH * g + CH)
            out = []
            for right, sel in ((1, [i for i in blocks if i <= j - 2]), (0, [i for i in blocks if i >= j + 2])):
                if sel:
                    out.append((right, (sel[0] - CH * g) * P, (sel[-1] + 1 - CH * g) * P))
            return out

        with nc.Block() as block:

            @block.sync
            def _(sp):
                sp.dma_start(rv_ends[:, 0, :], io["rel_v"][0, :].partition_broadcast(P)).then_inc(const_in, 16)
                sp.dma_start(rv_ends[:, 1, :], io["rel_v"][2 * M, :].partition_broadcast(P)).then_inc(const_in, 16)
                sp.wait_ge(const_set, 1)
                sp.dma_start(rv_win[:, 0, 0:HD], io["rel_v"][0, :].partition_broadcast(P)).then_inc(const_in, 16)
                sp.dma_start(rv_win[:, 1, 0:HD], io["rel_v"][0:M, :]).then_inc(const_in, 16)
                sp.dma_start(rv_win[:, 2, 0:HD], io["rel_v"][M:2 * M, :]).then_inc(const_in, 16)
                sp.dma_start(rv_win[:, 3, 0:HD], io["rel_v"][2 * M, :].partition_broadcast(P)).then_inc(const_in, 16)
                sp.wait_ge(const_set, 20)

                def step(hb, off):
                    if off % NB == 0:
                        x = Step(hb, off + NB)
                        if x.valid:
                            wait(sp, s1_mm, x.count(64, -64))
                            sp.dma_start(q_front[x.par][:, :], pair_rows(q_tab, x)).then_inc(qf_in[x.par], 16)
                            sp.dma_start(k_front[x.par][:, :], pair_rows(k_tab, x)).then_inc(kf_in[x.par], 16)
                    if off % NB == 2:
                        x = Step(hb, off)
                        if x.valid:
                            wait(sp, st_mm, x.count(64, -64))
                            sp.dma_start(q_back[x.par][0:ROWS, :], pair_rows(q_tab, x)).then_inc(back_in[x.par], 16)
                            sp.dma_start(k_left[x.par][0:ROWS, :], pair_rows(k_tab, x)).then_inc(back_in[x.par], 16)
                            sp.dma_start(k_right[x.par][0:ROWS, :], pair_rows(k_tab, x)).then_inc(back_in[x.par], 16)
                            wait(sp, v_built, x.count(1, 0))
                            sp.dma_start(v_raw[:, :, :], v_tab[x.n]).then_inc(v_in, 16)
                    if off % CH != 1:
                        return
                    x = Step(hb, off + LAG_R - 3)
                    r = x.r
                    if x.valid:
                        sp.wait_ge(r_evac, x.count(16, 4 * r + 4))
                        wait(sp, rel_in[x.par][r], x.count2(32 if r in (0, 3) else 16, 0))
                        sp.dma_start(dram["rel"][x.par, 4 * r:4 * r + 4].rearrange("s p w -> p s w"), rel[r % 2][:, :, :]).then_inc(rel_out[r], 16)
                    y = Step(hb, off - 9)
                    if y.valid:
                        sp.wait_ge(band_exp, y.count(16, 4 * y.r + 4))
                        wait(sp, win_in[y.r % 2], y.count(32, 16 * (y.r // 2 + 1) - 32))
                        sp.dma_start(dram["band_p"][y.par, 4 * y.r:4 * y.r + 4].rearrange("s p w -> p s w"),
                                     band[y.par][:, 4 * y.r:4 * y.r + 4, :]).then_inc(prob_out[y.r], 16)
                    x = Step(hb, off + LAG_R - 7)
                    r = x.r
                    if x.valid:
                        sp.wait_ge(rel_out[r], x.count(16, 16))
                        wait(sp, bandT_mm, x.count(16, 4 * r + 4 - 32))
                        wait(sp, prob_out[r], x.count(16, -16))
                        s0, s1 = 4 * r + (r == 0), 4 * r + 4 - (r == 3)
                        sp.dma_start(band[x.par][:, s0:s1, :], sheared(dram["rel"], x.par, s0, s1 - s0, WIN, WIN - 1, P, BAND)).then_inc(rel_in[x.par][r], 16)
                        if r == 0:
                            sp.dma_start(band[x.par][:, 0, P:BAND], sheared(dram["rel"], x.par, 0, 1, WIN, WIN - 1, 2 * P, BAND - P)[:, 0, :]).then_inc(rel_in[x.par][r], 16)
                        if r == 3:
                            sp.dma_start(band[x.par][:, NB - 1, 0:BAND - P], sheared(dram["rel"], x.par, NB - 1, 1, WIN, WIN - 1, P, BAND - P)[:, 0, :]).then_inc(rel_in[x.par][r], 16)
                    z = Step(hb, off - 13)
                    if z.valid:
                        sp.wait_ge(prob_out[z.r], z.count(16, 16))
                        wait(sp, winT_mm, z.count(16, 4 * z.r + 4 - 8))
                        sp.dma_start(pwin[z.r % 2][:, :, :], sheared(dram["band_p"], z.par, 4 * z.r, 4, BAND, BAND + 1, 0, NEARW)).then_inc(win_in[z.r % 2], 16)

                q_tab, k_tab, v_tab = dram["q_stack"], dram["k_stack"], dram["v"]

                def pair_rows(t, x):
                    return t[x.head, :, x.par * S:(x.par + 1) * S]

                def sheared(t, par, s, count, width, step_p, first, length):
                    return bass.AP(tensor=t.tensor, offset=t.offset + (par * NB + s) * P * width + first,
                                   ap=[[step_p, P], [P * width, count], [1, length]])

                loop(sp, step)

            @block.gpsimd
            def _(pool):
                pool.memset(rv_win[:, :, :], 0.0).then_inc(const_set, 1)
                pool.memset(zero[:, :, :], 0.0).then_inc(const_set, 1)
                for p in range(2):
                    pool.memset(rel_ends[p][:, :, :], 0.0).then_inc(const_set, 1)
                    pool.memset(part[p][:, :, :, :], LOWEST).then_inc(const_set, 1)
                    pool.memset(band[p][:, 0, 0:P], 0.0).then_inc(const_set, 1)
                    pool.memset(band[p][:, NB - 1, BAND - P:BAND], 0.0).then_inc(const_set, 1)
                    for v in (v_far[0][p], v_far[1][p], v_near[p]):
                        pool.memset(v[:, :, HD:HD + 1], 1.0)
                        pool.memset(v[:, :, HD + 1:32], 0.0).then_inc(const_set, 1)
                pool.memset(clip_mask[:, :, :], 1.0).then_inc(const_set, 1)
                pool.memset(neg_scale[:, :], -SCALE).then_inc(const_set, 1)
                pool.wait_ge(const_set, 18)
                pool.affine_select(out=clip_mask[:, 0, :], in_=clip_mask[:, 0, :], compare_op=ALU.is_gt, fill=0.0, base=0,
                                   pattern=[[1, P]], channel_multiplier=-1).then_inc(const_set, 1)
                pool.affine_select(out=clip_mask[:, 1, :], in_=clip_mask[:, 1, :], compare_op=ALU.is_ge, fill=0.0, base=0,
                                   pattern=[[-1, P]], channel_multiplier=1).then_inc(const_set, 1)
                pool.wait_ge(const_set, 20)
                pool.wait_ge(const_in, 16 * 6)

                def copied(dst, src):
                    return nc.gpsimd.tensor_tensor(dst, src, zero[:, :, :], ALU.add)

                def step(hb, off):
                    x = Step(hb, off + LAG_R - 3)
                    if off % CH == 1 and x.valid:
                        pool.wait_ge(r_evac, x.count(16, 4 * x.r + 4))
                        copied(rel_ends[x.par][:, 4 * x.r:4 * x.r + 4, 0:2], rel[x.r % 2][:, :, 0:WIN:WIN - 1]).then_inc(ends_done, 1)
                    w = Step(hb, off - LAG_T - 1)
                    if w.valid:
                        bi = order(w.s)
                        k0, k1 = int(bi == 0), 2 - int(bi == NB - 1)
                        pool.wait_ge(bandT_evac, w.count(16, w.s + 1))
                        if w.g == 0:
                            wait(pool, clip_used, w.count(4, w.r))
                        nc.gpsimd.tensor_tensor(clip_T[:, w.g, k0:k1, :],
                                                band_T[w.r % 2][:, w.g, :].rearrange("p (b c) -> p b c", b=3)[:, 2 * k0:2 * k1 - 1:2, :],
                                                clip_mask[:, k0:k1, :], ALU.mult).then_inc(clip_ready, 1)
                    y = Step(hb, off - 3)
                    if off % CH == 3 and y.valid:
                        g = y.count(4, y.r)
                        k = y.count(20, 5 * y.r)
                        four = slice(4 * y.r, 4 * y.r + 4)
                        t = shb[y.r % 2][:, :, :].rearrange("p g (k t) -> p g k t", k=2)
                        pool.wait_ge(rmax_ready, g + 1)
                        wait(pool, band_exp, y.count(16, 4 * y.r + 4 - 32))
                        nc.gpsimd.tensor_tensor(negm[y.par][:, four], rmax[y.par][:, four], neg_scale[:, 0:1].to_broadcast([P, CH]),
                                                ALU.mult).then_inc(negm_ready, 1)
                        wait(pool, rows_tp, y.count(4, y.r - 1))
                        nc.gpsimd.tensor_tensor(sh[:, :, :], rel_ends[y.par][:, four, 0:2],
                                                rmax[y.par][:, four].unsqueeze(2).to_broadcast([P, CH, 2]), ALU.subtract).then_inc(shift_link, 1)
                        pool.wait_ge(shift_link, k + 1)
                        copied(t[:, :, :, 0], sh[:, :, :]).then_inc(shift_link, 1)
                        pool.wait_ge(shift_link, k + 2)
                        nc.gpsimd.tensor_tensor(sh[:, :, :], sh[:, :, :], t[:, :, :, 0], ALU.subtract).then_inc(shift_link, 1)
                        pool.wait_ge(shift_link, k + 3)
                        copied(t[:, :, :, 1], sh[:, :, :]).then_inc(shift_link, 1)
                        pool.wait_ge(shift_link, k + 4)
                        nc.gpsimd.tensor_tensor(sh[:, :, :], sh[:, :, :], t[:, :, :, 1], ALU.subtract).then_inc(shift_link, 1)
                        pool.wait_ge(shift_link, k + 5)
                        copied(t[:, :, :, 2], sh[:, :, :]).then_inc(shift_ready, 1)
                    z = Step(hb, off)
                    if off % NB == 4 and z.valid:
                        pool.wait_ge(v_in, z.count(16, 16))
                        wait(pool, band_pv, z.count(4, -4))
                        for k in range(2):
                            nc.gpsimd.tensor_tensor(v_far[k][z.par][:, :, 0:HD], v_raw[:, :, :],
                                                    rv_ends[:, k, :].unsqueeze(1).to_broadcast([P, NB, HD]), ALU.add)
                        nc.gpsimd.tensor_copy(v_near[z.par][:, :, 0:HD], v_raw[:, :, :]).then_inc(v_built, 1)

                loop(pool, step)

            @block.tensor
            def _(pe):
                pe.wait_ge(const_set, 20)
                pe.wait_ge(shift_set, 8)
                pe.wait_ge(const_in, 16 * 6)

                def step(hb, off):
                    a = Step(hb, off)
                    t = Step(hb, off - LAG_T)
                    x = Step(hb, off + LAG_R)
                    w = Step(hb, off - LAG_T - 1)
                    y = Step(hb, off - 5)
                    o = Step(hb, off - LAG_T - 2)
                    i = order(a.s)
                    def shift_rows():
                        pe.wait_ge(shift_ready, y.count(4, y.r + 1))
                        wait(pe, rows_copied, y.count(4, y.r))
                        if w.valid:
                            wait(pe, winT_evac, w.count(16, w.s + 1))
                        for g in range(CH):
                            mm = nc.tensor.transpose(prow[0:SHIFTS, g * P:(g + 1) * P], shb[y.r % 2][:, g, :], con["ident_bf"][:, :])
                        mm.then_inc(rows_tp, 1)

                    def turn_back():
                        pe.wait_ge(out_evac, o.count(1, 1))
                        wait(pe, r_evac, x.count(16, x.s + 1) if x.valid else NBH * 16)
                        for r in range(CH):
                            mm = nc.tensor.transpose(prel[:, r * P:(r + 1) * P], outT[:, r * P:(r + 1) * P], con["ident"][:, :])
                        mm.then_inc(back_mm, 1)

                    def weighted(r, g, values, probs, last=False):
                        return nc.tensor.matmul(pout[32 * g:32 * g + 32, r * P:(r + 1) * P], values, probs, start=False, stop=last,
                                                skip_group_check=True)

                    def clipped_values(r):
                        pe.wait_ge(clip_ready, w.count(16, 4 * r + 4))
                        for k in range(2):
                            for g in range(CH):
                                if 0 <= CH * g + r + 2 * k - 1 < NB:
                                    mm = weighted(r, g, rv_win[:, 3 * k, :], clip_T[:, g, k, :])
                        mm.then_inc(clip_used, 1)

                    def band_values(r, parts):
                        for b in parts:
                            for g in range(CH):
                                j = CH * g + r + b - 1
                                if 0 <= j < NB:
                                    weighted(r, g, v_near[w.par][:, j, :], band_T[r % 2][:, g, b * P:(b + 1) * P])

                    def near_values(r):
                        pe.wait_ge(winT_evac, w.count(16, 4 * r + 4))
                        for b in range(2):
                            for g in range(CH):
                                mm = weighted(r, g, rv_win[:, 1 + b, :], pwin_T[r % 2][:, g, b * P:(b + 1) * P], last=(r == CH - 1 and b == 1))
                        mm.then_inc(band_pv, 1)

                    def far_values():
                        if w.s == 0:
                            pe.wait_ge(v_built, w.count(1, 1))
                            wait(pe, out_evac, w.count(1, 0))
                        pe.wait_ge(exp_done, w.count(64, 4 * w.s + 4))
                        for nth in range(2):
                            for g in range(CH):
                                pieces = far_pieces(w.s, g)
                                if nth < len(pieces):
                                    right, c0, c1 = pieces[nth]
                                    mm = nc.tensor.matmul(pout[32 * g:32 * g + 32, c0:c1], v_far[right][w.par][:, w.s, :], far_T[w.s % 2][:, g, c0:c1],
                                                          start=(w.s == 0 and nth == 0), stop=False, skip_group_check=True)
                        mm.then_inc(pv_done, 1)

                    if t.valid and t.s == 0:
                        pe.wait_ge(back_in[t.par], t.count2(48, 48))
                        pe.wait_ge(rows_copied, t.count(4, 4))
                    for u in range(CH):
                        if a.valid:
                            if a.s == 0 and u == 0:
                                pe.wait_ge(qf_in[a.par], a.count2(16, 16))
                                pe.wait_ge(kf_in[a.par], a.count2(16, 16))
                            wait(pe, s1_used, a.count(64, 4 * a.s + u - 1))
                            nc.tensor.matmul(ps1[u % 2][:, :], q_front[a.par][:, i * P:(i + 1) * P], k_front[a.par][:, u * CW:(u + 1) * CW],
                                             start=True, stop=True).then_inc(s1_mm, 1)
                        if t.valid:
                            wait(pe, exp_done, t.count(64, 4 * t.s + u - 1))
                            for right, c0, c1 in far_pieces(t.s, u):
                                k = (k_right if right else k_left)[t.par]
                                mm = nc.tensor.matmul(pst[u % 2][:, c0:c1], k[:, t.s * P:(t.s + 1) * P], q_back[t.par][:, u * CW + c0:u * CW + c1],
                                                      start=True, stop=True)
                            mm.then_inc(st_mm, 1)
                        if u == 1 and w.valid:
                            far_values()
                        if u == 1 and x.valid:
                            if x.s == 0:
                                pe.wait_ge(qf_in[x.par], x.count2(16, 16))
                            wait(pe, r_evac, x.count(16, x.s))
                            if t.s == 2:
                                wait(pe, norm_done, t.count(1, 0))
                            xi = order(x.s)
                            nc.tensor.matmul(prel[:, :], q_front[x.par][:, xi * P:(xi + 1) * P], con["rel_k"][:, :], start=True, stop=True).then_inc(r_mm, 1)
                        if u == 1 and off % CH == 1 and y.valid:
                            shift_rows()
                        if u == 2 and o.s == NB - 1 and o.valid:
                            turn_back()
                    if t.valid:
                        bi = order(t.s)
                        pe.wait_ge(band_exp, t.count(16, t.s + 1))
                        wait(pe, bandT_evac, t.count(16, t.s))
                        for j in band_blocks(bi):
                            b = j - bi + 1
                            mm = nc.tensor.transpose(pband[:, b * P:(b + 1) * P], band[t.par][:, t.s, b * P:(b + 1) * P], con["ident"][:, :])
                        mm.then_inc(bandT_mm, 1)
                        if t.g == 0:
                            pe.wait_ge(win_in[t.r % 2], t.count(32, 16 * (t.r // 2 + 1)))
                        wait(pe, winT_evac, t.count(16, t.s))
                        if off % CH == 1 and y.valid:
                            pe.wait_ge(rows_copied, y.count(4, y.r + 1))
                        for b in range(2):
                            mm = nc.tensor.transpose(pnear[:, b * P:(b + 1) * P], pwin[t.r % 2][:, t.g, b * P:(b + 1) * P], con["ident"][:, :])
                        mm.then_inc(winT_mm, 1)
                    if w.valid:
                        if w.g == CH - 1:
                            clipped_values(w.r)
                            if w.r == CH - 1:
                                band_values(w.r, (0, 1, 2))
                                near_values(w.r)
                        elif w.r > 0:
                            if w.g < 2:
                                band_values(w.r - 1, ((0, 1), (2,))[w.g])
                            else:
                                near_values(w.r - 1)

                loop(pe, step)

            @block.vector
            def _(dve):
                for p in range(2):
                    nc.vector.memset(k_left[p][ROWS:ALLROWS, :], 0.0).then_inc(shift_set, 1)
                    nc.vector.memset(k_right[p][ROWS:ALLROWS, :], 1.0).then_inc(shift_set, 1)
                dve.wait_ge(shift_set, 4)
                for p in range(2):
                    nc.vector.memset(k_left[p][ROWS:ROWS + 3, :], 1.0).then_inc(shift_set, 1)
                    nc.vector.memset(k_right[p][ROWS:ROWS + 3, :], 0.0).then_inc(shift_set, 1)
                dve.wait_ge(const_set, 20)

                def step(hb, off):
                    a = Step(hb, off)
                    i = order(a.s)
                    w = Step(hb, off - LAG_T - 1)

                    def near():
                        dve.wait_ge(winT_mm, w.count(16, w.s + 1))
                        if w.g == 0:
                            wait(dve, band_pv, w.count(4, w.r - 1))
                        nc.vector.tensor_copy(pwin_T[w.r % 2][:, w.g, :], pnear[:, :]).then_inc(winT_evac, 1)

                    for u in range(CH):
                        if a.valid and a.g == 0 and u == 0:
                            dve.wait_ge(rel_in[a.par][a.r], a.count2(32 if a.r in (0, 3) else 16, 32 if a.r in (0, 3) else 16))
                        if a.valid:
                            dve.wait_ge(s1_mm, a.count(64, 4 * a.s + u + 1))
                            blocks = range(CH * u, CH * u + CH)
                            pieces = [(0, [j for j in blocks if j <= i - 2]), (1, [j for j in blocks if j >= i + 2]),
                                      (2, [j for j in blocks if abs(j - i) <= 1])]
                            pieces = [(kind, sel) for kind, sel in pieces if sel]
                            for kind, sel in pieces:
                                src = ps1[u % 2][:, (sel[0] - CH * u) * P:(sel[-1] + 1 - CH * u) * P]
                                best = part[a.par][:, a.s, kind, u:u + 1]
                                if kind == 2:
                                    b = sel[0] - i + 1
                                    dst = band[a.par][:, a.s, b * P:(b + len(sel)) * P]
                                    ins = nc.vector.tensor_tensor_reduce(dst, src, dst, 1.0, LOWEST, ALU.add, ALU.max, best)
                                else:
                                    ins = nc.vector.tensor_reduce(best, src, AX_X, ALU.max)
                            ins.then_inc(s1_used, 1)
                        if u == 1 and w.valid:
                            near()
                    o = Step(hb, off - LAG_T - 2)
                    if o.s == NB - 1 and o.valid:
                        back = prel[:, :].rearrange("p (r g d) -> p r g d", r=CH, g=CH)
                        rv = rden[:, :].rearrange("p (r g) -> p r g", r=CH)
                        dve.wait_ge(back_mm, o.count(1, 1))
                        nc.vector.reciprocal(rv, back[:, :, :, HD]).then_inc(den_ready, 1)
                        dve.wait_ge(den_ready, o.count(1, 1))
                        dst = attn[:, o.n, :, :].rearrange("p (g r) d -> p r g d", g=CH)
                        for r in range(CH):
                            ins = nc.vector.tensor_tensor(dst[:, r], back[:, r, :, 0:HD], rv[:, r].unsqueeze(2).to_broadcast([P, CH, HD]), ALU.mult)
                        ins.then_inc(norm_done, 1)
                    if a.valid and a.g == CH - 1:
                        four = slice(4 * a.r, 4 * a.r + 4)
                        k = a.count(8, 2 * a.r)
                        dve.wait_ge(s1_used, a.count(64, 16 * a.r + 16))
                        nc.vector.tensor_reduce(lm[:, :, :], part[a.par][:, four, :, :], AX_X, ALU.max).then_inc(max_link, 1)
                        dve.wait_ge(max_link, k + 1)
                        dve.wait_ge(ends_done, a.count(4, a.r + 1))
                        nc.vector.tensor_tensor(lm[:, :, :], lm[:, :, :], rel_ends[a.par][:, four, :], ALU.add).then_inc(max_link, 1)
                        dve.wait_ge(max_link, k + 2)
                        wait(dve, shift_ready, a.count(4, a.r + 1 - 8))
                        nc.vector.tensor_reduce(rmax[a.par][:, four], lm[:, :, :], AX_X, ALU.max).then_inc(rmax_ready, 1)

                loop(dve, step)

            @block.scalar
            def _(act):
                def step(hb, off):
                    e = Step(hb, off - LAG_T - 1 - NB)
                    x = Step(hb, off + LAG_R)
                    t = Step(hb, off - LAG_T)
                    y = Step(hb, off - 5)
                    w = Step(hb, off - LAG_T - 1)

                    def finished():
                        act.wait_ge(band_pv, e.count(4, 4))
                        nc.scalar.activation(outT[:, :], pout[:, :], ACT.Copy).then_inc(out_evac, 1)

                    def turned():
                        bl = band_blocks(order(w.s))
                        c0, c1 = (bl[0] - order(w.s) + 1) * P, (bl[-1] - order(w.s) + 2) * P
                        act.wait_ge(bandT_mm, w.count(16, w.s + 1))
                        if w.g == 0:
                            wait(act, band_pv, w.count(4, w.r - 1))
                        nc.scalar.activation(band_T[w.r % 2][:, w.g, c0:c1], pband[:, c0:c1], ACT.Copy).then_inc(bandT_evac, 1)

                    def relative():
                        act.wait_ge(r_mm, x.count(16, x.s + 1))
                        if x.g == 0:
                            before = Step(hb, off + LAG_R - 8)
                            wait(act, rel_out[before.r], before.count(16, 16) if before.valid else 0)
                            wait(act, ends_done, x.count(4, x.r - 1))
                        nc.scalar.activation(rel[x.r % 2][:, x.g, :], prel[:, :], ACT.Copy).then_inc(r_evac, 1)

                    def shift_rows():
                        act.wait_ge(rows_tp, y.count(4, y.r + 1))
                        rows = q_back[y.par][ROWS:ALLROWS, :].rearrange("k (g r c) -> k g r c", g=CH, r=CH)[:, :, y.r, :]
                        nc.scalar.activation(rows, prow.rearrange("k (g c) -> k g c", g=CH), ACT.Copy).then_inc(rows_copied, 1)

                    if t.valid:
                        wait(act, pv_done, t.count(16, t.s - 1))
                    for u in range(CH):
                        if t.valid:
                            act.wait_ge(st_mm, t.count(64, 4 * t.s + u + 1))
                            for _, c0, c1 in far_pieces(t.s, u):
                                ins = nc.scalar.activation(far_T[t.s % 2][:, u, c0:c1], pst[u % 2][:, c0:c1], ACT.Exp, scale=SCALE)
                            ins.then_inc(exp_done, 1)
                        if u == 0 and e.s == 0 and e.valid:
                            finished()
                        if u == 1 and w.valid:
                            turned()
                        if u == 1 and x.valid:
                            relative()
                        if u == 1 and off % CH == 1 and y.valid:
                            shift_rows()
                    if y.valid:
                        bl = band_blocks(order(y.s))
                        c0, c1 = (bl[0] - order(y.s) + 1) * P, (bl[-1] - order(y.s) + 2) * P
                        if y.g == 0:
                            act.wait_ge(negm_ready, y.count(4, y.r + 1))
                        nc.scalar.activation(band[y.par][:, y.s, c0:c1], band[y.par][:, y.s, c0:c1], ACT.Exp,
                                             bias=negm[y.par][:, y.s:y.s + 1], scale=SCALE).then_inc(band_exp, 1)

                loop(act, step)


def experts(nc, io, dram, con, expert_i):
    with ExitStack() as ctx:
        def sb(name, shape, dt):
            return ctx.enter_context(nc.sbuf_tensor(name, shape, dt))

        def sem(name):
            return ctx.enter_context(nc.semaphore(name))

        def two(name, shape, dt):
            return [sb(f"{name}{i}", shape, dt) for i in range(2)]

        w1 = sb("w1", [P, NE, DC, FF], F32)
        w2 = sb("w2", [P, NE, FC, D], F32)
        xs = two("xs", [P, D], F32)
        xsT = two("xsT", [P, DC, P], F32)
        hid = two("hid", [P, FF], F32)
        hT = two("hT", [P, FC, P], F32)
        ys = two("ys", [P, D], F32)
        px = ctx.enter_context(nc.psum_tensor("px", [P, 512], F32))
        ph = [ctx.enter_context(nc.psum_tensor(f"ph{i}", [P, 512], F32)) for i in range(2)]
        pt = [ctx.enter_context(nc.psum_tensor(f"pt{i}", [P, 512], F32)) for i in range(2)]
        py = ctx.enter_context(nc.psum_tensor("py", [P, 512], F32))

        w1_in = sem("w1_in")
        w2_in = sem("w2_in")
        xs_in = [sem(f"xs_in{i}") for i in range(2)]
        x_tp = sem("x_tp")
        x_evac = sem("x_evac")
        h_mm = sem("h_mm")
        gelu_done = sem("gelu_done")
        h_tp = sem("h_tp")
        hT_evac = sem("hT_evac")
        y_mm = sem("y_mm")
        y_evac = sem("y_evac")
        y_out = [sem(f"y_out{i}") for i in range(2)]

        with nc.Block() as block:

            @block.sync
            def _(sp):
                for h in range(2):
                    sp.dma_start(xs[h][:, :], dram["xs"][h * P:(h + 1) * P, :]).then_inc(xs_in[h], 16)
                for e in range(NE):
                    sp.dma_start(w1[:, e], io["w1"][e].rearrange("(c p) f -> p c f", p=P)).then_inc(w1_in, 16)
                for e in range(NE):
                    sp.dma_start(w2[:, e], io["w2"][e].rearrange("(c p) d -> p c d", p=P)).then_inc(w2_in, 16)

                def tile(T, h, more):
                    if more:
                        sp.wait_ge(x_tp, T + 1)
                        sp.dma_start(xs[h][:, :], dram["xs"][bass.ds((T + 2) * P, P), :]).then_inc(xs_in[h], 16)
                    sp.wait_ge(y_evac, T + 1)
                    sp.dma_start(dram["ys"][bass.ds(T * P, P), :], ys[h][:, :]).then_inc(y_out[h], 16)

                with sp.Fori(0, XT // 2 - 1) as pair_i:
                    T0 = pair_i * 2
                    tile(T0, 0, True)
                    tile(T0 + 1, 1, True)
                tile(XT - 2, 0, False)
                tile(XT - 1, 1, False)
                for h in range(2):
                    sp.wait_ge(y_out[h], 16 * XT // 2)

            @block.tensor
            def _(pe):
                def hidden(T, T0, h, e):
                    pe.wait_ge(xs_in[h], T0 * 8 + 16)
                    wait(pe, x_evac, T)
                    for d in range(DC):
                        mm = nc.tensor.transpose(px[:, d * P:(d + 1) * P], xs[h][:, d * P:(d + 1) * P], con["ident"][:, :])
                    mm.then_inc(x_tp, 1)
                    pe.wait_ge(x_evac, T + 1)
                    for half in range(2):
                        wait(pe, gelu_done, T * 2 + half - 1)
                        for d in range(DC):
                            mm = nc.tensor.matmul(ph[half][:, :], xsT[h][:, d, :], w1[:, e, d, half * 512:(half + 1) * 512],
                                                  start=(d == 0), stop=(d == DC - 1))
                        mm.then_inc(h_mm, 1)

                def output(T, h, e):
                    for half in range(2):
                        pe.wait_ge(gelu_done, T * 2 + half + 1)
                        wait(pe, hT_evac, T * 2 + half - 1)
                        for k in range(4):
                            j = half * 4 + k
                            mm = nc.tensor.transpose(pt[half][:, k * P:(k + 1) * P], hid[h][:, j * P:(j + 1) * P], con["ident"][:, :])
                        mm.then_inc(h_tp, 1)
                    wait(pe, y_evac, T)
                    for j in range(FC):
                        if j % 4 == 0:
                            pe.wait_ge(hT_evac, T * 2 + j // 4 + 1)
                        mm = nc.tensor.matmul(py[:, 0:D], hT[h][:, j, :], w2[:, e, j, :], start=(j == 0), stop=(j == FC - 1))
                    mm.then_inc(y_mm, 1)

                def expert(T):
                    return pe.value_load(expert_i[0:1, bass.ds(T, 1)], min_val=0, max_val=NE - 1)

                pe.wait_ge(w1_in, 16 * NE)
                pe.wait_ge(w2_in, 16 * NE)

                def pair(T0):
                    e0 = expert(T0)
                    e1 = expert(T0 + 1)
                    hidden(T0, T0, 0, e0)
                    hidden(T0 + 1, T0, 1, e1)
                    output(T0, 0, e0)
                    output(T0 + 1, 1, e1)

                pair(0)
                with pe.Fori(1, XT // 2) as pair_i:
                    pair(pair_i * 2)

            @block.scalar
            def _(act):
                with act.Fori(0, XT // 2) as pair_i:
                    T0 = pair_i * 2
                    for h in range(2):
                        for half in range(2):
                            act.wait_ge(h_mm, T0 * 2 + (h * 2 + half + 1))
                            nc.scalar.activation(hid[h][:, half * 512:(half + 1) * 512], ph[half][:, :], ACT.Gelu_apprx_tanh).then_inc(gelu_done, 1)

            @block.vector
            def _(dve):
                def turn_x(T, h):
                    dve.wait_ge(x_tp, T + 1)
                    nc.vector.tensor_copy(xsT[h][:, :, :], px[:, 0:D].rearrange("p (c m) -> p c m", c=DC)).then_inc(x_evac, 1)

                def turn_h(T, T0, h):
                    for half in range(2):
                        dve.wait_ge(h_tp, T * 2 + half + 1)
                        nc.vector.tensor_copy(hT[h][:, half * 4:(half + 1) * 4, :], pt[half][:, :].rearrange("p (c m) -> p c m", c=4)).then_inc(hT_evac, 1)
                    dve.wait_ge(y_mm, T + 1)
                    dve.wait_ge(y_out[h], T0 * 8) if not isinstance(T0, int) else None
                    nc.vector.tensor_copy(ys[h][:, :], py[:, 0:D]).then_inc(y_evac, 1)

                def pair(T0):
                    turn_x(T0, 0)
                    turn_x(T0 + 1, 1)
                    turn_h(T0, T0, 0)
                    turn_h(T0 + 1, T0, 1)

                pair(0)
                with dve.Fori(1, XT // 2) as pair_i:
                    T0 = pair_i * 2
                    pair(T0)


def finish(nc, io, dram, con, attn, pos_i, out):
    with ExitStack() as ctx:
        def sb(name, shape, dt):
            return ctx.enter_context(nc.sbuf_tensor(name, shape, dt))

        def sem(name):
            return ctx.enter_context(nc.semaphore(name))

        def two(name, shape, dt):
            return [sb(f"{name}{i}", shape, dt) for i in range(2)]

        wo = sb("wo", [P, DC, D], F32)
        bo = sb("bo", [P, D], F32)
        x_in = two("xf", [P, D], F32)
        y_all = sb("y_all", [P, TILES, D], F32)
        at = two("at", [P, D], F32)
        aT = two("aT", [P, DC, P], F32)
        gate = two("gate", [P, D], F32)
        res = two("res", [P, D], F32)
        pa = [ctx.enter_context(nc.psum_tensor(f"pa{i}", [P, 512], F32)) for i in range(2)]
        po = [ctx.enter_context(nc.psum_tensor(f"po{i}", [P, 512], F32)) for i in range(2)]

        wo_in = sem("wo_in")
        x_ld = [sem(f"x_ld{i}") for i in range(2)]
        y_ld = sem("y_ld")
        at_ready = sem("at_ready")
        a_tp = sem("a_tp")
        a_evac = sem("a_evac")
        o_mm = sem("o_mm")
        gate_ready = sem("gate_ready")
        link_sem = sem("sum_link")
        res_ready = sem("res_ready")
        stored = [sem(f"stored{i}") for i in range(2)]
        x_v = io["x"].rearrange("b (t p) d -> (b t) p d", p=P)
        out_v = out.rearrange("b (t p) d -> (b t) p d", p=P)

        with nc.Block() as block:

            @block.sync
            def _(sp):
                sp.dma_start(wo[:, :, :], io["woT"].rearrange("(c p) n -> p c n", p=P)).then_inc(wo_in, 16)
                sp.dma_start(bo[:, :], io["bo"].partition_broadcast(P)).then_inc(wo_in, 16)
                for h in range(2):
                    sp.dma_start(x_in[h][:, :], x_v[h]).then_inc(x_ld[h], 16)

                def tile(t, h, more):
                    sp.wait_ge(res_ready, t + 1)
                    sp.dma_start(out_v[t], res[h][:, :]).then_inc(stored[h], 16)
                    if more:
                        sp.dma_start(x_in[h][:, :], x_v[t + 2]).then_inc(x_ld[h], 16)

                with sp.Fori(0, TILES // 2 - 1) as pair_i:
                    t0 = pair_i * 2
                    tile(t0, 0, True)
                    tile(t0 + 1, 1, True)
                tile(TILES - 2, 0, False)
                tile(TILES - 1, 1, False)
                for h in range(2):
                    sp.wait_ge(stored[h], 16 * TILES // 2)

            @block.gpsimd
            def _(pool):
                for t in range(TILES):
                    pool.indirect_dma_start(out=y_all[:, t, :], out_offset=None, in_=dram["ys"][:, :],
                                            in_offset=bass.IndirectOffsetOnAxis(ap=pos_i[:, t:t + 1], axis=0)).then_inc(y_ld, 16)

            @block.tensor
            def _(pe):
                pe.wait_ge(wo_in, 32)
                with pe.Fori(0, TILES // 2) as pair_i:
                    t0 = pair_i * 2
                    for h in range(2):
                        t = t0 + h
                        pe.wait_ge(at_ready, t + 1)
                        for d in range(DC):
                            mm = nc.tensor.transpose(pa[h][:, d * P:(d + 1) * P], at[h][:, d * P:(d + 1) * P], con["ident"][:, :])
                        mm.then_inc(a_tp, 1)
                        pe.wait_ge(a_evac, t + 1)
                        for d in range(DC):
                            mm = nc.tensor.matmul(po[h][:, 0:D], aT[h][:, d, :], wo[:, d, :], start=(d == 0), stop=(d == DC - 1))
                        mm.then_inc(o_mm, 1)

            @block.scalar
            def _(act):
                act.wait_ge(y_ld, 16 * TILES)

                def tile(t, h):
                    wait(act, res_ready, t - 1)
                    act.wait_ge(a_tp, t + 1)
                    nc.scalar.activation(aT[h][:, :, :], pa[h][:, 0:D].rearrange("p (c m) -> p c m", c=DC), ACT.Copy).then_inc(a_evac, 1)
                    nc.scalar.activation(gate[h][:, :], y_all[:, bass.ds(t, 1), :].rearrange("p t d -> p (t d)"), ACT.Silu).then_inc(gate_ready, 1)

                tile(0, 0)
                tile(1, 1)
                with act.Fori(1, TILES // 2) as pair_i:
                    t0 = pair_i * 2
                    tile(t0, 0)
                    tile(t0 + 1, 1)

            @block.vector
            def _(dve):
                dve.wait_ge(wo_in, 32)

                def tile(t, t0, h):
                    wait(dve, a_tp, t - 1)
                    src = attn[:, :, :, :].rearrange("p (h b) i d -> p h (b i) d", b=B)[:, :, bass.ds(t, 1), :].rearrange("p h t d -> p h (t d)")
                    nc.vector.tensor_copy(at[h][:, :].rearrange("p (h d) -> p h d", h=HEADS), src).then_inc(at_ready, 1)
                    dve.wait_ge(o_mm, t + 1)
                    if not isinstance(t0, int):
                        dve.wait_ge(stored[h], t0 * 8)
                    nc.vector.tensor_tensor(res[h][:, :], po[h][:, 0:D], bo[:, :], ALU.add).then_inc(link_sem, 1)
                    dve.wait_ge(link_sem, t * 2 + 1)
                    dve.wait_ge(gate_ready, t + 1)
                    nc.vector.tensor_tensor(res[h][:, :], res[h][:, :], gate[h][:, :], ALU.mult).then_inc(link_sem, 1)
                    dve.wait_ge(link_sem, t * 2 + 2)
                    dve.wait_ge(x_ld[h], t0 * 8 + 16)
                    nc.vector.tensor_tensor(res[h][:, :], res[h][:, :], x_in[h][:, :], ALU.add).then_inc(res_ready, 1)

                tile(0, 0, 0)
                tile(1, 0, 1)
                with dve.Fori(1, TILES // 2) as pair_i:
                    t0 = pair_i * 2
                    tile(t0, t0, 0)
                    tile(t0 + 1, t0, 1)


def build(nc, io, out):
    def scratch(name, shape, dt):
        return nc.dram_tensor(name, shape, dt, kind="Internal").ap()

    dram = dict(
        q_stack=scratch("q_stack", [HEADS, ROWS, B * S], BF16),
        k_stack=scratch("k_stack", [HEADS, ROWS, B * S], BF16),
        v=scratch("v_pairs", [NBH, P, NB, HD], F32),
        rel=scratch("rel_scores", [2, NB, P, WIN], F32),
        band_p=scratch("band_probs", [2, NB, P, BAND], F32),
        xs=scratch("x_sorted", [XT * P, D], F32),
        ys=scratch("y_sorted", [XT * P, D], F32),
    )
    with ExitStack() as ctx:
        def sb(name, shape, dt):
            return ctx.enter_context(nc.sbuf_tensor(name, shape, dt))

        con = dict(ident=sb("ident", [P, P], F32), ident_bf=sb("ident_bf", [P, P], BF16), rel_k=sb("rel_k", [ROWS, WIN], BF16))
        pos_i = sb("pos_i", [P, TILES], I32)
        expert_i = sb("expert_i", [P, XT], I32)
        with ExitStack() as early:
            x_all = early.enter_context(nc.sbuf_tensor("x_all", [P, TILES, D], F32))
            lg_all = early.enter_context(nc.sbuf_tensor("lg_all", [P, TILES, NE], F32))
            project(nc, io, dram, con, x_all, lg_all)
            route(nc, dram, con, x_all, lg_all, pos_i, expert_i)
        attn = sb("attn", [P, NBH, NB, HD], F32)
        attend(nc, io, dram, con, attn)
        experts(nc, io, dram, con, expert_i)
        finish(nc, io, dram, con, attn, pos_i, out)


_INS = ["x", "wqT", "wkT", "wvT", "wg", "bq", "bk", "bv", "bg", "rel_kT", "rel_v", "woT", "bo", "w1", "w2"]


def kernel(**inputs):
    import numpy as _np
    import concourse.bacc as _bacc
    from concourse import mybir as _mybir
    from concourse.bass_utils import run_bass_kernel_spmd as _run

    a = {k: _np.asarray(v) for k, v in inputs.items()}
    host = {
        "x": a["L0_attn_x"], "wqT": a["L0_attn_Wq"].T, "wkT": a["L0_attn_Wk"].T, "wvT": a["L0_attn_Wv"].T, "wg": a["L0_ffn_Wg"],
        "bq": a["L0_attn_bq"].reshape(DC, P).T, "bk": a["L0_attn_bk"].reshape(DC, P).T, "bv": a["L0_attn_bv"], "bg": a["L0_ffn_bg"],
        "rel_kT": a["L0_attn_rel_k"].T, "rel_v": a["L0_attn_rel_v"], "woT": a["L0_attn_Wo"].T, "bo": a["L0_attn_bo"],
        "w1": a["L0_ffn_W1"], "w2": a["L0_ffn_W2"],
    }
    nc = _bacc.Bacc("TRN2", target_bir_lowering=False, num_devices=1)
    nc.disable_value_cache = True
    arrays, io = {}, {}
    for name in _INS:
        arr = _np.ascontiguousarray(host[name])
        arrays[f"in_{name}_dram"] = arr
        io[name] = nc.dram_tensor(f"in_{name}_dram", arr.shape, _mybir.dt.from_np(arr.dtype), kind="ExternalInput").ap()
    out = nc.dram_tensor("out_dram", (B, S, D), F32, kind="ExternalOutput").ap()
    build(nc, io, out)
    r = _run(nc, [arrays], core_ids=[0])
    return r.results[0]["out_dram"]
```

```python
from contextlib import ExitStack

import concourse.bass as bass
from concourse import mybir

F32 = mybir.dt.float32
BF16 = mybir.dt.bfloat16
I32 = mybir.dt.int32
ALU = mybir.AluOpType
ACT = mybir.ActivationFunctionType
AX_X = mybir.AxisListType.X

P = 128
B, S, D = 2, 2048, 256
HEADS, HD = 16, 16
NBH = HEADS * B
NB = S // P
TILES = B * S // P
DC = D // P
M = 128
NE, FF = 8, 1024
FC = FF // P
XT = TILES + NE
EPS = 1e-5
SCALE = HD ** -0.5
LOWEST = -3.0e38

QTERM = (0, 0, 0, 1, 1, 2)
KTERM = (0, 1, 2, 0, 1, 0)
ROWS = len(QTERM) * HD
SHIFTS = 6
ALLROWS = ROWS + SHIFTS

BAND = 3 * P
WIN = 4 * P
NEARW = 2 * M
CH = 4
CW = S // CH

LAG_R = 14
LAG_T = 18


def order(s):
    return s // CH + CH * (s % CH)


def band_blocks(i):
    return [j for j in (i - 1, i, i + 1) if 0 <= j < NB]


def runs(blocks):
    out = []
    for b in blocks:
        if out and out[-1][0] + out[-1][1] == b:
            out[-1][1] += 1
        else:
            out.append([b, 1])
    return out


def wait(eng, sem, value):
    if not (isinstance(value, int) and value <= 0):
        eng.wait_ge(sem, value)


def chain(eng, sem):
    count = [0]

    def link(ins):
        count[0] += 1
        ins.then_inc(sem, 1)
        eng.wait_ge(sem, count[0])

    return link


def project(nc, io, dram, con, lg_all):
    CT = 4
    CHUNKS = TILES // CT
    QT = 2 * CT
    PAIRS = CHUNKS // 2
    CTOK = CT * P
    HALF = HEADS // DC
    NORM_LINKS = 8
    STACK_COUNT = 16 * 4 * len(QTERM)
    with ExitStack() as ctx:
        def sb(name, shape, dt):
            return ctx.enter_context(nc.sbuf_tensor(name, shape, dt))

        def sem(name):
            return ctx.enter_context(nc.semaphore(name))

        x_all = sb("x_all", [P, TILES, D], F32)
        wq = sb("wq", [P, DC, D], F32)
        wk = sb("wk", [P, DC, D], F32)
        wvg = sb("wvg", [P, DC, D + NE], F32)
        bqk = sb("bqk", [P, 2, DC], F32)
        bvg = sb("bvg", [P, D + NE], F32)
        stats = sb("stats", [P, TILES, 6], F32)
        mean = sb("mean", [P, TILES], F32)
        var = sb("var", [P, TILES], F32)
        std = sb("std", [P, TILES], F32)
        rstd = sb("rstd", [P, TILES], F32)
        tmp = sb("tmp", [P, TILES], F32)
        xn = [sb(f"xn{h}", [P, CT, D], F32) for h in range(2)]
        xT = [sb(f"xT{h}", [P, DC, CTOK], F32) for h in range(2)]
        qf = [[sb(f"qf{h}{u}", [P, CTOK], F32) for u in range(4)] for h in range(2)]
        terms = [[sb(f"terms{h}{u}", [P, 3, CTOK], BF16) for u in range(4)] for h in range(2)]
        v_all = sb("v_all", [P, HEADS, TILES, HD], F32)
        rkT = sb("rkT", [HD, 2 * M + 1], F32)
        rk_ext = sb("rk_ext", [HD, WIN], F32)
        rk_terms = sb("rk_terms", [HD, 3, WIN], BF16)
        zeros = sb("zeros", [P, D], F32)

        tp = [ctx.enter_context(nc.psum_tensor(f"tp{i}", [P, 512], F32)) for i in range(2)]
        pq = [ctx.enter_context(nc.psum_tensor(f"pq{i}", [P, 512], F32)) for i in range(2)]
        pv = [ctx.enter_context(nc.psum_tensor(f"pv{i}", [P, 512], F32)) for i in range(2)]

        x_first = sem("x_first")
        x_rest = sem("x_rest")
        w_in = sem("w_in")
        rk_in = sem("rk_in")
        rk_link = sem("rk_link")
        rk_split = sem("rk_split")
        rk_out = sem("rk_out")
        ident_set = sem("ident_set")
        zero_set = sem("zero_set")
        zeros_out = sem("zeros_out")
        stats_done = sem("stats_done")
        var_ready = sem("var_ready")
        std_ready = sem("std_ready")
        norm_link = sem("norm_link")
        xn_ready = sem("xn_ready")
        xn_out = [sem(f"xn_out{h}") for h in range(2)]
        tr_mm = sem("tr_mm")
        xT_evac = sem("xT_evac")
        qk_mm = sem("qk_mm")
        qk_evac = sem("qk_evac")
        split_link = sem("split_link")
        split_done = sem("split_done")
        stacked = [sem(f"stacked{h}") for h in range(2)]
        vg_mm = sem("vg_mm")
        vg_evac = sem("vg_evac")
        v_out = sem("v_out")

        x_v = io["x"].rearrange("b (t p) d -> p (b t) d", p=P)
        xn_v = dram["xn"].rearrange("(t p) d -> p t d", p=P)

        with nc.Block() as block:

            @block.sync
            def _(sp):
                sp.dma_start(x_all[:, 0:QT, :], x_v[:, 0:QT, :]).then_inc(x_first, 16)
                for t, name in ((wq, "wqT"), (wk, "wkT")):
                    sp.dma_start(t[:, :, :], io[name].rearrange("(c p) n -> p c n", p=P)).then_inc(w_in, 16)
                sp.dma_start(wvg[:, :, 0:D], io["wvT"].rearrange("(c p) n -> p c n", p=P)).then_inc(w_in, 16)
                sp.dma_start(wvg[:, :, D:D + NE], io["wg"].rearrange("(c p) n -> p c n", p=P)).then_inc(w_in, 16)
                for k, name in enumerate(("bq", "bk")):
                    sp.dma_start(bqk[:, k, :], io[name]).then_inc(w_in, 16)
                sp.dma_start(bvg[:, 0:D], io["bv"].partition_broadcast(P)).then_inc(w_in, 16)
                sp.dma_start(bvg[:, D:D + NE], io["bg"].partition_broadcast(P)).then_inc(w_in, 16)
                sp.dma_start(x_all[:, QT:TILES, :], x_v[:, QT:TILES, :]).then_inc(x_rest, 16)
                sp.dma_start(rkT[:, :], io["rel_kT"]).then_inc(rk_in, 16)

                def rows_out(c, half):
                    sp.wait_ge(xn_ready, c * CT + CT)
                    sp.dma_start(xn_v[:, bass.ds(c * CT, CT), :], xn[half][:, :, :]).then_inc(xn_out[half], 16)

                def stacks_out(c, half):
                    for u in range(4):
                        sp.wait_ge(split_done, c * 4 + u + 1)
                        tab, which = ((dram["q_stack"], QTERM), (dram["k_stack"], KTERM))[u // 2]
                        for slot in range(len(which)):
                            dst = tab[HALF * (u % 2):HALF * (u % 2 + 1), slot * HD:(slot + 1) * HD, bass.ds(c * CTOK, CTOK)]
                            sp.dma_start(dst, terms[half][u][:, which[slot], :]).then_inc(stacked[half], 16)

                rows_out(0, 0)
                rows_out(1, 1)
                stacks_out(0, 0)
                sp.wait_ge(zero_set, 1)
                sp.dma_start(dram["xs"].rearrange("(t p) d -> p t d", p=P), zeros[:, :].unsqueeze(1).to_broadcast([P, XT, D])).then_inc(zeros_out, 16)
                sp.wait_ge(rk_split, 3)
                for slot in range(len(KTERM)):
                    sp.dma_start(con["rel_k"][slot * HD:(slot + 1) * HD, :], rk_terms[:, KTERM[slot], :]).then_inc(rk_out, 16)
                with sp.Fori(1, PAIRS) as pair_i:
                    c0 = pair_i * 2
                    stacks_out(c0 - 1, 1)
                    rows_out(c0, 0)
                    rows_out(c0 + 1, 1)
                    stacks_out(c0, 0)
                stacks_out(CHUNKS - 1, 1)
                for h in range(2):
                    sp.wait_ge(stacked[h], STACK_COUNT * CHUNKS // 2)
                for h in range(2):
                    sp.wait_ge(xn_out[h], 16 * CHUNKS // 2)
                sp.wait_ge(zeros_out, 16)
                sp.wait_ge(rk_out, 16 * len(KTERM))

            @block.gpsimd
            def _(pool):
                pool.memset(zeros[:, :], 0.0).then_inc(zero_set, 1)
                pool.memset(con["ident"][:, :], 0.0).then_inc(ident_set, 1)
                pool.memset(con["ident_bf"][:, :], 0.0).then_inc(ident_set, 1)
                pool.wait_ge(ident_set, 2)
                for m in (con["ident"], con["ident_bf"]):
                    pool.affine_select(out=m[:, :], in_=m[:, :], compare_op=ALU.not_equal, fill=1.0, base=0,
                                       pattern=[[-1, P]], channel_multiplier=1).then_inc(ident_set, 1)
                v_pairs = dram["v"].rearrange("(h b) p i d -> b p h (i d)", b=B)
                for b in range(B):
                    pool.wait_ge(vg_evac, NB * (b + 1))
                    pool.dma_start(v_pairs[b], v_all[:, :, NB * b:NB * (b + 1), :].rearrange("p h t d -> p h (t d)")).then_inc(v_out, 16)
                pool.wait_ge(v_out, 16 * B)

            @block.vector
            def _(dve):
                v = nc.vector

                def relative_keys():
                    link = chain(dve, rk_link)
                    dve.wait_ge(rk_in, 16)
                    v.tensor_copy(rk_ext[:, P:P + 2 * M + 1], rkT[:, :])
                    v.tensor_copy(rk_ext[:, 0:P], rkT[:, 0:1].to_broadcast([HD, P]))
                    link(v.tensor_copy(rk_ext[:, P + 2 * M + 1:WIN], rkT[:, 2 * M:2 * M + 1].to_broadcast([HD, WIN - P - 2 * M - 1])))
                    v.tensor_copy(rk_terms[:, 0, :], rk_ext[:, :]).then_inc(rk_split, 1)
                    dve.wait_ge(rk_split, 1)
                    link(v.tensor_tensor(rk_ext[:, :], rk_ext[:, :], rk_terms[:, 0, :], ALU.subtract))
                    v.tensor_copy(rk_terms[:, 1, :], rk_ext[:, :]).then_inc(rk_split, 1)
                    dve.wait_ge(rk_split, 2)
                    v.tensor_tensor(rk_terms[:, 2, :], rk_ext[:, :], rk_terms[:, 1, :], ALU.subtract).then_inc(rk_split, 1)

                def linked(i, n, ins):
                    ins.then_inc(norm_link, 1)
                    dve.wait_ge(norm_link, i * NORM_LINKS + n)

                def variance(i):
                    for k in range(QT):
                        t = bass.ds(i * QT + k, 1)
                        v.bn_stats(stats[:, t, :].rearrange("p t s -> p (t s)"), x_all[:, t, :].rearrange("p t d -> p (t d)")).then_inc(stats_done, 1)
                    q = bass.ds(i * QT, QT)
                    mn, vr, tm = mean[:, q], var[:, q], tmp[:, q]
                    dve.wait_ge(stats_done, i * QT + QT)
                    v.tensor_tensor(mn, stats[:, q, 1], stats[:, q, 4], ALU.add)
                    v.tensor_tensor(tm, stats[:, q, 1], stats[:, q, 4], ALU.subtract)
                    linked(i, 1, v.tensor_tensor(vr, stats[:, q, 2], stats[:, q, 5], ALU.add))
                    v.tensor_scalar(mn, mn, 0.5, None, ALU.mult)
                    v.tensor_scalar(vr, vr, 1.0 / D, EPS, ALU.mult, ALU.add)
                    linked(i, 2, v.tensor_scalar(tm, tm, 0.5, None, ALU.mult))
                    linked(i, 3, v.tensor_tensor(tm, tm, tm, ALU.mult))
                    v.tensor_tensor(vr, vr, tm, ALU.add).then_inc(var_ready, 1)

                def inverse(i):
                    q = bass.ds(i * QT, QT)
                    rs, tm = rstd[:, q], tmp[:, q]
                    dve.wait_ge(std_ready, i + 1)
                    linked(i, 4, v.reciprocal(rs, std[:, q]))
                    linked(i, 5, v.tensor_tensor(tm, rs, rs, ALU.mult))
                    linked(i, 6, v.tensor_tensor(tm, tm, var[:, q], ALU.mult))
                    linked(i, 7, v.tensor_scalar(tm, tm, -0.5, 1.5, ALU.mult, ALU.add))
                    linked(i, 8, v.tensor_tensor(rs, rs, tm, ALU.mult))

                def normalise(c, half, out_count):
                    wait(dve, tr_mm, c * CT - CT)
                    wait(dve, xn_out[half], out_count)
                    for k in range(CT):
                        t = c * CT + k
                        v.tensor_scalar(xn[half][:, k, :], x_all[:, bass.ds(t, 1), :].rearrange("p t d -> p (t d)"), mean[:, bass.ds(t, 1)],
                                        rstd[:, bass.ds(t, 1)], ALU.subtract, ALU.mult).then_inc(xn_ready, 1)

                def split(c, half):
                    for u in range(4):
                        n = c * 4 + u
                        dve.wait_ge(qk_evac, n + 1)
                        v.tensor_tensor(qf[half][u][:, :], qf[half][u][:, :], terms[half][u][:, 0, :], ALU.subtract).then_inc(split_link, 1)
                        dve.wait_ge(split_link, n * 2 + 1)
                        v.tensor_copy(terms[half][u][:, 1, :], qf[half][u][:, :]).then_inc(split_link, 1)
                        dve.wait_ge(split_link, n * 2 + 2)
                        v.tensor_tensor(terms[half][u][:, 2, :], qf[half][u][:, :], terms[half][u][:, 1, :], ALU.subtract).then_inc(split_done, 1)

                def values(c):
                    for k in range(CT):
                        t = c * CT + k
                        dve.wait_ge(vg_mm, t + 1)
                        v.tensor_tensor(v_all[:, :, bass.ds(t, 1), :].rearrange("p h t d -> p h (t d)"),
                                        pv[k % 2][:, 0:D].rearrange("p (h d) -> p h d", h=HEADS),
                                        bvg[:, 0:D].rearrange("p (h d) -> p h d", h=HEADS), ALU.add)
                        v.tensor_tensor(lg_all[:, bass.ds(t, 1), :].rearrange("p t e -> p (t e)"), pv[k % 2][:, D:D + NE],
                                        bvg[:, D:D + NE], ALU.add).then_inc(vg_evac, 1)

                def pair(i, out_count, last=False):
                    c0 = i * 2
                    normalise(c0, 0, out_count)
                    split(c0 - 1, 1)
                    values(c0 - 1)
                    if not last:
                        variance(i + 1)
                    normalise(c0 + 1, 1, out_count)
                    split(c0, 0)
                    values(c0)
                    if not last:
                        inverse(i + 1)

                dve.wait_ge(x_first, 16)
                variance(0)
                inverse(0)
                normalise(0, 0, 0)
                normalise(1, 1, 0)
                dve.wait_ge(x_rest, 16)
                variance(1)
                dve.wait_ge(w_in, 16 * 8)
                split(0, 0)
                values(0)
                inverse(1)
                relative_keys()
                with dve.Fori(1, PAIRS - 1) as pair_i:
                    pair(pair_i, pair_i * 16)
                pair(PAIRS - 1, 16 * (PAIRS - 1), last=True)
                split(CHUNKS - 1, 1)
                values(CHUNKS - 1)

            @block.scalar
            def _(act):
                def root(i):
                    act.wait_ge(var_ready, i + 1)
                    nc.scalar.activation(std[:, bass.ds(i * QT, QT)], var[:, bass.ds(i * QT, QT)], ACT.Sqrt).then_inc(std_ready, 1)

                def turn(c, half):
                    wait(act, vg_mm, c * CT - CT)
                    for k in range(CT):
                        act.wait_ge(tr_mm, c * CT + k + 1)
                        nc.scalar.activation(xT[half][:, :, k * P:(k + 1) * P], tp[k % 2][:, 0:D].rearrange("p (c m) -> p c m", c=DC),
                                             ACT.Copy).then_inc(xT_evac, 1)

                def bias(c, half, stack_count):
                    wait(act, stacked[half], stack_count)
                    for u in range(4):
                        act.wait_ge(qk_mm, c * 4 + u + 1)
                        b = bqk[:, u // 2, u % 2:u % 2 + 1]
                        nc.scalar.activation(qf[half][u][:, :], pq[u % 2][:, :], ACT.Identity, bias=b)
                        nc.scalar.activation(terms[half][u][:, 0, :], pq[u % 2][:, :], ACT.Identity, bias=b).then_inc(qk_evac, 1)

                root(0)
                act.wait_ge(w_in, 16 * 8)
                turn(0, 0)
                turn(1, 1)
                root(1)
                bias(0, 0, 0)
                bias(1, 1, 0)
                with act.Fori(1, PAIRS - 1) as pair_i:
                    c0 = pair_i * 2
                    turn(c0, 0)
                    bias(c0, 0, pair_i * STACK_COUNT)
                    turn(c0 + 1, 1)
                    root(pair_i + 1)
                    bias(c0 + 1, 1, pair_i * STACK_COUNT)
                c0 = CHUNKS - 2
                turn(c0, 0)
                bias(c0, 0, (PAIRS - 1) * STACK_COUNT)
                turn(c0 + 1, 1)
                bias(c0 + 1, 1, (PAIRS - 1) * STACK_COUNT)

            @block.tensor
            def _(pe):
                def turn(c, half):
                    for k in range(CT):
                        pe.wait_ge(xn_ready, c * CT + k + 1)
                        wait(pe, xT_evac, c * CT + k - 1)
                        for d in range(DC):
                            mm = nc.tensor.transpose(tp[k % 2][:, d * P:(d + 1) * P], xn[half][:, k, d * P:(d + 1) * P], con["ident"][:, :])
                        mm.then_inc(tr_mm, 1)

                def queries_keys(c, half):
                    pe.wait_ge(xT_evac, c * CT + CT)
                    for u in range(4):
                        w = wq if u < 2 else wk
                        wait(pe, qk_evac, c * 4 + u - 1)
                        for d in range(DC):
                            mm = nc.tensor.matmul(pq[u % 2][:, :], w[:, d, (u % 2) * P:(u % 2 + 1) * P], xT[half][:, d, :],
                                                  start=(d == 0), stop=(d == DC - 1))
                        mm.then_inc(qk_mm, 1)

                def values(c, half):
                    for k in range(CT):
                        wait(pe, vg_evac, c * CT + k - 1)
                        for d in range(DC):
                            mm = nc.tensor.matmul(pv[k % 2][:, 0:D + NE], xT[half][:, d, k * P:(k + 1) * P], wvg[:, d, :],
                                                  start=(d == 0), stop=(d == DC - 1))
                        mm.then_inc(vg_mm, 1)

                pe.wait_ge(ident_set, 4)
                turn(0, 0)
                turn(1, 1)
                pe.wait_ge(w_in, 16 * 8)
                queries_keys(0, 0)
                values(0, 0)
                with pe.Fori(1, PAIRS) as pair_i:
                    c0 = pair_i * 2
                    queries_keys(c0 - 1, 1)
                    turn(c0, 0)
                    values(c0 - 1, 1)
                    queries_keys(c0, 0)
                    turn(c0 + 1, 1)
                    values(c0, 0)
                queries_keys(CHUNKS - 1, 1)
                values(CHUNKS - 1, 1)


def route(nc, lg_all, pos_i, expert_i):
    with ExitStack() as ctx:
        def sb(name, shape, dt):
            return ctx.enter_context(nc.sbuf_tensor(name, shape, dt))

        def sem(name):
            return ctx.enter_context(nc.semaphore(name))

        iota_i = sb("iota_i", [P, XT], I32)
        iota_f = sb("iota_f", [P, XT], F32)
        iota_e = sb("iota_e", [P, NE], F32)
        iota_c = sb("iota_c", [P, TILES], F32)
        before = sb("before", [P, P], BF16)
        ones = sb("ones", [P, P], BF16)
        top = sb("top", [P, TILES], F32)
        eq = sb("eq", [P, TILES, NE], F32)
        pick = sb("pick", [P, TILES], F32)
        oh = sb("oh", [P, TILES, NE], BF16)
        tot = sb("tot", [P, TILES, NE], F32)
        cum = [sb(f"cum{i}", [P, TILES, NE], F32) for i in range(2)]
        base = sb("base", [P, TILES, NE], F32)
        more = sb("more", [P, NE, TILES], F32)
        nt = sb("nt", [P, NE], F32)
        end = [sb(f"end{i}", [P, NE], F32) for i in range(2)]
        first = sb("first", [P, NE], F32)
        posf = sb("posf", [P, TILES], F32)
        past = sb("past", [P, XT, NE], F32)
        expf = sb("expf", [P, XT], F32)
        pr = ctx.enter_context(nc.psum_tensor("pr", [P, 2, TILES * NE], F32))

        iota_set = sem("iota_set")
        tri_set = sem("tri_set")
        link_sem = sem("route_link")
        oh_ready = sem("oh_ready")
        counts_mm = sem("counts_mm")
        pos_ready = sem("pos_ready")

        with nc.Block() as block:

            @block.gpsimd
            def _(pool):
                pool.iota(iota_i[:, :], pattern=[[1, XT]], base=0, channel_multiplier=0).then_inc(iota_set, 1)
                pool.memset(ones[:, :], 1.0).then_inc(tri_set, 1)
                pool.memset(before[:, :], 1.0).then_inc(tri_set, 1)
                pool.wait_ge(tri_set, 2)
                pool.affine_select(out=before[:, :], in_=before[:, :], compare_op=ALU.is_gt, fill=0.0, base=0,
                                   pattern=[[1, P]], channel_multiplier=-1).then_inc(tri_set, 1)

            @block.tensor
            def _(pe):
                pe.wait_ge(tri_set, 3)
                pe.wait_ge(oh_ready, 1)
                ohv = oh[:, :, :].rearrange("p t e -> p (t e)")
                nc.tensor.matmul(pr[:, 0, :], before[:, :], ohv, start=True, stop=True)
                nc.tensor.matmul(pr[:, 1, :], ones[:, :], ohv, start=True, stop=True).then_inc(counts_mm, 1)

            @block.vector
            def _(dve):
                link = chain(dve, link_sem)
                v = nc.vector

                def over(ap, shape, axis):
                    return ap.unsqueeze(axis).to_broadcast(shape)

                TE = [P, TILES, NE]
                dve.wait_ge(iota_set, 1)
                link(v.tensor_copy(iota_f[:, :], iota_i[:, :]))
                v.tensor_scalar(iota_e[:, :], iota_f[:, 0:NE], -float(NE), None, ALU.add)
                v.tensor_scalar(iota_c[:, :], iota_f[:, 0:TILES], float(P), None, ALU.mult)
                link(v.tensor_reduce(top[:, :], lg_all[:, :, :], AX_X, ALU.max))
                link(v.tensor_tensor(eq[:, :, :], lg_all[:, :, :], over(top[:, :], TE, 2), ALU.is_ge))
                link(v.tensor_tensor(eq[:, :, :], eq[:, :, :], over(iota_e[:, :], TE, 1), ALU.mult))
                link(v.tensor_reduce(pick[:, :], eq[:, :, :], AX_X, ALU.min))
                v.tensor_tensor(oh[:, :, :], over(iota_e[:, :], TE, 1), over(pick[:, :], TE, 2), ALU.is_equal).then_inc(oh_ready, 1)
                dve.wait_ge(counts_mm, 1)
                v.tensor_copy(cum[0][:, :, :], pr[:, 1, :].rearrange("p (t e) -> p t e", e=NE))
                link(v.tensor_copy(tot[:, :, :], pr[:, 1, :].rearrange("p (t e) -> p t e", e=NE)))
                a = 0
                k = 1
                while k < TILES:
                    v.tensor_copy(cum[1 - a][:, 0:k, :], cum[a][:, 0:k, :])
                    link(v.tensor_tensor(cum[1 - a][:, k:, :], cum[a][:, k:, :], cum[a][:, 0:TILES - k, :], ALU.add))
                    a, k = 1 - a, 2 * k
                ET = [P, NE, TILES]
                link(v.tensor_tensor(more[:, :, :], over(cum[a][:, TILES - 1, :], ET, 2), over(iota_c[:, :], ET, 1), ALU.is_gt))
                link(v.tensor_reduce(nt[:, :], more[:, :, :], AX_X, ALU.add))
                link(v.tensor_copy(end[0][:, :], nt[:, :]))
                b, k = 0, 1
                while k < NE:
                    v.tensor_copy(end[1 - b][:, 0:k], end[b][:, 0:k])
                    link(v.tensor_tensor(end[1 - b][:, k:], end[b][:, k:], end[b][:, 0:NE - k], ALU.add))
                    b, k = 1 - b, 2 * k
                link(v.tensor_tensor(first[:, :], end[b][:, :], nt[:, :], ALU.subtract))
                link(v.tensor_scalar(first[:, :], first[:, :], float(P), None, ALU.mult))
                link(v.tensor_tensor(base[:, :, :], cum[a][:, :, :], tot[:, :, :], ALU.subtract))
                link(v.tensor_tensor(base[:, :, :], base[:, :, :], pr[:, 0, :].rearrange("p (t e) -> p t e", e=NE), ALU.add))
                link(v.tensor_tensor(base[:, :, :], base[:, :, :], over(first[:, :], TE, 1), ALU.add))
                link(v.tensor_tensor(base[:, :, :], base[:, :, :], oh[:, :, :], ALU.mult))
                link(v.tensor_reduce(posf[:, :], base[:, :, :], AX_X, ALU.add))
                v.tensor_copy(pos_i[:, :], posf[:, :]).then_inc(pos_ready, 1)
                XE = [P, XT, NE]
                link(v.tensor_tensor(past[:, :, :], over(iota_f[:, :], XE, 2), over(end[b][:, :], XE, 1), ALU.is_ge))
                link(v.tensor_reduce(expf[:, :], past[:, :, :], AX_X, ALU.add))
                link(v.tensor_scalar(expf[:, :], expf[:, :], float(NE - 1), None, ALU.min))
                v.tensor_copy(expert_i[:, :], expf[:, :]).then_inc(pos_ready, 1)


def attend(nc, io, dram, con, pos_i, attn):
    with ExitStack() as ctx:
        def sb(name, shape, dt):
            return ctx.enter_context(nc.sbuf_tensor(name, shape, dt))

        def sem(name):
            return ctx.enter_context(nc.semaphore(name))

        def two(name, shape, dt):
            return [sb(f"{name}{i}", shape, dt) for i in range(2)]

        q_front = two("q_front", [ROWS, S], BF16)
        k_front = two("k_front", [ROWS, S], BF16)
        q_back = two("q_back", [ALLROWS, S], BF16)
        k_left = two("k_left", [ALLROWS, S], BF16)
        k_right = two("k_right", [ALLROWS, S], BF16)
        rel = two("rel", [P, CH, WIN], F32)
        band = two("band", [P, NB, BAND], F32)
        pwin = two("pwin", [P, CH, NEARW], F32)
        band_T = two("band_T", [P, CH, BAND], F32)
        pwin_T = two("pwin_T", [P, CH, NEARW], F32)
        clip_T = sb("clip_T", [P, CH, 2, P], F32)
        clip_mask = sb("clip_mask", [P, 2, P], F32)
        far_T = two("far_T", [P, CH, CW], F32)
        v_raw = sb("v_raw", [P, NB, HD], F32)
        v_far = [two(f"v_far{k}", [P, NB, 32], F32) for k in range(2)]
        v_near = two("v_near", [P, NB, 32], F32)
        rv_ends = sb("rv_ends", [P, 2, HD], F32)
        rv_win = sb("rv_win", [P, CH, 32], F32)
        part = two("part", [P, NB, 3, CH], F32)
        lm = sb("lm", [P, CH, 3], F32)
        rmax = two("rmax", [P, NB], F32)
        negm = two("negm", [P, NB], F32)
        rel_ends = two("rel_ends", [P, NB, 3], F32)
        sh = sb("sh", [P, CH, 2], F32)
        shb = two("shb", [P, CH, SHIFTS], BF16)
        outT = sb("outT", [P, CW], F32)
        rden = sb("rden", [P, NB], F32)
        zero = sb("zero", [P, CH, 2], F32)
        neg_scale = sb("neg_scale", [P, 1], F32)
        row = two("row", [P, D], F32)

        ps1 = [ctx.enter_context(nc.psum_tensor(f"ps1_{i}", [P, 512], F32)) for i in range(2)]
        pst = [ctx.enter_context(nc.psum_tensor(f"pst{i}", [P, 512], F32)) for i in range(2)]
        pout = ctx.enter_context(nc.psum_tensor("pout", [P, 512], F32))
        prel = ctx.enter_context(nc.psum_tensor("prel", [P, 512], F32))
        pband = ctx.enter_context(nc.psum_tensor("pband", [P, 512], F32))
        psmall = ctx.enter_context(nc.psum_tensor("psmall", [P, 512], F32))
        pnear = psmall[:, 0:NEARW]
        prow = psmall[0:SHIFTS, NEARW:512].bitcast(BF16)

        const_in = sem("const_in")
        const_set = sem("const_set")
        shift_set = sem("shift_set")
        qf_in = [sem(f"qf_in{i}") for i in range(2)]
        kf_in = [sem(f"kf_in{i}") for i in range(2)]
        back_in = [sem(f"back_in{i}") for i in range(2)]
        v_in = sem("v_in")
        v_built = sem("v_built")
        s1_mm = sem("s1_mm")
        s1_used = sem("s1_used")
        r_mm = sem("r_mm")
        r_evac = sem("r_evac")
        ends_done = sem("ends_done")
        rel_out = [sem(f"rel_out{r}") for r in range(4)]
        rel_in = [[sem(f"rel_in{p}{r}") for r in range(4)] for p in range(2)]
        max_link = sem("max_link")
        rmax_ready = sem("rmax_ready")
        negm_ready = sem("negm_ready")
        shift_link = sem("shift_link")
        shift_ready = sem("shift_ready")
        rows_tp = sem("rows_tp")
        rows_copied = sem("rows_copied")
        band_exp = sem("band_exp")
        prob_out = [sem(f"prob_out{r}") for r in range(4)]
        win_in = [sem(f"win_in{i}") for i in range(2)]
        st_mm = sem("st_mm")
        exp_done = sem("exp_done")
        pv_done = sem("pv_done")
        bandT_mm = sem("bandT_mm")
        bandT_evac = sem("bandT_evac")
        winT_mm = sem("winT_mm")
        winT_evac = sem("winT_evac")
        clip_ready = sem("clip_ready")
        clip_used = sem("clip_used")
        band_pv = sem("band_pv")
        out_evac = sem("out_evac")
        back_mm = sem("back_mm")
        den_ready = sem("den_ready")
        norm_done = sem("norm_done")
        row_in = [sem(f"row_in{i}") for i in range(2)]
        sorted_out = [sem(f"sorted_out{i}") for i in range(2)]

        class Step:

            def __init__(self, hb, off):
                self.dn, self.s = divmod(off, NB)
                self.hb = hb
                self.par = self.dn % 2
                self.head = hb + self.dn // 2
                self.n = hb * 2 + self.dn
                self.r, self.g = divmod(self.s, CH)
                self.valid = not isinstance(hb, int) or 0 <= self.n < NBH

            def count(self, per, more):
                return self.sum(2 * per, self.dn * per + more)

            def count2(self, per, more):
                return self.sum(per, self.dn // 2 * per + more)

            def sum(self, per, more):
                return self.hb * per + more if more else (self.hb - 1) * per + per

        def loop(eng, step):
            for off in range(-NB, 2 * NB):
                step(0, off)
            with eng.Fori(1, HEADS - 1) as hb:
                for off in range(2 * NB):
                    step(hb, off)
            for off in range(2 * NB + LAG_T + 3):
                step(HEADS - 1, off)

        def far_pieces(j, g):
            blocks = range(CH * g, CH * g + CH)
            out = []
            for right, sel in ((1, [i for i in blocks if i <= j - 2]), (0, [i for i in blocks if i >= j + 2])):
                if sel:
                    out.append((right, (sel[0] - CH * g) * P, (sel[-1] + 1 - CH * g) * P))
            return out

        with nc.Block() as block:

            @block.sync
            def _(sp):
                sp.dma_start(rv_ends[:, 0, :], io["rel_v"][0, :].partition_broadcast(P)).then_inc(const_in, 16)
                sp.dma_start(rv_ends[:, 1, :], io["rel_v"][2 * M, :].partition_broadcast(P)).then_inc(const_in, 16)
                sp.wait_ge(const_set, 1)
                sp.dma_start(rv_win[:, 0, 0:HD], io["rel_v"][0, :].partition_broadcast(P)).then_inc(const_in, 16)
                sp.dma_start(rv_win[:, 1, 0:HD], io["rel_v"][0:M, :]).then_inc(const_in, 16)
                sp.dma_start(rv_win[:, 2, 0:HD], io["rel_v"][M:2 * M, :]).then_inc(const_in, 16)
                sp.dma_start(rv_win[:, 3, 0:HD], io["rel_v"][2 * M, :].partition_broadcast(P)).then_inc(const_in, 16)
                sp.wait_ge(const_set, 20)

                def step(hb, off):
                    if off % NB == 0:
                        x = Step(hb, off + NB)
                        if x.valid:
                            wait(sp, s1_mm, x.count(64, -64))
                            sp.dma_start(q_front[x.par][:, :], pair_rows(q_tab, x)).then_inc(qf_in[x.par], 16)
                            sp.dma_start(k_front[x.par][:, :], pair_rows(k_tab, x)).then_inc(kf_in[x.par], 16)
                    if off % NB == 2:
                        x = Step(hb, off)
                        if x.valid:
                            wait(sp, st_mm, x.count(64, -64))
                            sp.dma_start(q_back[x.par][0:ROWS, :], pair_rows(q_tab, x)).then_inc(back_in[x.par], 16)
                            sp.dma_start(k_left[x.par][0:ROWS, :], pair_rows(k_tab, x)).then_inc(back_in[x.par], 16)
                            sp.dma_start(k_right[x.par][0:ROWS, :], pair_rows(k_tab, x)).then_inc(back_in[x.par], 16)
                            wait(sp, v_built, x.count(1, 0))
                            sp.dma_start(v_raw[:, :, :], v_tab[x.n]).then_inc(v_in, 16)
                    if type(hb) is int and hb == 0 and 0 <= off < TILES:
                        wait(sp, sorted_out[off % 2], 16 * (off // 2))
                        sp.dma_start(row[off % 2][:, :], dram["xn"][off * P:(off + 1) * P, :]).then_inc(row_in[off % 2], 16)
                    if off % CH != 1:
                        return
                    x = Step(hb, off + LAG_R - 3)
                    r = x.r
                    if x.valid:
                        sp.wait_ge(r_evac, x.count(16, 4 * r + 4))
                        wait(sp, rel_in[x.par][r], x.count2(32 if r in (0, 3) else 16, 0))
                        sp.dma_start(dram["rel"][x.par, 4 * r:4 * r + 4].rearrange("s p w -> p s w"), rel[r % 2][:, :, :]).then_inc(rel_out[r], 16)
                    y = Step(hb, off - 9)
                    if y.valid:
                        sp.wait_ge(band_exp, y.count(16, 4 * y.r + 4))
                        wait(sp, win_in[y.r % 2], y.count(32, 16 * (y.r // 2 + 1) - 32))
                        sp.dma_start(dram["band_p"][y.par, 4 * y.r:4 * y.r + 4].rearrange("s p w -> p s w"),
                                     band[y.par][:, 4 * y.r:4 * y.r + 4, :]).then_inc(prob_out[y.r], 16)
                    x = Step(hb, off + LAG_R - 7)
                    r = x.r
                    if x.valid:
                        sp.wait_ge(rel_out[r], x.count(16, 16))
                        wait(sp, bandT_mm, x.count(16, 4 * r + 4 - 32))
                        wait(sp, prob_out[r], x.count(16, -16))
                        s0, s1 = 4 * r + (r == 0), 4 * r + 4 - (r == 3)
                        sp.dma_start(band[x.par][:, s0:s1, :], sheared(dram["rel"], x.par, s0, s1 - s0, WIN, WIN - 1, P, BAND)).then_inc(rel_in[x.par][r], 16)
                        if r == 0:
                            sp.dma_start(band[x.par][:, 0, P:BAND], sheared(dram["rel"], x.par, 0, 1, WIN, WIN - 1, 2 * P, BAND - P)[:, 0, :]).then_inc(rel_in[x.par][r], 16)
                        if r == 3:
                            sp.dma_start(band[x.par][:, NB - 1, 0:BAND - P], sheared(dram["rel"], x.par, NB - 1, 1, WIN, WIN - 1, P, BAND - P)[:, 0, :]).then_inc(rel_in[x.par][r], 16)
                    z = Step(hb, off - 13)
                    if z.valid:
                        sp.wait_ge(prob_out[z.r], z.count(16, 16))
                        wait(sp, winT_mm, z.count(16, 4 * z.r + 4 - 8))
                        sp.dma_start(pwin[z.r % 2][:, :, :], sheared(dram["band_p"], z.par, 4 * z.r, 4, BAND, BAND + 1, 0, NEARW)).then_inc(win_in[z.r % 2], 16)

                q_tab, k_tab, v_tab = dram["q_stack"], dram["k_stack"], dram["v"]

                def pair_rows(t, x):
                    return t[x.head, :, x.par * S:(x.par + 1) * S]

                def sheared(t, par, s, count, width, step_p, first, length):
                    return bass.AP(tensor=t.tensor, offset=t.offset + (par * NB + s) * P * width + first,
                                   ap=[[step_p, P], [P * width, count], [1, length]])

                loop(sp, step)

            @block.gpsimd
            def _(pool):
                pool.memset(rv_win[:, :, :], 0.0).then_inc(const_set, 1)
                pool.memset(zero[:, :, :], 0.0).then_inc(const_set, 1)
                for p in range(2):
                    pool.memset(rel_ends[p][:, :, :], 0.0).then_inc(const_set, 1)
                    pool.memset(part[p][:, :, :, :], LOWEST).then_inc(const_set, 1)
                    pool.memset(band[p][:, 0, 0:P], 0.0).then_inc(const_set, 1)
                    pool.memset(band[p][:, NB - 1, BAND - P:BAND], 0.0).then_inc(const_set, 1)
                    for v in (v_far[0][p], v_far[1][p], v_near[p]):
                        pool.memset(v[:, :, HD:HD + 1], 1.0)
                        pool.memset(v[:, :, HD + 1:32], 0.0).then_inc(const_set, 1)
                pool.memset(clip_mask[:, :, :], 1.0).then_inc(const_set, 1)
                pool.memset(neg_scale[:, :], -SCALE).then_inc(const_set, 1)
                pool.wait_ge(const_set, 18)
                pool.affine_select(out=clip_mask[:, 0, :], in_=clip_mask[:, 0, :], compare_op=ALU.is_gt, fill=0.0, base=0,
                                   pattern=[[1, P]], channel_multiplier=-1).then_inc(const_set, 1)
                pool.affine_select(out=clip_mask[:, 1, :], in_=clip_mask[:, 1, :], compare_op=ALU.is_ge, fill=0.0, base=0,
                                   pattern=[[-1, P]], channel_multiplier=1).then_inc(const_set, 1)
                pool.wait_ge(const_set, 20)
                pool.wait_ge(const_in, 16 * 6)

                def copied(dst, src):
                    return nc.gpsimd.tensor_tensor(dst, src, zero[:, :, :], ALU.add)

                def step(hb, off):
                    x = Step(hb, off + LAG_R - 3)
                    if off % CH == 1 and x.valid:
                        pool.wait_ge(r_evac, x.count(16, 4 * x.r + 4))
                        copied(rel_ends[x.par][:, 4 * x.r:4 * x.r + 4, 0:2], rel[x.r % 2][:, :, 0:WIN:WIN - 1]).then_inc(ends_done, 1)
                    w = Step(hb, off - LAG_T - 1)
                    if w.valid:
                        bi = order(w.s)
                        k0, k1 = int(bi == 0), 2 - int(bi == NB - 1)
                        pool.wait_ge(bandT_evac, w.count(16, w.s + 1))
                        if w.g == 0:
                            wait(pool, clip_used, w.count(4, w.r))
                        nc.gpsimd.tensor_tensor(clip_T[:, w.g, k0:k1, :],
                                                band_T[w.r % 2][:, w.g, :].rearrange("p (b c) -> p b c", b=3)[:, 2 * k0:2 * k1 - 1:2, :],
                                                clip_mask[:, k0:k1, :], ALU.mult).then_inc(clip_ready, 1)
                    y = Step(hb, off - 3)
                    if off % CH == 3 and y.valid:
                        g = y.count(4, y.r)
                        k = y.count(20, 5 * y.r)
                        four = slice(4 * y.r, 4 * y.r + 4)
                        t = shb[y.r % 2][:, :, :].rearrange("p g (k t) -> p g k t", k=2)
                        pool.wait_ge(rmax_ready, g + 1)
                        wait(pool, band_exp, y.count(16, 4 * y.r + 4 - 32))
                        nc.gpsimd.tensor_tensor(negm[y.par][:, four], rmax[y.par][:, four], neg_scale[:, 0:1].to_broadcast([P, CH]),
                                                ALU.mult).then_inc(negm_ready, 1)
                        wait(pool, rows_tp, y.count(4, y.r - 1))
                        nc.gpsimd.tensor_tensor(sh[:, :, :], rel_ends[y.par][:, four, 0:2],
                                                rmax[y.par][:, four].unsqueeze(2).to_broadcast([P, CH, 2]), ALU.subtract).then_inc(shift_link, 1)
                        pool.wait_ge(shift_link, k + 1)
                        copied(t[:, :, :, 0], sh[:, :, :]).then_inc(shift_link, 1)
                        pool.wait_ge(shift_link, k + 2)
                        nc.gpsimd.tensor_tensor(sh[:, :, :], sh[:, :, :], t[:, :, :, 0], ALU.subtract).then_inc(shift_link, 1)
                        pool.wait_ge(shift_link, k + 3)
                        copied(t[:, :, :, 1], sh[:, :, :]).then_inc(shift_link, 1)
                        pool.wait_ge(shift_link, k + 4)
                        nc.gpsimd.tensor_tensor(sh[:, :, :], sh[:, :, :], t[:, :, :, 1], ALU.subtract).then_inc(shift_link, 1)
                        pool.wait_ge(shift_link, k + 5)
                        copied(t[:, :, :, 2], sh[:, :, :]).then_inc(shift_ready, 1)
                    z = Step(hb, off)
                    if off % NB == 4 and z.valid:
                        pool.wait_ge(v_in, z.count(16, 16))
                        wait(pool, band_pv, z.count(4, -4))
                        for k in range(2):
                            nc.gpsimd.tensor_tensor(v_far[k][z.par][:, :, 0:HD], v_raw[:, :, :],
                                                    rv_ends[:, k, :].unsqueeze(1).to_broadcast([P, NB, HD]), ALU.add)
                        nc.gpsimd.tensor_copy(v_near[z.par][:, :, 0:HD], v_raw[:, :, :]).then_inc(v_built, 1)

                    if type(hb) is int and hb == 0 and 0 <= off < TILES:
                        pool.wait_ge(row_in[off % 2], 16 * (off // 2 + 1))
                        pool.indirect_dma_start(out=dram["xs"][:, :], out_offset=bass.IndirectOffsetOnAxis(ap=pos_i[:, off:off + 1], axis=0),
                                                in_=row[off % 2][:, :], in_offset=None).then_inc(sorted_out[off % 2], 16)

                loop(pool, step)
                for h in range(2):
                    pool.wait_ge(sorted_out[h], 16 * TILES // 2)

            @block.tensor
            def _(pe):
                pe.wait_ge(const_set, 20)
                pe.wait_ge(const_in, 16 * 6)

                def step(hb, off):
                    a = Step(hb, off)
                    t = Step(hb, off - LAG_T)
                    x = Step(hb, off + LAG_R)
                    w = Step(hb, off - LAG_T - 1)
                    y = Step(hb, off - 5)
                    o = Step(hb, off - LAG_T - 2)
                    i = order(a.s)
                    def shift_rows():
                        pe.wait_ge(shift_ready, y.count(4, y.r + 1))
                        wait(pe, rows_copied, y.count(4, y.r))
                        if w.valid:
                            wait(pe, winT_evac, w.count(16, w.s + 1))
                        for g in range(CH):
                            mm = nc.tensor.transpose(prow[0:SHIFTS, g * P:(g + 1) * P], shb[y.r % 2][:, g, :], con["ident_bf"][:, :])
                        mm.then_inc(rows_tp, 1)

                    def turn_back():
                        pe.wait_ge(out_evac, o.count(1, 1))
                        wait(pe, r_evac, x.count(16, x.s + 1) if x.valid else NBH * 16)
                        for r in range(CH):
                            mm = nc.tensor.transpose(prel[:, r * P:(r + 1) * P], outT[:, r * P:(r + 1) * P], con["ident"][:, :])
                        mm.then_inc(back_mm, 1)

                    def weighted(r, g, values, probs, last=False):
                        return nc.tensor.matmul(pout[32 * g:32 * g + 32, r * P:(r + 1) * P], values, probs, start=False, stop=last,
                                                skip_group_check=True)

                    def clipped_values(r):
                        pe.wait_ge(clip_ready, w.count(16, 4 * r + 4))
                        for k in range(2):
                            for g in range(CH):
                                if 0 <= CH * g + r + 2 * k - 1 < NB:
                                    mm = weighted(r, g, rv_win[:, 3 * k, :], clip_T[:, g, k, :])
                        mm.then_inc(clip_used, 1)

                    def band_values(r, parts):
                        for b in parts:
                            for g in range(CH):
                                j = CH * g + r + b - 1
                                if 0 <= j < NB:
                                    weighted(r, g, v_near[w.par][:, j, :], band_T[r % 2][:, g, b * P:(b + 1) * P])

                    def near_values(r):
                        pe.wait_ge(winT_evac, w.count(16, 4 * r + 4))
                        for b in range(2):
                            for g in range(CH):
                                mm = weighted(r, g, rv_win[:, 1 + b, :], pwin_T[r % 2][:, g, b * P:(b + 1) * P], last=(r == CH - 1 and b == 1))
                        mm.then_inc(band_pv, 1)

                    def far_values():
                        if w.s == 0:
                            pe.wait_ge(v_built, w.count(1, 1))
                            wait(pe, out_evac, w.count(1, 0))
                        pe.wait_ge(exp_done, w.count(64, 4 * w.s + 4))
                        for nth in range(2):
                            for g in range(CH):
                                pieces = far_pieces(w.s, g)
                                if nth < len(pieces):
                                    right, c0, c1 = pieces[nth]
                                    mm = nc.tensor.matmul(pout[32 * g:32 * g + 32, c0:c1], v_far[right][w.par][:, w.s, :], far_T[w.s % 2][:, g, c0:c1],
                                                          start=(w.s == 0 and nth == 0), stop=False, skip_group_check=True)
                        mm.then_inc(pv_done, 1)

                    if t.valid and t.s == 0:
                        if type(hb) is int and t.n == 0:
                            pe.wait_ge(shift_set, 8)
                        pe.wait_ge(back_in[t.par], t.count2(48, 48))
                        pe.wait_ge(rows_copied, t.count(4, 4))
                    for u in range(CH):
                        if a.valid:
                            if a.s == 0 and u == 0:
                                pe.wait_ge(qf_in[a.par], a.count2(16, 16))
                                pe.wait_ge(kf_in[a.par], a.count2(16, 16))
                            wait(pe, s1_used, a.count(64, 4 * a.s + u - 1))
                            nc.tensor.matmul(ps1[u % 2][:, :], q_front[a.par][:, i * P:(i + 1) * P], k_front[a.par][:, u * CW:(u + 1) * CW],
                                             start=True, stop=True).then_inc(s1_mm, 1)
                        if t.valid:
                            wait(pe, exp_done, t.count(64, 4 * t.s + u - 1))
                            for right, c0, c1 in far_pieces(t.s, u):
                                k = (k_right if right else k_left)[t.par]
                                mm = nc.tensor.matmul(pst[u % 2][:, c0:c1], k[:, t.s * P:(t.s + 1) * P], q_back[t.par][:, u * CW + c0:u * CW + c1],
                                                      start=True, stop=True)
                            mm.then_inc(st_mm, 1)
                        if u == 1 and w.valid:
                            far_values()
                        if u == 1 and x.valid:
                            if x.s == 0:
                                pe.wait_ge(qf_in[x.par], x.count2(16, 16))
                            wait(pe, r_evac, x.count(16, x.s))
                            if t.s == 2:
                                wait(pe, norm_done, t.count(1, 0))
                            xi = order(x.s)
                            nc.tensor.matmul(prel[:, :], q_front[x.par][:, xi * P:(xi + 1) * P], con["rel_k"][:, :], start=True, stop=True).then_inc(r_mm, 1)
                        if u == 1 and off % CH == 1 and y.valid:
                            shift_rows()
                        if u == 2 and o.s == NB - 1 and o.valid:
                            turn_back()
                    if t.valid:
                        bi = order(t.s)
                        pe.wait_ge(band_exp, t.count(16, t.s + 1))
                        wait(pe, bandT_evac, t.count(16, t.s))
                        for j in band_blocks(bi):
                            b = j - bi + 1
                            mm = nc.tensor.transpose(pband[:, b * P:(b + 1) * P], band[t.par][:, t.s, b * P:(b + 1) * P], con["ident"][:, :])
                        mm.then_inc(bandT_mm, 1)
                        if t.g == 0:
                            pe.wait_ge(win_in[t.r % 2], t.count(32, 16 * (t.r // 2 + 1)))
                        wait(pe, winT_evac, t.count(16, t.s))
                        if off % CH == 1 and y.valid:
                            pe.wait_ge(rows_copied, y.count(4, y.r + 1))
                        for b in range(2):
                            mm = nc.tensor.transpose(pnear[:, b * P:(b + 1) * P], pwin[t.r % 2][:, t.g, b * P:(b + 1) * P], con["ident"][:, :])
                        mm.then_inc(winT_mm, 1)
                    if w.valid:
                        if w.g == CH - 1:
                            clipped_values(w.r)
                            if w.r == CH - 1:
                                band_values(w.r, (0, 1, 2))
                                near_values(w.r)
                        elif w.r > 0:
                            if w.g < 2:
                                band_values(w.r - 1, ((0, 1), (2,))[w.g])
                            else:
                                near_values(w.r - 1)

                loop(pe, step)

            @block.vector
            def _(dve):
                for p in range(2):
                    nc.vector.memset(k_left[p][ROWS:ALLROWS, :], 0.0).then_inc(shift_set, 1)
                    nc.vector.memset(k_right[p][ROWS:ALLROWS, :], 1.0).then_inc(shift_set, 1)
                dve.wait_ge(shift_set, 4)
                for p in range(2):
                    nc.vector.memset(k_left[p][ROWS:ROWS + 3, :], 1.0).then_inc(shift_set, 1)
                    nc.vector.memset(k_right[p][ROWS:ROWS + 3, :], 0.0).then_inc(shift_set, 1)
                dve.wait_ge(const_set, 20)

                def step(hb, off):
                    a = Step(hb, off)
                    i = order(a.s)
                    w = Step(hb, off - LAG_T - 1)

                    def near():
                        dve.wait_ge(winT_mm, w.count(16, w.s + 1))
                        if w.g == 0:
                            wait(dve, band_pv, w.count(4, w.r - 1))
                        nc.vector.tensor_copy(pwin_T[w.r % 2][:, w.g, :], pnear[:, :]).then_inc(winT_evac, 1)

                    for u in range(CH):
                        if a.valid and a.g == 0 and u == 0:
                            dve.wait_ge(rel_in[a.par][a.r], a.count2(32 if a.r in (0, 3) else 16, 32 if a.r in (0, 3) else 16))
                        if a.valid:
                            dve.wait_ge(s1_mm, a.count(64, 4 * a.s + u + 1))
                            blocks = range(CH * u, CH * u + CH)
                            pieces = [(0, [j for j in blocks if j <= i - 2]), (1, [j for j in blocks if j >= i + 2]),
                                      (2, [j for j in blocks if abs(j - i) <= 1])]
                            pieces = [(kind, sel) for kind, sel in pieces if sel]
                            for kind, sel in pieces:
                                src = ps1[u % 2][:, (sel[0] - CH * u) * P:(sel[-1] + 1 - CH * u) * P]
                                best = part[a.par][:, a.s, kind, u:u + 1]
                                if kind == 2:
                                    b = sel[0] - i + 1
                                    dst = band[a.par][:, a.s, b * P:(b + len(sel)) * P]
                                    ins = nc.vector.tensor_tensor_reduce(dst, src, dst, 1.0, LOWEST, ALU.add, ALU.max, best)
                                else:
                                    ins = nc.vector.tensor_reduce(best, src, AX_X, ALU.max)
                            ins.then_inc(s1_used, 1)
                        if u == 1 and w.valid:
                            near()
                    o = Step(hb, off - LAG_T - 2)
                    if o.s == NB - 1 and o.valid:
                        back = prel[:, :].rearrange("p (r g d) -> p r g d", r=CH, g=CH)
                        rv = rden[:, :].rearrange("p (r g) -> p r g", r=CH)
                        dve.wait_ge(back_mm, o.count(1, 1))
                        nc.vector.reciprocal(rv, back[:, :, :, HD]).then_inc(den_ready, 1)
                        dve.wait_ge(den_ready, o.count(1, 1))
                        dst = attn[:, o.n, :, :].rearrange("p (g r) d -> p r g d", g=CH)
                        for r in range(CH):
                            ins = nc.vector.tensor_tensor(dst[:, r], back[:, r, :, 0:HD], rv[:, r].unsqueeze(2).to_broadcast([P, CH, HD]), ALU.mult)
                        ins.then_inc(norm_done, 1)
                    if a.valid and a.g == CH - 1:
                        four = slice(4 * a.r, 4 * a.r + 4)
                        k = a.count(8, 2 * a.r)
                        dve.wait_ge(s1_used, a.count(64, 16 * a.r + 16))
                        nc.vector.tensor_reduce(lm[:, :, :], part[a.par][:, four, :, :], AX_X, ALU.max).then_inc(max_link, 1)
                        dve.wait_ge(max_link, k + 1)
                        dve.wait_ge(ends_done, a.count(4, a.r + 1))
                        nc.vector.tensor_tensor(lm[:, :, :], lm[:, :, :], rel_ends[a.par][:, four, :], ALU.add).then_inc(max_link, 1)
                        dve.wait_ge(max_link, k + 2)
                        wait(dve, shift_ready, a.count(4, a.r + 1 - 8))
                        nc.vector.tensor_reduce(rmax[a.par][:, four], lm[:, :, :], AX_X, ALU.max).then_inc(rmax_ready, 1)

                loop(dve, step)

            @block.scalar
            def _(act):
                def step(hb, off):
                    e = Step(hb, off - LAG_T - 1 - NB)
                    x = Step(hb, off + LAG_R)
                    t = Step(hb, off - LAG_T)
                    y = Step(hb, off - 5)
                    w = Step(hb, off - LAG_T - 1)

                    def finished():
                        act.wait_ge(band_pv, e.count(4, 4))
                        nc.scalar.activation(outT[:, :], pout[:, :], ACT.Copy).then_inc(out_evac, 1)

                    def turned():
                        bl = band_blocks(order(w.s))
                        c0, c1 = (bl[0] - order(w.s) + 1) * P, (bl[-1] - order(w.s) + 2) * P
                        act.wait_ge(bandT_mm, w.count(16, w.s + 1))
                        if w.g == 0:
                            wait(act, band_pv, w.count(4, w.r - 1))
                        nc.scalar.activation(band_T[w.r % 2][:, w.g, c0:c1], pband[:, c0:c1], ACT.Copy).then_inc(bandT_evac, 1)

                    def relative():
                        act.wait_ge(r_mm, x.count(16, x.s + 1))
                        if x.g == 0:
                            before = Step(hb, off + LAG_R - 8)
                            wait(act, rel_out[before.r], before.count(16, 16) if before.valid else 0)
                            wait(act, ends_done, x.count(4, x.r - 1))
                        nc.scalar.activation(rel[x.r % 2][:, x.g, :], prel[:, :], ACT.Copy).then_inc(r_evac, 1)

                    def shift_rows():
                        act.wait_ge(rows_tp, y.count(4, y.r + 1))
                        rows = q_back[y.par][ROWS:ALLROWS, :].rearrange("k (g r c) -> k g r c", g=CH, r=CH)[:, :, y.r, :]
                        nc.scalar.activation(rows, prow.rearrange("k (g c) -> k g c", g=CH), ACT.Copy).then_inc(rows_copied, 1)

                    if t.valid:
                        wait(act, pv_done, t.count(16, t.s - 1))
                    for u in range(CH):
                        if t.valid:
                            act.wait_ge(st_mm, t.count(64, 4 * t.s + u + 1))
                            for _, c0, c1 in far_pieces(t.s, u):
                                ins = nc.scalar.activation(far_T[t.s % 2][:, u, c0:c1], pst[u % 2][:, c0:c1], ACT.Exp, scale=SCALE)
                            ins.then_inc(exp_done, 1)
                        if u == 0 and e.s == 0 and e.valid:
                            finished()
                        if u == 1 and w.valid:
                            turned()
                        if u == 1 and x.valid:
                            relative()
                        if u == 1 and off % CH == 1 and y.valid:
                            shift_rows()
                    if y.valid:
                        bl = band_blocks(order(y.s))
                        c0, c1 = (bl[0] - order(y.s) + 1) * P, (bl[-1] - order(y.s) + 2) * P
                        if y.g == 0:
                            act.wait_ge(negm_ready, y.count(4, y.r + 1))
                        nc.scalar.activation(band[y.par][:, y.s, c0:c1], band[y.par][:, y.s, c0:c1], ACT.Exp,
                                             bias=negm[y.par][:, y.s:y.s + 1], scale=SCALE).then_inc(band_exp, 1)

                loop(act, step)


def experts(nc, io, dram, con, attn, expert_i):
    with ExitStack() as ctx:
        def sb(name, shape, dt):
            return ctx.enter_context(nc.sbuf_tensor(name, shape, dt))

        def sem(name):
            return ctx.enter_context(nc.semaphore(name))

        def two(name, shape, dt):
            return [sb(f"{name}{i}", shape, dt) for i in range(2)]

        w1 = sb("w1", [P, NE, DC, FF], F32)
        w2 = sb("w2", [P, NE, FC, D], F32)
        wo = sb("wo", [P, DC, D], F32)
        bo = sb("bo", [P, D], F32)
        at = two("at", [P, D], F32)
        aT = two("aT", [P, DC, P], F32)
        xs = two("xs", [P, D], F32)
        xsT = two("xsT", [P, DC, P], F32)
        hid = two("hid", [P, FF], F32)
        hT = two("hT", [P, FC, P], F32)
        ys = two("ys", [P, D], F32)
        px = ctx.enter_context(nc.psum_tensor("px", [P, 512], F32))
        ph = [ctx.enter_context(nc.psum_tensor(f"ph{i}", [P, 512], F32)) for i in range(2)]
        pt = [ctx.enter_context(nc.psum_tensor(f"pt{i}", [P, 512], F32)) for i in range(2)]
        py = ctx.enter_context(nc.psum_tensor("py", [P, 512], F32))
        pa, po = pt, ph

        wo_in = sem("wo_in")
        at_ready = sem("at_ready")
        a_tp = sem("a_tp")
        a_evac = sem("a_evac")
        o_mm = sem("o_mm")
        o_evac = sem("o_evac")
        w1_in = sem("w1_in")
        w2_in = sem("w2_in")
        xs_in = [sem(f"xs_in{i}") for i in range(2)]
        x_tp = sem("x_tp")
        x_evac = sem("x_evac")
        h_mm = sem("h_mm")
        gelu_done = sem("gelu_done")
        h_tp = sem("h_tp")
        hT_evac = sem("hT_evac")
        y_mm = sem("y_mm")
        y_evac = sem("y_evac")
        y_out = [sem(f"y_out{i}") for i in range(2)]

        def token_tile(t):
            return attn[:, :, :, :].rearrange("p (h b) i d -> p h (b i) d", b=B)[:, :, bass.ds(t, 1), :].rearrange("p h t d -> p h (t d)")

        def heads(ap):
            return ap.rearrange("p (h d) -> p h d", h=HEADS)

        with nc.Block() as block:

            @block.sync
            def _(sp):
                sp.dma_start(wo[:, :, :], io["woT"].rearrange("(c p) n -> p c n", p=P)).then_inc(wo_in, 16)
                sp.dma_start(bo[:, :], io["bo"].partition_broadcast(P)).then_inc(wo_in, 16)
                for h in range(2):
                    sp.dma_start(xs[h][:, :], dram["xs"][h * P:(h + 1) * P, :]).then_inc(xs_in[h], 16)
                for e in range(NE):
                    sp.dma_start(w1[:, e], io["w1"][e].rearrange("(c p) f -> p c f", p=P)).then_inc(w1_in, 16)
                for e in range(NE):
                    sp.dma_start(w2[:, e], io["w2"][e].rearrange("(c p) d -> p c d", p=P)).then_inc(w2_in, 16)

                def load(T, h):
                    sp.wait_ge(x_tp, T + 1)
                    sp.dma_start(xs[h][:, :], dram["xs"][bass.ds((T + 2) * P, P), :]).then_inc(xs_in[h], 16)

                def store(T, h):
                    sp.wait_ge(y_evac, T + 1)
                    sp.dma_start(dram["ys"][bass.ds(T * P, P), :], ys[h][:, :]).then_inc(y_out[h], 16)

                with sp.Fori(0, XT // 2 - 1) as pair_i:
                    T0 = pair_i * 2
                    for h in range(2):
                        load(T0 + h, h)
                    for h in range(2):
                        store(T0 + h, h)
                store(XT - 2, 0)
                store(XT - 1, 1)
                for h in range(2):
                    sp.wait_ge(y_out[h], 16 * XT // 2)

            @block.tensor
            def _(pe):
                def turn_attn(t, h):
                    pe.wait_ge(at_ready, t + 1)
                    wait(pe, a_evac, t - 1)
                    for d in range(DC):
                        mm = nc.tensor.transpose(pa[h][:, d * P:(d + 1) * P], at[h][:, d * P:(d + 1) * P], con["ident"][:, :])
                    mm.then_inc(a_tp, 1)

                def project_out(t, h):
                    pe.wait_ge(a_evac, t + 1)
                    wait(pe, o_evac, t - 1)
                    for d in range(DC):
                        mm = nc.tensor.matmul(po[h][:, 0:D], aT[h][:, d, :], wo[:, d, :], start=(d == 0), stop=(d == DC - 1))
                    mm.then_inc(o_mm, 1)

                pe.wait_ge(wo_in, 32)
                turn_attn(0, 0)
                turn_attn(1, 1)
                project_out(0, 0)
                with pe.Fori(1, TILES // 2) as pair_i:
                    t0 = pair_i * 2
                    turn_attn(t0, 0)
                    project_out(t0 - 1, 1)
                    turn_attn(t0 + 1, 1)
                    project_out(t0, 0)
                project_out(TILES - 1, 1)

                def turn_x(T, xs_count, h):
                    pe.wait_ge(xs_in[h], xs_count)
                    wait(pe, x_evac, T)
                    for d in range(DC):
                        mm = nc.tensor.transpose(px[:, d * P:(d + 1) * P], xs[h][:, d * P:(d + 1) * P], con["ident"][:, :])
                    mm.then_inc(x_tp, 1)

                def hidden(T, h, e, half):
                    if half == 0:
                        pe.wait_ge(x_evac, T + 1)
                    wait(pe, gelu_done, T * 2 + half - 1)
                    for d in range(DC):
                        mm = nc.tensor.matmul(ph[half][:, :], xsT[h][:, d, :], w1[:, e, d, half * 512:(half + 1) * 512],
                                              start=(d == 0), stop=(d == DC - 1))
                    mm.then_inc(h_mm, 1)

                def turn_hidden(T, h, half):
                    pe.wait_ge(gelu_done, T * 2 + (half + 1))
                    wait(pe, hT_evac, T * 2 + half - 1)
                    for k in range(4):
                        j = half * 4 + k
                        mm = nc.tensor.transpose(pt[half][:, k * P:(k + 1) * P], hid[h][:, j * P:(j + 1) * P], con["ident"][:, :])
                    mm.then_inc(h_tp, 1)

                def output(T, h, e):
                    wait(pe, y_evac, T)
                    for j in range(FC):
                        if j % 4 == 0:
                            pe.wait_ge(hT_evac, T * 2 + (j // 4 + 1))
                        mm = nc.tensor.matmul(py[:, 0:D], hT[h][:, j, :], w2[:, e, j, :], start=(j == 0), stop=(j == FC - 1))
                    mm.then_inc(y_mm, 1)

                def expert(T):
                    return pe.value_load(expert_i[0:1, bass.ds(T, 1)], min_val=0, max_val=NE - 1)

                def step(T, h, e, e_before, next_count):
                    for half in range(2):
                        hidden(T, h, e, half)
                        turn_hidden(T - 1, 1 - h, half)
                    if next_count is not None:
                        turn_x(T + 1, next_count, 1 - h)
                    output(T - 1, 1 - h, e_before)

                wait(pe, o_evac, TILES)
                turn_x(0, 16, 0)
                pe.wait_ge(w1_in, 16 * NE)
                e0 = expert(0)
                for half in range(2):
                    hidden(0, 0, e0, half)
                turn_x(1, 16, 1)
                pe.wait_ge(w2_in, 16 * NE)
                step(1, 1, expert(1), e0, 32)
                with pe.Fori(1, XT // 2 - 1) as pair_i:
                    T0 = pair_i * 2
                    e_last, e0, e1 = expert(T0 - 1), expert(T0), expert(T0 + 1)
                    step(T0, 0, e0, e_last, T0 * 8 + 16)
                    step(T0 + 1, 1, e1, e0, T0 * 8 + 32)
                e_last, e0, e1 = expert(XT - 3), expert(XT - 2), expert(XT - 1)
                step(XT - 2, 0, e0, e_last, XT // 2 * 16)
                step(XT - 1, 1, e1, e0, None)
                for half in range(2):
                    turn_hidden(XT - 1, 1, half)
                output(XT - 1, 1, e1)

            @block.scalar
            def _(act):
                def turn_attn(t, h):
                    wait(act, o_mm, t - 1)
                    act.wait_ge(a_tp, t + 1)
                    nc.scalar.activation(aT[h][:, :, :], pa[h][:, 0:D].rearrange("p (c m) -> p c m", c=DC), ACT.Copy).then_inc(a_evac, 1)

                turn_attn(0, 0)
                turn_attn(1, 1)
                with act.Fori(1, TILES // 2) as pair_i:
                    t0 = pair_i * 2
                    turn_attn(t0, 0)
                    turn_attn(t0 + 1, 1)

                def hidden(T, T0, h):
                    for half in range(2):
                        act.wait_ge(h_mm, T0 * 2 + (h * 2 + half + 1))
                        wait(act, h_tp, T * 2 + half - 3)
                        nc.scalar.activation(hid[h][:, half * 512:(half + 1) * 512], ph[half][:, :], ACT.Gelu_apprx_tanh).then_inc(gelu_done, 1)

                hidden(0, 0, 0)
                hidden(1, 0, 1)
                with act.Fori(1, XT // 2) as pair_i:
                    T0 = pair_i * 2
                    hidden(T0, T0, 0)
                    hidden(T0 + 1, T0, 1)

            @block.vector
            def _(dve):
                def gather(t, h):
                    wait(dve, a_tp, t - 1)
                    nc.vector.tensor_copy(heads(at[h][:, :]), token_tile(t)).then_inc(at_ready, 1)

                def add_bias(t, h):
                    dve.wait_ge(o_mm, t + 1)
                    nc.vector.tensor_tensor(token_tile(t), heads(po[h][:, 0:D]), heads(bo[:, :]), ALU.add).then_inc(o_evac, 1)

                dve.wait_ge(wo_in, 32)
                gather(0, 0)
                gather(1, 1)
                with dve.Fori(1, TILES // 2) as pair_i:
                    t0 = pair_i * 2
                    gather(t0, 0)
                    add_bias(t0 - 2, 0)
                    gather(t0 + 1, 1)
                    add_bias(t0 - 1, 1)
                add_bias(TILES - 2, 0)
                add_bias(TILES - 1, 1)

                def turn_x(T, h):
                    dve.wait_ge(x_tp, T + 1)
                    wait(dve, h_mm, T * 2 - 2)
                    nc.vector.tensor_copy(xsT[h][:, :, :], px[:, 0:D].rearrange("p (c m) -> p c m", c=DC)).then_inc(x_evac, 1)

                def turn_hidden(T, h):
                    for half in range(2):
                        dve.wait_ge(h_tp, T * 2 + (half + 1))
                        wait(dve, y_mm, T - 1)
                        nc.vector.tensor_copy(hT[h][:, half * 4:(half + 1) * 4, :], pt[half][:, :].rearrange("p (c m) -> p c m", c=4)).then_inc(hT_evac, 1)

                def output(T, h, out_count):
                    dve.wait_ge(y_mm, T + 1)
                    wait(dve, y_out[h], out_count)
                    nc.vector.tensor_copy(ys[h][:, :], py[:, 0:D]).then_inc(y_evac, 1)

                def step(T, h, out_count, more=True):
                    turn_hidden(T - 1, 1 - h)
                    if more:
                        turn_x(T + 1, 1 - h)
                    output(T - 1, 1 - h, out_count)

                turn_x(0, 0)
                turn_x(1, 1)
                step(1, 1, 0)
                step(2, 0, 0)
                step(3, 1, 16)
                with dve.Fori(2, XT // 2 - 1) as pair_i:
                    T0 = pair_i * 2
                    step(T0, 0, T0 * 8 - 16)
                    step(T0 + 1, 1, T0 * 8)
                step(XT - 2, 0, XT // 2 * 16 - 32)
                step(XT - 1, 1, XT // 2 * 16 - 16, more=False)
                turn_hidden(XT - 1, 1)
                output(XT - 1, 1, XT // 2 * 16 - 16)


def finish(nc, io, dram, attn, pos_i, out):
    GROUP = 4
    GROUPS = TILES // GROUP
    with ExitStack() as ctx:
        def sb(name, shape, dt):
            return ctx.enter_context(nc.sbuf_tensor(name, shape, dt))

        def sem(name):
            return ctx.enter_context(nc.semaphore(name))

        x_in = sb("x_in", [P, TILES, D], F32)
        y_all = sb("y_all", [P, TILES, D], F32)

        x_ld = [sem(f"x_ld{g}") for g in range(GROUPS)]
        y_ld = [sem(f"y_ld{g}") for g in range(GROUPS)]
        gate_ready = sem("gate_ready")
        gated = sem("gated")
        res_ready = sem("res_ready")
        stored = sem("stored")
        x_v = io["x"].rearrange("b (t p) d -> p (b t) d", p=P)
        out_v = out.rearrange("b (t p) d -> p (b t) d", p=P)

        def tiles(g):
            return slice(g * GROUP, (g + 1) * GROUP)

        with nc.Block() as block:

            @block.sync
            def _(sp):
                for g in range(GROUPS):
                    sp.dma_start(x_in[:, tiles(g), :], x_v[:, tiles(g), :]).then_inc(x_ld[g], 16)
                for g in range(GROUPS):
                    sp.wait_ge(res_ready, g + 1)
                    sp.dma_start(out_v[:, tiles(g), :], y_all[:, tiles(g), :]).then_inc(stored, 16)
                sp.wait_ge(stored, 16 * GROUPS)

            @block.gpsimd
            def _(pool):
                for t in range(TILES):
                    pool.indirect_dma_start(out=y_all[:, t, :], out_offset=None, in_=dram["ys"][:, :],
                                            in_offset=bass.IndirectOffsetOnAxis(ap=pos_i[:, t:t + 1], axis=0)).then_inc(y_ld[t // GROUP], 16)

            @block.scalar
            def _(act):
                for g in range(GROUPS):
                    act.wait_ge(y_ld[g], 16 * GROUP)
                    nc.scalar.activation(y_all[:, tiles(g), :], y_all[:, tiles(g), :], ACT.Silu).then_inc(gate_ready, 1)

            @block.vector
            def _(dve):
                s_all = attn[:, :, :, :].rearrange("p (h b) i d -> p h (b i) d", b=B)
                for g in range(GROUPS):
                    dve.wait_ge(gate_ready, g + 1)
                    y = y_all[:, tiles(g), :]
                    for k in range(GROUP):
                        t = g * GROUP + k
                        ins = nc.vector.tensor_tensor(y_all[:, t, :].rearrange("p (h d) -> p h d", h=HEADS),
                                                      y_all[:, t, :].rearrange("p (h d) -> p h d", h=HEADS), s_all[:, :, t, :], ALU.mult)
                    ins.then_inc(gated, 1)
                    dve.wait_ge(gated, g + 1)
                    dve.wait_ge(x_ld[g], 16)
                    nc.vector.tensor_tensor(y, y, x_in[:, tiles(g), :], ALU.add).then_inc(res_ready, 1)


def build(nc, io, out):
    def scratch(name, shape, dt):
        return nc.dram_tensor(name, shape, dt, kind="Internal").ap()

    dram = dict(
        q_stack=scratch("q_stack", [HEADS, ROWS, B * S], BF16),
        k_stack=scratch("k_stack", [HEADS, ROWS, B * S], BF16),
        v=scratch("v_pairs", [NBH, P, NB, HD], F32),
        rel=scratch("rel_scores", [2, NB, P, WIN], F32),
        band_p=scratch("band_probs", [2, NB, P, BAND], F32),
        xn=scratch("x_norm", [TILES * P, D], F32),
        xs=scratch("x_sorted", [XT * P, D], F32),
        ys=scratch("y_sorted", [XT * P, D], F32),
    )
    with ExitStack() as ctx:
        def sb(name, shape, dt):
            return ctx.enter_context(nc.sbuf_tensor(name, shape, dt))

        con = dict(ident=sb("ident", [P, P], F32), ident_bf=sb("ident_bf", [P, P], BF16), rel_k=sb("rel_k", [ROWS, WIN], BF16))
        pos_i = sb("pos_i", [P, TILES], I32)
        expert_i = sb("expert_i", [P, XT], I32)
        with ExitStack() as early:
            lg_all = early.enter_context(nc.sbuf_tensor("lg_all", [P, TILES, NE], F32))
            project(nc, io, dram, con, lg_all)
            route(nc, lg_all, pos_i, expert_i)
        attn = sb("attn", [P, NBH, NB, HD], F32)
        attend(nc, io, dram, con, pos_i, attn)
        experts(nc, io, dram, con, attn, expert_i)
        finish(nc, io, dram, attn, pos_i, out)


_INS = ["x", "wqT", "wkT", "wvT", "wg", "bq", "bk", "bv", "bg", "rel_kT", "rel_v", "woT", "bo", "w1", "w2"]


def kernel(**inputs):
    import numpy as _np
    import concourse.bacc as _bacc
    from concourse import mybir as _mybir
    from concourse.bass_utils import run_bass_kernel_spmd as _run

    a = {k: _np.asarray(v) for k, v in inputs.items()}
    host = {
        "x": a["L0_attn_x"], "wqT": a["L0_attn_Wq"].T, "wkT": a["L0_attn_Wk"].T, "wvT": a["L0_attn_Wv"].T, "wg": a["L0_ffn_Wg"],
        "bq": a["L0_attn_bq"].reshape(DC, P).T, "bk": a["L0_attn_bk"].reshape(DC, P).T, "bv": a["L0_attn_bv"], "bg": a["L0_ffn_bg"],
        "rel_kT": a["L0_attn_rel_k"].T, "rel_v": a["L0_attn_rel_v"], "woT": a["L0_attn_Wo"].T, "bo": a["L0_attn_bo"],
        "w1": a["L0_ffn_W1"], "w2": a["L0_ffn_W2"],
    }
    nc = _bacc.Bacc("TRN2", target_bir_lowering=False, num_devices=1)
    nc.disable_value_cache = True
    arrays, io = {}, {}
    for name in _INS:
        arr = _np.ascontiguousarray(host[name])
        arrays[f"in_{name}_dram"] = arr
        io[name] = nc.dram_tensor(f"in_{name}_dram", arr.shape, _mybir.dt.from_np(arr.dtype), kind="ExternalInput").ap()
    out = nc.dram_tensor("out_dram", (B, S, D), F32, kind="ExternalOutput").ap()
    build(nc, io, out)
    r = _run(nc, [arrays], core_ids=[0])
    return r.results[0]["out_dram"]
```

```python
from contextlib import ExitStack

import concourse.bass as bass
from concourse import mybir

F32 = mybir.dt.float32
BF16 = mybir.dt.bfloat16
I32 = mybir.dt.int32
ALU = mybir.AluOpType
ACT = mybir.ActivationFunctionType
AX_X = mybir.AxisListType.X

P = 128
B, S, D = 2, 2048, 256
HEADS, HD = 16, 16
NBH = HEADS * B
NB = S // P
TILES = B * S // P
DC = D // P
M = 128
NE, FF = 8, 1024
FC = FF // P
XT = TILES + NE - 1
EPS = 1e-5
SCALE = HD ** -0.5
LOWEST = -3.0e38

QTERM = (0, 0, 0, 1, 1, 2)
KTERM = (0, 1, 2, 0, 1, 0)
ROWS = len(QTERM) * HD
SHIFTS = 6
ALLROWS = ROWS + SHIFTS

BAND = 3 * P
RELS = 2 * M + 1
WIN = 4 * P
NEARW = 2 * M
CH = 4
CW = S // CH

LAG_R = 14
LAG_T = 18
LAG_O = LAG_T + 5


def order(s):
    return s // CH + CH * (s % CH)


def band_blocks(i):
    return [j for j in (i - 1, i, i + 1) if 0 <= j < NB]


def runs(blocks):
    out = []
    for b in blocks:
        if out and out[-1][0] + out[-1][1] == b:
            out[-1][1] += 1
        else:
            out.append([b, 1])
    return out


def wait(eng, sem, value):
    if not (isinstance(value, int) and value <= 0):
        eng.wait_ge(sem, value)


def chain(eng, sem):
    count = [0]

    def link(ins):
        count[0] += 1
        ins.then_inc(sem, 1)
        eng.wait_ge(sem, count[0])

    return link


def project(nc, io, dram, con, lg_all):
    CT = 4
    CHUNKS = TILES // CT
    QT = 2 * CT
    PAIRS = CHUNKS // 2
    CTOK = CT * P
    HALF = HEADS // DC
    FIRST, REST = slice(0, QT), slice(QT, TILES)
    STACK_COUNT = 16 * 2 * len(QTERM)
    with ExitStack() as ctx:
        def sb(name, shape, dt):
            return ctx.enter_context(nc.sbuf_tensor(name, shape, dt))

        def sem(name):
            return ctx.enter_context(nc.semaphore(name))

        x_all = sb("x_all", [P, TILES, D], F32)
        wq = sb("wq", [P, DC, D], F32)
        wk = sb("wk", [P, DC, D], F32)
        wvg = sb("wvg", [P, DC, D + NE], F32)
        bqk = sb("bqk", [P, 2, DC], F32)
        bvg = sb("bvg", [P, D + NE], F32)
        stats = sb("stats", [P, TILES, 6], F32)
        mean = sb("mean", [P, TILES], F32)
        var = sb("var", [P, TILES], F32)
        std = sb("std", [P, TILES], F32)
        rstd = sb("rstd", [P, TILES], F32)
        tmp = sb("tmp", [P, TILES], F32)
        xn = [sb(f"xn{h}", [P, CT, D], F32) for h in range(2)]
        xT = [sb(f"xT{h}", [P, DC, CTOK], F32) for h in range(2)]
        qf = [[sb(f"qf{h}{u}", [P, CTOK], F32) for u in range(4)] for h in range(2)]
        terms = [[sb(f"terms{h}{u}", [P, 3, CTOK], BF16) for u in range(4)] for h in range(2)]
        v_all = sb("v_all", [P, HEADS, TILES, HD], F32)
        rkT = sb("rkT", [HD, RELS], F32)
        rk_terms = sb("rk_terms", [HD, 3, RELS], BF16)
        zeros = sb("zeros", [P, D], F32)

        tp = [ctx.enter_context(nc.psum_tensor(f"tp{i}", [P, 512], F32)) for i in range(2)]
        pq = [ctx.enter_context(nc.psum_tensor(f"pq{i}", [P, 512], F32)) for i in range(2)]
        pv = [ctx.enter_context(nc.psum_tensor(f"pv{i}", [P, 512], F32)) for i in range(2)]

        x_first = sem("x_first")
        x_rest = sem("x_rest")
        w_in = sem("w_in")
        rk_in = sem("rk_in")
        rk_link = sem("rk_link")
        rk_split = sem("rk_split")
        rk_out = sem("rk_out")
        ident_set = sem("ident_set")
        zero_set = sem("zero_set")
        zeros_out = sem("zeros_out")
        stats_done = sem("stats_done")
        var_ready = sem("var_ready")
        std_ready = sem("std_ready")
        norm_link = sem("norm_link")
        xn_ready = sem("xn_ready")
        xn_out = [sem(f"xn_out{h}") for h in range(2)]
        tr_mm = sem("tr_mm")
        xT_evac = sem("xT_evac")
        qk_mm = sem("qk_mm")
        qk_evac = sem("qk_evac")
        rest_ready = sem("rest_ready")
        second_ready = sem("second_ready")
        split_done = sem("split_done")
        stacked = [[sem(f"stacked{of}{h}") for h in range(2)] for of in ("_q", "_k")]
        vg_mm = sem("vg_mm")
        vg_evac = sem("vg_evac")
        v_out = sem("v_out")

        x_v = io["x"].rearrange("b (t p) d -> p (b t) d", p=P)
        xn_v = dram["xn"].rearrange("(t p) d -> p t d", p=P)

        def stacks_out(eng, of, c, half):
            tab, which = ((dram["q_stack"], QTERM), (dram["k_stack"], KTERM))[of]
            for u in (2 * of, 2 * of + 1):
                eng.wait_ge(split_done, c * 4 + u + 1)
                for slot in range(len(which)):
                    dst = tab[HALF * (u % 2):HALF * (u % 2 + 1), slot * HD:(slot + 1) * HD, bass.ds(c * CTOK, CTOK)]
                    eng.dma_start(dst, terms[half][u][:, which[slot], :]).then_inc(stacked[of][half], 16)

        with nc.Block() as block:

            @block.sync
            def _(sp):
                sp.dma_start(x_all[:, 0:QT, :], x_v[:, 0:QT, :]).then_inc(x_first, 16)
                for t, name in ((wq, "wqT"), (wk, "wkT")):
                    sp.dma_start(t[:, :, :], io[name].rearrange("(c p) n -> p c n", p=P)).then_inc(w_in, 16)
                sp.dma_start(wvg[:, :, 0:D], io["wvT"].rearrange("(c p) n -> p c n", p=P)).then_inc(w_in, 16)
                sp.dma_start(wvg[:, :, D:D + NE], io["wg"].rearrange("(c p) n -> p c n", p=P)).then_inc(w_in, 16)
                for k, name in enumerate(("bq", "bk")):
                    sp.dma_start(bqk[:, k, :], io[name]).then_inc(w_in, 16)
                sp.dma_start(bvg[:, 0:D], io["bv"].partition_broadcast(P)).then_inc(w_in, 16)
                sp.dma_start(bvg[:, D:D + NE], io["bg"].partition_broadcast(P)).then_inc(w_in, 16)
                sp.dma_start(x_all[:, QT:TILES, :], x_v[:, QT:TILES, :]).then_inc(x_rest, 16)
                sp.dma_start(rkT[:, :], io["rel_kT"]).then_inc(rk_in, 16)

                def rows_out(c, half):
                    sp.wait_ge(xn_ready, c * CT + CT)
                    sp.dma_start(xn_v[:, bass.ds(c * CT, CT), :], xn[half][:, :, :]).then_inc(xn_out[half], 16)

                rows_out(0, 0)
                rows_out(1, 1)
                stacks_out(sp, 0, 0, 0)
                sp.wait_ge(zero_set, 1)
                sp.dma_start(dram["xs"].rearrange("(t p) d -> p t d", p=P), zeros[:, :].unsqueeze(1).to_broadcast([P, XT, D])).then_inc(zeros_out, 16)
                sp.wait_ge(rk_split, 3)
                for slot in range(len(KTERM)):
                    sp.dma_start(con["rel_k"][slot * HD:(slot + 1) * HD, :], rk_terms[:, KTERM[slot], :]).then_inc(rk_out, 16)
                with sp.Fori(1, PAIRS) as pair_i:
                    c0 = pair_i * 2
                    stacks_out(sp, 0, c0 - 1, 1)
                    rows_out(c0, 0)
                    rows_out(c0 + 1, 1)
                    stacks_out(sp, 0, c0, 0)
                stacks_out(sp, 0, CHUNKS - 1, 1)
                for of in range(2):
                    for h in range(2):
                        sp.wait_ge(stacked[of][h], STACK_COUNT * CHUNKS // 2)
                for h in range(2):
                    sp.wait_ge(xn_out[h], 16 * CHUNKS // 2)
                sp.wait_ge(zeros_out, 16)
                sp.wait_ge(rk_out, 16 * len(KTERM))

            @block.gpsimd
            def _(pool):
                pool.memset(zeros[:, :], 0.0).then_inc(zero_set, 1)
                pool.memset(con["ident"][:, :], 0.0).then_inc(ident_set, 1)
                pool.memset(con["ident_bf"][:, :], 0.0).then_inc(ident_set, 1)
                pool.wait_ge(ident_set, 2)
                for m in (con["ident"], con["ident_bf"]):
                    pool.affine_select(out=m[:, :], in_=m[:, :], compare_op=ALU.not_equal, fill=1.0, base=0,
                                       pattern=[[-1, P]], channel_multiplier=1).then_inc(ident_set, 1)
                v_pairs = dram["v"].rearrange("(h b) p i d -> b p h (i d)", b=B)
                for b in range(B):
                    with pool.Fori(b * (PAIRS // B), (b + 1) * (PAIRS // B)) as pair_i:
                        c0 = pair_i * 2
                        stacks_out(pool, 1, c0, 0)
                        stacks_out(pool, 1, c0 + 1, 1)
                    pool.wait_ge(vg_evac, NB * (b + 1))
                    pool.dma_start(v_pairs[b], v_all[:, :, NB * b:NB * (b + 1), :].rearrange("p h t d -> p h (t d)")).then_inc(v_out, 16)
                pool.wait_ge(v_out, 16 * B)

            @block.vector
            def _(dve):
                v = nc.vector

                def relative_keys():
                    link = chain(dve, rk_link)
                    dve.wait_ge(rk_in, 16)
                    v.tensor_copy(rk_terms[:, 0, :], rkT[:, :]).then_inc(rk_split, 1)
                    dve.wait_ge(rk_split, 1)
                    link(v.tensor_tensor(rkT[:, :], rkT[:, :], rk_terms[:, 0, :], ALU.subtract))
                    v.tensor_copy(rk_terms[:, 1, :], rkT[:, :]).then_inc(rk_split, 1)
                    dve.wait_ge(rk_split, 2)
                    v.tensor_tensor(rk_terms[:, 2, :], rkT[:, :], rk_terms[:, 1, :], ALU.subtract).then_inc(rk_split, 1)

                link = chain(dve, norm_link)

                def variance(tiles):
                    for t in range(tiles.start, tiles.stop):
                        v.bn_stats(stats[:, t, :], x_all[:, t, :]).then_inc(stats_done, 1)
                    mn, vr, tm = mean[:, tiles], var[:, tiles], tmp[:, tiles]
                    dve.wait_ge(stats_done, tiles.stop)
                    v.tensor_tensor(mn, stats[:, tiles, 1], stats[:, tiles, 4], ALU.add)
                    v.tensor_tensor(tm, stats[:, tiles, 1], stats[:, tiles, 4], ALU.subtract)
                    link(v.tensor_tensor(vr, stats[:, tiles, 2], stats[:, tiles, 5], ALU.add))
                    v.tensor_scalar(mn, mn, 0.5, None, ALU.mult)
                    v.tensor_scalar(vr, vr, 1.0 / D, EPS, ALU.mult, ALU.add)
                    link(v.tensor_scalar(tm, tm, 0.5, None, ALU.mult))
                    link(v.tensor_tensor(tm, tm, tm, ALU.mult))
                    v.tensor_tensor(vr, vr, tm, ALU.add).then_inc(var_ready, 1)

                def inverse(part, tiles):
                    vr, rs, tm = var[:, tiles], rstd[:, tiles], tmp[:, tiles]
                    dve.wait_ge(std_ready, part + 1)
                    link(v.reciprocal(rs, std[:, tiles]))
                    link(v.tensor_tensor(tm, rs, rs, ALU.mult))
                    link(v.tensor_tensor(tm, tm, vr, ALU.mult))
                    link(v.tensor_scalar(tm, tm, -0.5, 1.5, ALU.mult, ALU.add))
                    link(v.tensor_tensor(rs, rs, tm, ALU.mult))

                def normalise(c, half, out_count):
                    wait(dve, tr_mm, c * CT - CT)
                    wait(dve, xn_out[half], out_count)
                    for k in range(CT):
                        t = c * CT + k
                        v.tensor_scalar(xn[half][:, k, :], x_all[:, bass.ds(t, 1), :].rearrange("p t d -> p (t d)"), mean[:, bass.ds(t, 1)],
                                        rstd[:, bass.ds(t, 1)], ALU.subtract, ALU.mult).then_inc(xn_ready, 1)

                def first_rests(c, half):
                    for u in range(4):
                        dve.wait_ge(qk_evac, c * 4 + u + 1)
                        v.tensor_tensor(qf[half][u][:, :], qf[half][u][:, :], terms[half][u][:, 0, :], ALU.subtract).then_inc(rest_ready, 1)

                def third_terms(c, half):
                    for u in range(4):
                        dve.wait_ge(second_ready, c * 4 + u + 1)
                        v.tensor_tensor(terms[half][u][:, 2, :], qf[half][u][:, :], terms[half][u][:, 1, :], ALU.subtract).then_inc(split_done, 1)

                def values(c):
                    for k in range(CT):
                        t = c * CT + k
                        dve.wait_ge(vg_mm, t + 1)
                        v.tensor_tensor(v_all[:, :, bass.ds(t, 1), :].rearrange("p h t d -> p h (t d)"),
                                        pv[k % 2][:, 0:D].rearrange("p (h d) -> p h d", h=HEADS),
                                        bvg[:, 0:D].rearrange("p (h d) -> p h d", h=HEADS), ALU.add)
                        v.tensor_tensor(lg_all[:, bass.ds(t, 1), :].rearrange("p t e -> p (t e)"), pv[k % 2][:, D:D + NE],
                                        bvg[:, D:D + NE], ALU.add).then_inc(vg_evac, 1)

                def products(c, half):
                    first_rests(c, half)
                    third_terms(c, half)
                    values(c)

                dve.wait_ge(x_first, 16)
                variance(FIRST)
                inverse(0, FIRST)
                normalise(0, 0, 0)
                normalise(1, 1, 0)
                dve.wait_ge(x_rest, 16)
                variance(REST)
                dve.wait_ge(w_in, 16 * 8)
                products(0, 0)
                inverse(1, REST)
                relative_keys()
                with dve.Fori(1, PAIRS) as pair_i:
                    c0 = pair_i * 2
                    normalise(c0, 0, pair_i * 16)
                    products(c0 - 1, 1)
                    normalise(c0 + 1, 1, pair_i * 16)
                    products(c0, 0)
                products(CHUNKS - 1, 1)

            @block.scalar
            def _(act):
                def root(part, tiles):
                    act.wait_ge(var_ready, part + 1)
                    nc.scalar.activation(std[:, tiles], var[:, tiles], ACT.Sqrt).then_inc(std_ready, 1)

                def turn(c, half):
                    wait(act, vg_mm, c * CT - CT)
                    for k in range(CT):
                        act.wait_ge(tr_mm, c * CT + k + 1)
                        nc.scalar.activation(xT[half][:, :, k * P:(k + 1) * P], tp[k % 2][:, 0:D].rearrange("p (c m) -> p c m", c=DC),
                                             ACT.Copy).then_inc(xT_evac, 1)

                def bias(c, half, stack_count, follow=True):
                    for of in range(2):
                        wait(act, stacked[of][half], stack_count)
                    for u in range(4):
                        act.wait_ge(qk_mm, c * 4 + u + 1)
                        b = bqk[:, u // 2, u % 2:u % 2 + 1]
                        nc.scalar.activation(qf[half][u][:, :], pq[u % 2][:, :], ACT.Identity, bias=b)
                        nc.scalar.activation(terms[half][u][:, 0, :], pq[u % 2][:, :], ACT.Identity, bias=b).then_inc(qk_evac, 1)
                        if u > 0 and follow:
                            second(c, half, u - 1)

                def second(c, half, u):
                    act.wait_ge(rest_ready, c * 4 + u + 1)
                    nc.scalar.activation(terms[half][u][:, 1, :], qf[half][u][:, :], ACT.Copy).then_inc(second_ready, 1)

                root(0, FIRST)
                act.wait_ge(w_in, 16 * 8)
                turn(0, 0)
                turn(1, 1)
                bias(0, 0, 0, follow=False)
                root(1, REST)
                for u in range(4):
                    second(0, 0, u)
                bias(1, 1, 0)
                with act.Fori(1, PAIRS) as pair_i:
                    c0 = pair_i * 2
                    turn(c0, 0)
                    second(c0 - 1, 1, 3)
                    bias(c0, 0, pair_i * STACK_COUNT)
                    turn(c0 + 1, 1)
                    second(c0, 0, 3)
                    bias(c0 + 1, 1, pair_i * STACK_COUNT)
                second(CHUNKS - 1, 1, 3)

            @block.tensor
            def _(pe):
                def turn(c, half):
                    for k in range(CT):
                        pe.wait_ge(xn_ready, c * CT + k + 1)
                        wait(pe, xT_evac, c * CT + k - 1)
                        for d in range(DC):
                            mm = nc.tensor.transpose(tp[k % 2][:, d * P:(d + 1) * P], xn[half][:, k, d * P:(d + 1) * P], con["ident"][:, :])
                        mm.then_inc(tr_mm, 1)

                def queries_keys(c, half):
                    pe.wait_ge(xT_evac, c * CT + CT)
                    for u in range(4):
                        w = wq if u < 2 else wk
                        wait(pe, qk_evac, c * 4 + u - 1)
                        for d in range(DC):
                            mm = nc.tensor.matmul(pq[u % 2][:, :], w[:, d, (u % 2) * P:(u % 2 + 1) * P], xT[half][:, d, :],
                                                  start=(d == 0), stop=(d == DC - 1))
                        mm.then_inc(qk_mm, 1)

                def values(c, half):
                    for k in range(CT):
                        wait(pe, vg_evac, c * CT + k - 1)
                        for d in range(DC):
                            mm = nc.tensor.matmul(pv[k % 2][:, 0:D + NE], xT[half][:, d, k * P:(k + 1) * P], wvg[:, d, :],
                                                  start=(d == 0), stop=(d == DC - 1))
                        mm.then_inc(vg_mm, 1)

                pe.wait_ge(ident_set, 4)
                turn(0, 0)
                turn(1, 1)
                pe.wait_ge(w_in, 16 * 8)
                queries_keys(0, 0)
                values(0, 0)
                with pe.Fori(1, PAIRS) as pair_i:
                    c0 = pair_i * 2
                    queries_keys(c0 - 1, 1)
                    turn(c0, 0)
                    values(c0 - 1, 1)
                    queries_keys(c0, 0)
                    turn(c0 + 1, 1)
                    values(c0, 0)
                queries_keys(CHUNKS - 1, 1)
                values(CHUNKS - 1, 1)


def route(nc, lg_all, pos_i, expert_i):
    with ExitStack() as ctx:
        def sb(name, shape, dt):
            return ctx.enter_context(nc.sbuf_tensor(name, shape, dt))

        def sem(name):
            return ctx.enter_context(nc.semaphore(name))

        iota_i = sb("iota_i", [P, XT], I32)
        iota_f = sb("iota_f", [P, XT], F32)
        iota_e = sb("iota_e", [P, NE], F32)
        iota_c = sb("iota_c", [P, TILES], F32)
        before = sb("before", [P, P], BF16)
        ones = sb("ones", [P, P], BF16)
        top = sb("top", [P, TILES], F32)
        eq = sb("eq", [P, TILES, NE], F32)
        pick = sb("pick", [P, TILES], F32)
        oh = sb("oh", [P, TILES, NE], BF16)
        tot = sb("tot", [P, TILES, NE], F32)
        cum = [sb(f"cum{i}", [P, TILES, NE], F32) for i in range(2)]
        base = sb("base", [P, TILES, NE], F32)
        more = sb("more", [P, NE, TILES], F32)
        nt = sb("nt", [P, NE], F32)
        end = [sb(f"end{i}", [P, NE], F32) for i in range(2)]
        first = sb("first", [P, NE], F32)
        posf = sb("posf", [P, TILES], F32)
        past = sb("past", [P, XT, NE], F32)
        expf = sb("expf", [P, XT], F32)
        pr = ctx.enter_context(nc.psum_tensor("pr", [P, 2, TILES * NE], F32))

        iota_set = sem("iota_set")
        tri_set = sem("tri_set")
        link_sem = sem("route_link")
        oh_ready = sem("oh_ready")
        counts_mm = sem("counts_mm")
        pos_ready = sem("pos_ready")

        with nc.Block() as block:

            @block.gpsimd
            def _(pool):
                pool.iota(iota_i[:, :], pattern=[[1, XT]], base=0, channel_multiplier=0).then_inc(iota_set, 1)
                pool.memset(ones[:, :], 1.0).then_inc(tri_set, 1)
                pool.memset(before[:, :], 1.0).then_inc(tri_set, 1)
                pool.wait_ge(tri_set, 2)
                pool.affine_select(out=before[:, :], in_=before[:, :], compare_op=ALU.is_gt, fill=0.0, base=0,
                                   pattern=[[1, P]], channel_multiplier=-1).then_inc(tri_set, 1)

            @block.tensor
            def _(pe):
                pe.wait_ge(tri_set, 3)
                pe.wait_ge(oh_ready, 1)
                ohv = oh[:, :, :].rearrange("p t e -> p (t e)")
                nc.tensor.matmul(pr[:, 0, :], before[:, :], ohv, start=True, stop=True)
                nc.tensor.matmul(pr[:, 1, :], ones[:, :], ohv, start=True, stop=True).then_inc(counts_mm, 1)

            @block.vector
            def _(dve):
                link = chain(dve, link_sem)
                v = nc.vector

                def over(ap, shape, axis):
                    return ap.unsqueeze(axis).to_broadcast(shape)

                TE = [P, TILES, NE]
                dve.wait_ge(iota_set, 1)
                link(v.tensor_copy(iota_f[:, :], iota_i[:, :]))
                v.tensor_scalar(iota_e[:, :], iota_f[:, 0:NE], -float(NE), None, ALU.add)
                v.tensor_scalar(iota_c[:, :], iota_f[:, 0:TILES], float(P), None, ALU.mult)
                link(v.tensor_reduce(top[:, :], lg_all[:, :, :], AX_X, ALU.max))
                link(v.tensor_tensor(eq[:, :, :], lg_all[:, :, :], over(top[:, :], TE, 2), ALU.is_ge))
                link(v.tensor_tensor(eq[:, :, :], eq[:, :, :], over(iota_e[:, :], TE, 1), ALU.mult))
                link(v.tensor_reduce(pick[:, :], eq[:, :, :], AX_X, ALU.min))
                v.tensor_tensor(oh[:, :, :], over(iota_e[:, :], TE, 1), over(pick[:, :], TE, 2), ALU.is_equal).then_inc(oh_ready, 1)
                dve.wait_ge(counts_mm, 1)
                v.tensor_copy(cum[0][:, :, :], pr[:, 1, :].rearrange("p (t e) -> p t e", e=NE))
                link(v.tensor_copy(tot[:, :, :], pr[:, 1, :].rearrange("p (t e) -> p t e", e=NE)))
                a = 0
                k = 1
                while k < TILES:
                    v.tensor_copy(cum[1 - a][:, 0:k, :], cum[a][:, 0:k, :])
                    link(v.tensor_tensor(cum[1 - a][:, k:, :], cum[a][:, k:, :], cum[a][:, 0:TILES - k, :], ALU.add))
                    a, k = 1 - a, 2 * k
                ET = [P, NE, TILES]
                link(v.tensor_tensor(more[:, :, :], over(cum[a][:, TILES - 1, :], ET, 2), over(iota_c[:, :], ET, 1), ALU.is_gt))
                link(v.tensor_reduce(nt[:, :], more[:, :, :], AX_X, ALU.add))
                link(v.tensor_copy(end[0][:, :], nt[:, :]))
                b, k = 0, 1
                while k < NE:
                    v.tensor_copy(end[1 - b][:, 0:k], end[b][:, 0:k])
                    link(v.tensor_tensor(end[1 - b][:, k:], end[b][:, k:], end[b][:, 0:NE - k], ALU.add))
                    b, k = 1 - b, 2 * k
                link(v.tensor_tensor(first[:, :], end[b][:, :], nt[:, :], ALU.subtract))
                link(v.tensor_scalar(first[:, :], first[:, :], float(P), None, ALU.mult))
                link(v.tensor_tensor(base[:, :, :], cum[a][:, :, :], tot[:, :, :], ALU.subtract))
                link(v.tensor_tensor(base[:, :, :], base[:, :, :], pr[:, 0, :].rearrange("p (t e) -> p t e", e=NE), ALU.add))
                link(v.tensor_tensor(base[:, :, :], base[:, :, :], over(first[:, :], TE, 1), ALU.add))
                link(v.tensor_tensor(base[:, :, :], base[:, :, :], oh[:, :, :], ALU.mult))
                link(v.tensor_reduce(posf[:, :], base[:, :, :], AX_X, ALU.add))
                v.tensor_copy(pos_i[:, :], posf[:, :]).then_inc(pos_ready, 1)
                XE = [P, XT, NE]
                link(v.tensor_tensor(past[:, :, :], over(iota_f[:, :], XE, 2), over(end[b][:, :], XE, 1), ALU.is_ge))
                link(v.tensor_reduce(expf[:, :], past[:, :, :], AX_X, ALU.add))
                link(v.tensor_scalar(expf[:, :], expf[:, :], float(NE - 1), None, ALU.min))
                v.tensor_copy(expert_i[:, :], expf[:, :]).then_inc(pos_ready, 1)


def attend(nc, io, dram, con, pos_i, attn):
    with ExitStack() as ctx:
        def sb(name, shape, dt):
            return ctx.enter_context(nc.sbuf_tensor(name, shape, dt))

        def sem(name):
            return ctx.enter_context(nc.semaphore(name))

        def two(name, shape, dt):
            return [sb(f"{name}{i}", shape, dt) for i in range(2)]

        q_front = two("q_front", [ROWS, S], BF16)
        k_front = two("k_front", [ROWS, S], BF16)
        q_back = two("q_back", [ALLROWS, S], BF16)
        k_left = two("k_left", [ALLROWS, S], BF16)
        k_right = two("k_right", [ALLROWS, S], BF16)
        rel = two("rel", [P, CH, WIN], F32)
        band = two("band", [P, NB, BAND], F32)
        pwin = two("pwin", [P, CH, NEARW], F32)
        band_T = two("band_T", [P, CH, BAND], F32)
        pwin_T = two("pwin_T", [P, CH, NEARW], F32)
        clip_T = sb("clip_T", [P, CH, 2, P], F32)
        clip_mask = sb("clip_mask", [P, 2, P], F32)
        far_T = two("far_T", [P, CH, CW], F32)
        v_raw = sb("v_raw", [P, NB, HD], F32)
        v_far = [two(f"v_far{k}", [P, NB, 32], F32) for k in range(2)]
        v_near = two("v_near", [P, NB, 32], F32)
        rv_ends = sb("rv_ends", [P, 2, HD], F32)
        rv_win = sb("rv_win", [P, CH, 32], F32)
        part = two("part", [P, NB, 3, CH], F32)
        lm = sb("lm", [P, CH, 3], F32)
        rmax = two("rmax", [P, NB], F32)
        negm = two("negm", [P, NB], F32)
        rel_ends = two("rel_ends", [P, NB, 3], F32)
        sh = sb("sh", [P, CH, 2], F32)
        shb = two("shb", [P, CH, SHIFTS], BF16)
        outT = sb("outT", [P, CW], F32)
        rden = sb("rden", [P, NB], F32)
        zero = sb("zero", [P, CH, 2], F32)
        neg_scale = sb("neg_scale", [P, 1], F32)
        row = two("row", [P, D], F32)

        ps1 = [ctx.enter_context(nc.psum_tensor(f"ps1_{i}", [P, 512], F32)) for i in range(2)]
        pst = [ctx.enter_context(nc.psum_tensor(f"pst{i}", [P, 512], F32)) for i in range(2)]
        pout = ctx.enter_context(nc.psum_tensor("pout", [P, 512], F32))
        prel = ctx.enter_context(nc.psum_tensor("prel", [P, 512], F32))
        pband = ctx.enter_context(nc.psum_tensor("pband", [P, 512], F32))
        psmall = ctx.enter_context(nc.psum_tensor("psmall", [P, 512], F32))
        pnear = psmall[:, 0:NEARW]
        prow = psmall[0:SHIFTS, NEARW:512].bitcast(BF16)

        const_in = sem("const_in")
        const_set = sem("const_set")
        shift_set = sem("shift_set")
        qf_in = [sem(f"qf_in{i}") for i in range(2)]
        kf_in = [sem(f"kf_in{i}") for i in range(2)]
        back_in = [sem(f"back_in{i}") for i in range(2)]
        v_in = sem("v_in")
        v_built = sem("v_built")
        s1_mm = sem("s1_mm")
        s1_used = sem("s1_used")
        r_mm = sem("r_mm")
        r_evac = sem("r_evac")
        ends_done = sem("ends_done")
        sides_done = sem("sides_done")
        rel_out = [sem(f"rel_out{r}") for r in range(4)]
        rel_in = [[sem(f"rel_in{p}{r}") for r in range(4)] for p in range(2)]
        max_link = sem("max_link")
        rmax_ready = sem("rmax_ready")
        negm_ready = sem("negm_ready")
        shift_link = sem("shift_link")
        shift_ready = sem("shift_ready")
        rows_tp = sem("rows_tp")
        rows_copied = sem("rows_copied")
        band_exp = sem("band_exp")
        prob_out = [sem(f"prob_out{r}") for r in range(4)]
        win_in = [sem(f"win_in{i}") for i in range(2)]
        st_mm = sem("st_mm")
        exp_done = sem("exp_done")
        pv_done = sem("pv_done")
        bandT_mm = sem("bandT_mm")
        bandT_evac = sem("bandT_evac")
        winT_mm = sem("winT_mm")
        winT_evac = sem("winT_evac")
        clip_ready = sem("clip_ready")
        clip_used = sem("clip_used")
        band_pv = sem("band_pv")
        out_evac = sem("out_evac")
        back_mm = sem("back_mm")
        den_ready = sem("den_ready")
        norm_done = sem("norm_done")
        row_in = [sem(f"row_in{i}") for i in range(2)]
        sorted_out = [sem(f"sorted_out{i}") for i in range(2)]

        class Step:

            def __init__(self, hb, off):
                self.dn, self.s = divmod(off, NB)
                self.hb = hb
                self.par = self.dn % 2
                self.head = hb + self.dn // 2
                self.n = hb * 2 + self.dn
                self.r, self.g = divmod(self.s, CH)
                self.valid = not isinstance(hb, int) or 0 <= self.n < NBH

            def count(self, per, more):
                return self.sum(2 * per, self.dn * per + more)

            def count2(self, per, more):
                return self.sum(per, self.dn // 2 * per + more)

            def sum(self, per, more):
                return self.hb * per + more if more else (self.hb - 1) * per + per

        def at_start(hb):
            return isinstance(hb, int) and hb == 0

        def at_end(hb):
            return isinstance(hb, int) and hb == HEADS - 1

        def loop(eng, step):
            for off in range(-NB, 2 * NB):
                step(0, off)
            with eng.Fori(1, HEADS - 1) as hb:
                for off in range(2 * NB):
                    step(hb, off)
            for off in range(2 * NB + LAG_O):
                step(HEADS - 1, off)

        def far_pieces(j, g):
            blocks = range(CH * g, CH * g + CH)
            out = []
            for right, sel in ((1, [i for i in blocks if i <= j - 2]), (0, [i for i in blocks if i >= j + 2])):
                if sel:
                    out.append((right, (sel[0] - CH * g) * P, (sel[-1] + 1 - CH * g) * P))
            return out

        with nc.Block() as block:

            @block.sync
            def _(sp):
                def step(hb, off):
                    if at_start(hb) and off == 1 - NB:
                        sp.dma_start(rv_ends[:, 0, :], io["rel_v"][0, :].partition_broadcast(P)).then_inc(const_in, 16)
                        sp.dma_start(rv_ends[:, 1, :], io["rel_v"][2 * M, :].partition_broadcast(P)).then_inc(const_in, 16)
                        sp.wait_ge(const_set, 1)
                        sp.dma_start(rv_win[:, 0, 0:HD], io["rel_v"][0, :].partition_broadcast(P)).then_inc(const_in, 16)
                        sp.dma_start(rv_win[:, 1, 0:HD], io["rel_v"][0:M, :]).then_inc(const_in, 16)
                        sp.dma_start(rv_win[:, 2, 0:HD], io["rel_v"][M:2 * M, :]).then_inc(const_in, 16)
                        sp.dma_start(rv_win[:, 3, 0:HD], io["rel_v"][2 * M, :].partition_broadcast(P)).then_inc(const_in, 16)
                        sp.wait_ge(const_set, 22)
                    if off % NB == 0:
                        x = Step(hb, off + NB)
                        if x.valid:
                            wait(sp, s1_mm, x.count(64, -64))
                            sp.dma_start(q_front[x.par][:, :], pair_rows(q_tab, x)).then_inc(qf_in[x.par], 16)
                            sp.dma_start(k_front[x.par][:, :], pair_rows(k_tab, x)).then_inc(kf_in[x.par], 16)
                    if off % NB == 2:
                        x = Step(hb, off)
                        if x.valid:
                            wait(sp, st_mm, x.count(64, -64))
                            sp.dma_start(q_back[x.par][0:ROWS, :], pair_rows(q_tab, x)).then_inc(back_in[x.par], 16)
                            sp.dma_start(k_left[x.par][0:ROWS, :], pair_rows(k_tab, x)).then_inc(back_in[x.par], 16)
                            sp.dma_start(k_right[x.par][0:ROWS, :], pair_rows(k_tab, x)).then_inc(back_in[x.par], 16)
                            wait(sp, v_built, x.count(1, 0))
                            sp.dma_start(v_raw[:, :, :], v_tab[x.n]).then_inc(v_in, 16)
                    if at_end(hb) and off < TILES:
                        wait(sp, sorted_out[off % 2], 16 * (off // 2))
                        sp.dma_start(row[off % 2][:, :], dram["xn"][off * P:(off + 1) * P, :]).then_inc(row_in[off % 2], 16)
                    if off % CH != 1:
                        return
                    y = Step(hb, off - 9)
                    if y.valid:
                        sp.wait_ge(band_exp, y.count(16, 4 * y.r + 4))
                        wait(sp, win_in[y.r % 2], y.count(32, 16 * (y.r // 2 + 1) - 32))
                        sp.dma_start(dram["band_p"][y.par, 4 * y.r:4 * y.r + 4].rearrange("s p w -> p s w"),
                                     band[y.par][:, 4 * y.r:4 * y.r + 4, :]).then_inc(prob_out[y.r], 16)
                    x = Step(hb, off + LAG_R - 7)
                    r = x.r
                    if x.valid:
                        sp.wait_ge(rel_out[r], x.count(16, 16))
                        wait(sp, bandT_mm, x.count(16, 4 * r + 4 - 32))
                        wait(sp, prob_out[r], x.count(16, -16))
                        s0, s1 = 4 * r + (r == 0), 4 * r + 4 - (r == 3)
                        sp.dma_start(band[x.par][:, s0:s1, :], sheared(dram["rel"], x.par, s0, s1 - s0, WIN, WIN - 1, P, BAND)).then_inc(rel_in[x.par][r], 16)
                        if r == 0:
                            sp.dma_start(band[x.par][:, 0, P:BAND], sheared(dram["rel"], x.par, 0, 1, WIN, WIN - 1, 2 * P, BAND - P)[:, 0, :]).then_inc(rel_in[x.par][r], 16)
                        if r == 3:
                            sp.dma_start(band[x.par][:, NB - 1, 0:BAND - P], sheared(dram["rel"], x.par, NB - 1, 1, WIN, WIN - 1, P, BAND - P)[:, 0, :]).then_inc(rel_in[x.par][r], 16)
                    z = Step(hb, off - 13)
                    if z.valid:
                        sp.wait_ge(prob_out[z.r], z.count(16, 16))
                        wait(sp, winT_mm, z.count(16, 4 * z.r + 4 - 8))
                        sp.dma_start(pwin[z.r % 2][:, :, :], sheared(dram["band_p"], z.par, 4 * z.r, 4, BAND, BAND + 1, 0, NEARW)).then_inc(win_in[z.r % 2], 16)
                    x = Step(hb, off + LAG_R - 3)
                    r = x.r
                    if x.valid:
                        sp.wait_ge(sides_done, x.count(4, r + 1))
                        wait(sp, rel_in[x.par][r], x.count2(32 if r in (0, 3) else 16, 0))
                        sp.dma_start(dram["rel"][x.par, 4 * r:4 * r + 4].rearrange("s p w -> p s w"), rel[r % 2][:, :, :]).then_inc(rel_out[r], 16)

                q_tab, k_tab, v_tab = dram["q_stack"], dram["k_stack"], dram["v"]

                def pair_rows(t, x):
                    return t[x.head, :, x.par * S:(x.par + 1) * S]

                def sheared(t, par, s, count, width, step_p, first, length):
                    return bass.AP(tensor=t.tensor, offset=t.offset + (par * NB + s) * P * width + first,
                                   ap=[[step_p, P], [P * width, count], [1, length]])

                loop(sp, step)

            @block.gpsimd
            def _(pool):
                pool.memset(rv_win[:, :, :], 0.0).then_inc(const_set, 1)
                pool.memset(zero[:, :, :], 0.0).then_inc(const_set, 1)
                for p in range(2):
                    pool.memset(rel_ends[p][:, :, :], 0.0).then_inc(const_set, 1)
                    pool.memset(rel[p][:, :, 0:1], 0.0).then_inc(const_set, 1)
                    pool.memset(part[p][:, :, :, :], LOWEST).then_inc(const_set, 1)
                    pool.memset(band[p][:, 0, 0:P], 0.0).then_inc(const_set, 1)
                    pool.memset(band[p][:, NB - 1, BAND - P:BAND], 0.0).then_inc(const_set, 1)
                    for v in (v_far[0][p], v_far[1][p], v_near[p]):
                        pool.memset(v[:, :, HD:HD + 1], 1.0)
                        pool.memset(v[:, :, HD + 1:32], 0.0).then_inc(const_set, 1)
                pool.memset(clip_mask[:, :, :], 1.0).then_inc(const_set, 1)
                pool.memset(neg_scale[:, :], -SCALE).then_inc(const_set, 1)
                pool.wait_ge(const_set, 20)
                pool.affine_select(out=clip_mask[:, 0, :], in_=clip_mask[:, 0, :], compare_op=ALU.is_gt, fill=0.0, base=0,
                                   pattern=[[1, P]], channel_multiplier=-1).then_inc(const_set, 1)
                pool.affine_select(out=clip_mask[:, 1, :], in_=clip_mask[:, 1, :], compare_op=ALU.is_ge, fill=0.0, base=0,
                                   pattern=[[-1, P]], channel_multiplier=1).then_inc(const_set, 1)
                pool.wait_ge(const_set, 22)
                pool.wait_ge(const_in, 16 * 6)

                zero_sides = zero[:, :, :].unsqueeze(3).to_broadcast([P, CH, 2, M - 1])

                def copied(dst, src):
                    return nc.gpsimd.tensor_tensor(dst, src, zero[:, :, :], ALU.add)

                def step(hb, off):
                    w = Step(hb, off - LAG_T - 1)
                    if w.valid:
                        bi = order(w.s)
                        k0, k1 = int(bi == 0), 2 - int(bi == NB - 1)
                        pool.wait_ge(bandT_evac, w.count(16, w.s + 1))
                        if w.g == 0:
                            wait(pool, clip_used, w.count(4, w.r))
                        nc.gpsimd.tensor_tensor(clip_T[:, w.g, k0:k1, :],
                                                band_T[w.r % 2][:, w.g, :].rearrange("p (b c) -> p b c", b=3)[:, 2 * k0:2 * k1 - 1:2, :],
                                                clip_mask[:, k0:k1, :], ALU.mult).then_inc(clip_ready, 1)
                    y = Step(hb, off - 4)
                    if off % CH == 0 and y.valid:
                        g = y.count(4, y.r)
                        k = y.count(20, 5 * y.r)
                        four = slice(4 * y.r, 4 * y.r + 4)
                        t = shb[y.r % 2][:, :, :].rearrange("p g (k t) -> p g k t", k=2)
                        pool.wait_ge(rmax_ready, g + 1)
                        wait(pool, band_exp, y.count(16, 4 * y.r + 4 - 32))
                        nc.gpsimd.tensor_tensor(negm[y.par][:, four], rmax[y.par][:, four], neg_scale[:, 0:1].to_broadcast([P, CH]),
                                                ALU.mult).then_inc(negm_ready, 1)
                        wait(pool, rows_tp, y.count(4, y.r - 1))
                        nc.gpsimd.tensor_tensor(sh[:, :, :], rel_ends[y.par][:, four, 0:2],
                                                rmax[y.par][:, four].unsqueeze(2).to_broadcast([P, CH, 2]), ALU.subtract).then_inc(shift_link, 1)
                        pool.wait_ge(shift_link, k + 1)
                        copied(t[:, :, :, 0], sh[:, :, :]).then_inc(shift_link, 1)
                        pool.wait_ge(shift_link, k + 2)
                        nc.gpsimd.tensor_tensor(sh[:, :, :], sh[:, :, :], t[:, :, :, 0], ALU.subtract).then_inc(shift_link, 1)
                        pool.wait_ge(shift_link, k + 3)
                        copied(t[:, :, :, 1], sh[:, :, :]).then_inc(shift_link, 1)
                        pool.wait_ge(shift_link, k + 4)
                        nc.gpsimd.tensor_tensor(sh[:, :, :], sh[:, :, :], t[:, :, :, 1], ALU.subtract).then_inc(shift_link, 1)
                        pool.wait_ge(shift_link, k + 5)
                        copied(t[:, :, :, 2], sh[:, :, :]).then_inc(shift_ready, 1)
                    x = Step(hb, off + LAG_R - 3)
                    if off % CH == 1 and x.valid:
                        pool.wait_ge(r_evac, x.count(16, 4 * x.r + 4))
                        ends = rel[x.r % 2][:, :, M:M + RELS:RELS - 1]
                        copied(rel_ends[x.par][:, 4 * x.r:4 * x.r + 4, 0:2], ends).then_inc(ends_done, 1)
                        sides = rel[x.r % 2][:, :, :].rearrange("p g (b w) -> p g b w", w=M)[:, :, 0:4:3, 1:M]
                        nc.gpsimd.tensor_tensor(sides, ends.unsqueeze(3).to_broadcast([P, CH, 2, M - 1]), zero_sides, ALU.add).then_inc(sides_done, 1)
                    z = Step(hb, off)
                    if off % NB == 7 and z.valid:
                        pool.wait_ge(v_in, z.count(16, 16))
                        wait(pool, band_pv, z.count(4, -4))
                        for k in range(2):
                            nc.gpsimd.tensor_tensor(v_far[k][z.par][:, :, 0:HD], v_raw[:, :, :],
                                                    rv_ends[:, k, :].unsqueeze(1).to_broadcast([P, NB, HD]), ALU.add)
                        nc.gpsimd.tensor_copy(v_near[z.par][:, :, 0:HD], v_raw[:, :, :]).then_inc(v_built, 1)

                    tok = off - 1
                    if at_end(hb) and 0 <= tok < TILES:
                        pool.wait_ge(row_in[tok % 2], 16 * (tok // 2 + 1))
                        pool.indirect_dma_start(out=dram["xs"][:, :], out_offset=bass.IndirectOffsetOnAxis(ap=pos_i[:, tok:tok + 1], axis=0),
                                                in_=row[tok % 2][:, :], in_offset=None).then_inc(sorted_out[tok % 2], 16)

                loop(pool, step)
                for h in range(2):
                    pool.wait_ge(sorted_out[h], 16 * TILES // 2)

            @block.tensor
            def _(pe):
                def step(hb, off):
                    a = Step(hb, off)
                    t = Step(hb, off - LAG_T)
                    x = Step(hb, off + LAG_R)
                    w = Step(hb, off - LAG_T - 1)
                    y = Step(hb, off - 5)
                    o = Step(hb, off - LAG_O)
                    i = order(a.s)

                    def shift_rows():
                        pe.wait_ge(shift_ready, y.count(4, y.r + 1))
                        wait(pe, rows_copied, y.count(4, y.r))
                        if w.valid:
                            wait(pe, winT_evac, w.count(16, w.s + 1))
                        for g in range(CH):
                            mm = nc.tensor.transpose(prow[0:SHIFTS, g * P:(g + 1) * P], shb[y.r % 2][:, g, :], con["ident_bf"][:, :])
                        mm.then_inc(rows_tp, 1)

                    def turn_back():
                        pe.wait_ge(out_evac, o.count(1, 1))
                        wait(pe, r_evac, x.count(16, x.s + 1) if x.valid else NBH * 16)
                        for r in range(CH):
                            mm = nc.tensor.transpose(prel[:, r * P:(r + 1) * P], outT[:, r * P:(r + 1) * P], con["ident"][:, :])
                        mm.then_inc(back_mm, 1)

                    def weighted(r, g, values, probs, last=False):
                        return nc.tensor.matmul(pout[32 * g:32 * g + 32, r * P:(r + 1) * P], values, probs, start=False, stop=last,
                                                skip_group_check=True)

                    def clipped_values(r):
                        pe.wait_ge(clip_ready, w.count(16, 4 * r + 4))
                        for k in range(2):
                            for g in range(CH):
                                if 0 <= CH * g + r + 2 * k - 1 < NB:
                                    mm = weighted(r, g, rv_win[:, 3 * k, :], clip_T[:, g, k, :])
                        mm.then_inc(clip_used, 1)

                    def band_values(r, parts):
                        for b in parts:
                            for g in range(CH):
                                j = CH * g + r + b - 1
                                if 0 <= j < NB:
                                    weighted(r, g, v_near[w.par][:, j, :], band_T[r % 2][:, g, b * P:(b + 1) * P])

                    def near_values(r):
                        pe.wait_ge(winT_evac, w.count(16, 4 * r + 4))
                        for b in range(2):
                            for g in range(CH):
                                mm = weighted(r, g, rv_win[:, 1 + b, :], pwin_T[r % 2][:, g, b * P:(b + 1) * P], last=(r == CH - 1 and b == 1))
                        mm.then_inc(band_pv, 1)

                    def far_values():
                        if w.s == 0:
                            pe.wait_ge(v_built, w.count(1, 1))
                            wait(pe, out_evac, w.count(1, 0))
                        pe.wait_ge(exp_done, w.count(64, 4 * w.s + 4))
                        for nth in range(2):
                            for g in range(CH):
                                pieces = far_pieces(w.s, g)
                                if nth < len(pieces):
                                    right, c0, c1 = pieces[nth]
                                    mm = nc.tensor.matmul(pout[32 * g:32 * g + 32, c0:c1], v_far[right][w.par][:, w.s, :], far_T[w.s % 2][:, g, c0:c1],
                                                          start=(w.s == 0 and nth == 0), stop=False, skip_group_check=True)
                        mm.then_inc(pv_done, 1)

                    if t.valid and t.s == 0:
                        if at_start(hb) and t.n == 0:
                            pe.wait_ge(shift_set, 8)
                            pe.wait_ge(const_set, 22)
                            pe.wait_ge(const_in, 16 * 6)
                        pe.wait_ge(back_in[t.par], t.count2(48, 48))
                        pe.wait_ge(rows_copied, t.count(4, 4))
                    for u in range(CH):
                        if a.valid:
                            if a.s == 0 and u == 0:
                                pe.wait_ge(qf_in[a.par], a.count2(16, 16))
                                pe.wait_ge(kf_in[a.par], a.count2(16, 16))
                            wait(pe, s1_used, a.count(64, 4 * a.s + u - 1))
                            nc.tensor.matmul(ps1[u % 2][:, :], q_front[a.par][:, i * P:(i + 1) * P], k_front[a.par][:, u * CW:(u + 1) * CW],
                                             start=True, stop=True).then_inc(s1_mm, 1)
                        if t.valid:
                            wait(pe, exp_done, t.count(64, 4 * t.s + u - 1))
                            for right, c0, c1 in far_pieces(t.s, u):
                                k = (k_right if right else k_left)[t.par]
                                mm = nc.tensor.matmul(pst[u % 2][:, c0:c1], k[:, t.s * P:(t.s + 1) * P], q_back[t.par][:, u * CW + c0:u * CW + c1],
                                                      start=True, stop=True)
                            mm.then_inc(st_mm, 1)
                        if u == 1 and w.valid:
                            far_values()
                        if u == 1 and x.valid:
                            if x.s == 0:
                                pe.wait_ge(qf_in[x.par], x.count2(16, 16))
                            wait(pe, r_evac, x.count(16, x.s))
                            if t.s == LAG_O - LAG_T:
                                wait(pe, norm_done, t.count(1, 0))
                            xi = order(x.s)
                            nc.tensor.matmul(prel[:, 0:RELS], q_front[x.par][:, xi * P:(xi + 1) * P], con["rel_k"][:, :], start=True, stop=True).then_inc(r_mm, 1)
                        if u == 1 and off % CH == 1 and y.valid:
                            shift_rows()
                        if u == 2 and o.s == NB - 1 and o.valid:
                            turn_back()
                    if t.valid:
                        bi = order(t.s)
                        pe.wait_ge(band_exp, t.count(16, t.s + 1))
                        wait(pe, bandT_evac, t.count(16, t.s))
                        for j in band_blocks(bi):
                            b = j - bi + 1
                            mm = nc.tensor.transpose(pband[:, b * P:(b + 1) * P], band[t.par][:, t.s, b * P:(b + 1) * P], con["ident"][:, :])
                        mm.then_inc(bandT_mm, 1)
                        if t.g == 0:
                            pe.wait_ge(win_in[t.r % 2], t.count(32, 16 * (t.r // 2 + 1)))
                        wait(pe, winT_evac, t.count(16, t.s))
                        if off % CH == 1 and y.valid:
                            pe.wait_ge(rows_copied, y.count(4, y.r + 1))
                        for b in range(2):
                            mm = nc.tensor.transpose(pnear[:, b * P:(b + 1) * P], pwin[t.r % 2][:, t.g, b * P:(b + 1) * P], con["ident"][:, :])
                        mm.then_inc(winT_mm, 1)
                    if w.valid:
                        if w.g == CH - 1:
                            clipped_values(w.r)
                            if w.r == CH - 1:
                                band_values(w.r, (0, 1, 2))
                                near_values(w.r)
                        elif w.r > 0:
                            if w.g < 2:
                                band_values(w.r - 1, ((0, 1), (2,))[w.g])
                            else:
                                near_values(w.r - 1)

                loop(pe, step)

            @block.vector
            def _(dve):
                for p in range(2):
                    nc.vector.memset(k_left[p][ROWS:ALLROWS, :], 0.0).then_inc(shift_set, 1)
                    nc.vector.memset(k_right[p][ROWS:ALLROWS, :], 1.0).then_inc(shift_set, 1)
                dve.wait_ge(shift_set, 4)
                for p in range(2):
                    nc.vector.memset(k_left[p][ROWS:ROWS + 3, :], 1.0).then_inc(shift_set, 1)
                    nc.vector.memset(k_right[p][ROWS:ROWS + 3, :], 0.0).then_inc(shift_set, 1)
                dve.wait_ge(const_set, 22)

                def step(hb, off):
                    a = Step(hb, off)
                    i = order(a.s)
                    w = Step(hb, off - LAG_T - 1)
                    last = Step(hb, off - 1)
                    four = slice(4 * last.r, 4 * last.r + 4)
                    links = last.count(8, 2 * last.r)

                    def piece_maxima():
                        dve.wait_ge(s1_used, last.count(64, 16 * last.r + 16))
                        nc.vector.tensor_reduce(lm[:, :, :], part[last.par][:, four, :, :], AX_X, ALU.max).then_inc(max_link, 1)

                    def add_relative():
                        dve.wait_ge(max_link, links + 1)
                        dve.wait_ge(ends_done, last.count(4, last.r + 1))
                        nc.vector.tensor_tensor(lm[:, :, :], lm[:, :, :], rel_ends[last.par][:, four, :], ALU.add).then_inc(max_link, 1)

                    def row_maxima():
                        dve.wait_ge(max_link, links + 2)
                        wait(dve, shift_ready, last.count(4, last.r + 1 - 8))
                        nc.vector.tensor_reduce(rmax[last.par][:, four], lm[:, :, :], AX_X, ALU.max).then_inc(rmax_ready, 1)

                    maxima = (piece_maxima, add_relative, row_maxima)

                    def near():
                        dve.wait_ge(winT_mm, w.count(16, w.s + 1))
                        if w.g == 0:
                            wait(dve, band_pv, w.count(4, w.r - 1))
                        nc.vector.tensor_copy(pwin_T[w.r % 2][:, w.g, :], pnear[:, :]).then_inc(winT_evac, 1)

                    for u in range(CH):
                        if a.valid and a.g == 0 and u == 0:
                            dve.wait_ge(rel_in[a.par][a.r], a.count2(32 if a.r in (0, 3) else 16, 32 if a.r in (0, 3) else 16))
                        if a.valid:
                            dve.wait_ge(s1_mm, a.count(64, 4 * a.s + u + 1))
                            blocks = range(CH * u, CH * u + CH)
                            pieces = [(0, [j for j in blocks if j <= i - 2]), (1, [j for j in blocks if j >= i + 2]),
                                      (2, [j for j in blocks if abs(j - i) <= 1])]
                            pieces = [(kind, sel) for kind, sel in pieces if sel]
                            for kind, sel in pieces:
                                src = ps1[u % 2][:, (sel[0] - CH * u) * P:(sel[-1] + 1 - CH * u) * P]
                                peak = part[a.par][:, a.s, kind, u:u + 1]
                                if kind == 2:
                                    b = sel[0] - i + 1
                                    dst = band[a.par][:, a.s, b * P:(b + len(sel)) * P]
                                    ins = nc.vector.tensor_tensor_reduce(dst, src, dst, 1.0, LOWEST, ALU.add, ALU.max, peak)
                                else:
                                    ins = nc.vector.tensor_reduce(peak, src, AX_X, ALU.max)
                            ins.then_inc(s1_used, 1)
                        if u == 0 and w.valid:
                            near()
                        if last.valid and last.g == CH - 1 and u < 3:
                            maxima[u]()
                    o = Step(hb, off - LAG_O)
                    if o.s == NB - 1 and o.valid:
                        back = prel[:, :].rearrange("p (r g d) -> p r g d", r=CH, g=CH)
                        rv = rden[:, :].rearrange("p (r g) -> p r g", r=CH)
                        dve.wait_ge(back_mm, o.count(1, 1))
                        nc.vector.reciprocal(rv, back[:, :, :, HD]).then_inc(den_ready, 1)
                        dve.wait_ge(den_ready, o.count(1, 1))
                        dst = attn[:, o.n, :, :].rearrange("p (g r) d -> p r g d", g=CH)
                        nc.vector.tensor_tensor(dst, back[:, :, :, 0:HD], rv.unsqueeze(3).to_broadcast([P, CH, CH, HD]), ALU.mult).then_inc(norm_done, 1)

                loop(dve, step)

            @block.scalar
            def _(act):
                def step(hb, off):
                    e = Step(hb, off - LAG_T - 1 - NB)
                    x = Step(hb, off + LAG_R)
                    t = Step(hb, off - LAG_T)
                    y = Step(hb, off - 5)
                    w = Step(hb, off - LAG_T - 1)

                    def finished():
                        act.wait_ge(band_pv, e.count(4, 4))
                        nc.scalar.activation(outT[:, :], pout[:, :], ACT.Copy).then_inc(out_evac, 1)

                    def turned():
                        bl = band_blocks(order(w.s))
                        c0, c1 = (bl[0] - order(w.s) + 1) * P, (bl[-1] - order(w.s) + 2) * P
                        act.wait_ge(bandT_mm, w.count(16, w.s + 1))
                        if w.g == 0:
                            wait(act, band_pv, w.count(4, w.r - 1))
                        nc.scalar.activation(band_T[w.r % 2][:, w.g, c0:c1], pband[:, c0:c1], ACT.Copy).then_inc(bandT_evac, 1)

                    def relative():
                        act.wait_ge(r_mm, x.count(16, x.s + 1))
                        if x.g == 0:
                            before = Step(hb, off + LAG_R - 8)
                            wait(act, rel_out[before.r], before.count(16, 16) if before.valid else 0)
                            wait(act, ends_done, x.count(4, x.r - 1))
                        nc.scalar.activation(rel[x.r % 2][:, x.g, M:M + RELS], prel[:, 0:RELS], ACT.Copy).then_inc(r_evac, 1)

                    def shift_rows():
                        act.wait_ge(rows_tp, y.count(4, y.r + 1))
                        rows = q_back[y.par][ROWS:ALLROWS, :].rearrange("k (g r c) -> k g r c", g=CH, r=CH)[:, :, y.r, :]
                        nc.scalar.activation(rows, prow.rearrange("k (g c) -> k g c", g=CH), ACT.Copy).then_inc(rows_copied, 1)

                    if e.s == 0 and e.valid:
                        finished()
                    if t.valid:
                        wait(act, pv_done, t.count(16, t.s - 1))
                    for u in range(CH):
                        if t.valid:
                            act.wait_ge(st_mm, t.count(64, 4 * t.s + u + 1))
                            for _, c0, c1 in far_pieces(t.s, u):
                                ins = nc.scalar.activation(far_T[t.s % 2][:, u, c0:c1], pst[u % 2][:, c0:c1], ACT.Exp, scale=SCALE)
                            ins.then_inc(exp_done, 1)
                        if u == 1 and w.valid:
                            turned()
                        if u == 1 and x.valid:
                            relative()
                        if u == 1 and off % CH == 1 and y.valid:
                            shift_rows()
                    if y.valid:
                        bl = band_blocks(order(y.s))
                        c0, c1 = (bl[0] - order(y.s) + 1) * P, (bl[-1] - order(y.s) + 2) * P
                        if y.g == 0:
                            act.wait_ge(negm_ready, y.count(4, y.r + 1))
                        nc.scalar.activation(band[y.par][:, y.s, c0:c1], band[y.par][:, y.s, c0:c1], ACT.Exp,
                                             bias=negm[y.par][:, y.s:y.s + 1], scale=SCALE).then_inc(band_exp, 1)

                loop(act, step)


def experts(nc, io, dram, con, attn, expert_i):
    with ExitStack() as ctx:
        def sb(name, shape, dt):
            return ctx.enter_context(nc.sbuf_tensor(name, shape, dt))

        def sem(name):
            return ctx.enter_context(nc.semaphore(name))

        def two(name, shape, dt):
            return [sb(f"{name}{i}", shape, dt) for i in range(2)]

        w1 = sb("w1", [P, NE, DC, FF], F32)
        w2 = sb("w2", [P, NE, FC, D], F32)
        wo = sb("wo", [P, DC, D], F32)
        bo = sb("bo", [P, D], F32)
        at = two("at", [P, D], F32)
        aT = two("aT", [P, DC, P], F32)
        xs = two("xs", [P, D], F32)
        xsT = two("xsT", [P, DC, P], F32)
        hid = two("hid", [P, FF], F32)
        hT = two("hT", [P, FC, P], F32)
        ys = two("ys", [P, D], F32)
        px = ctx.enter_context(nc.psum_tensor("px", [P, 512], F32))
        ph = [ctx.enter_context(nc.psum_tensor(f"ph{i}", [P, 512], F32)) for i in range(2)]
        pt = [ctx.enter_context(nc.psum_tensor(f"pt{i}", [P, 512], F32)) for i in range(2)]
        py = ctx.enter_context(nc.psum_tensor("py", [P, 512], F32))
        pa, po = pt, ph
        LAST = XT - 1

        wo_in = sem("wo_in")
        at_ready = sem("at_ready")
        a_tp = sem("a_tp")
        a_evac = sem("a_evac")
        o_mm = sem("o_mm")
        o_evac = sem("o_evac")
        w1_in = sem("w1_in")
        w2_in = sem("w2_in")
        xs_in = [sem(f"xs_in{i}") for i in range(2)]
        x_tp = sem("x_tp")
        x_evac = sem("x_evac")
        h_mm = sem("h_mm")
        gelu_done = sem("gelu_done")
        h_tp = sem("h_tp")
        hT_evac = sem("hT_evac")
        y_mm = sem("y_mm")
        y_evac = sem("y_evac")
        y_out = [sem(f"y_out{i}") for i in range(2)]

        def token_tile(t):
            return attn[:, :, :, :].rearrange("p (h b) i d -> p h (b i) d", b=B)[:, :, bass.ds(t, 1), :].rearrange("p h t d -> p h (t d)")

        def heads(ap):
            return ap.rearrange("p (h d) -> p h d", h=HEADS)

        with nc.Block() as block:

            @block.sync
            def _(sp):
                sp.dma_start(wo[:, :, :], io["woT"].rearrange("(c p) n -> p c n", p=P)).then_inc(wo_in, 16)
                sp.dma_start(bo[:, :], io["bo"].partition_broadcast(P)).then_inc(wo_in, 16)
                for h in range(2):
                    sp.dma_start(xs[h][:, :], dram["xs"][h * P:(h + 1) * P, :]).then_inc(xs_in[h], 16)
                for e in range(NE):
                    sp.dma_start(w1[:, e], io["w1"][e].rearrange("(c p) f -> p c f", p=P)).then_inc(w1_in, 16)
                for e in range(NE):
                    sp.dma_start(w2[:, e], io["w2"][e].rearrange("(c p) d -> p c d", p=P)).then_inc(w2_in, 16)

                def load(T, h):
                    sp.wait_ge(x_tp, T + 1)
                    sp.dma_start(xs[h][:, :], dram["xs"][bass.ds((T + 2) * P, P), :]).then_inc(xs_in[h], 16)

                def store(T, h):
                    sp.wait_ge(y_evac, T + 1)
                    sp.dma_start(dram["ys"][bass.ds(T * P, P), :], ys[h][:, :]).then_inc(y_out[h], 16)

                with sp.Fori(0, LAST // 2 - 1) as pair_i:
                    T0 = pair_i * 2
                    for h in range(2):
                        load(T0 + h, h)
                    for h in range(2):
                        store(T0 + h, h)
                load(LAST - 2, 0)
                store(LAST - 2, 0)
                store(LAST - 1, 1)
                store(LAST, 0)
                for h in range(2):
                    sp.wait_ge(y_out[h], 16 * (LAST // 2 + 1 - h))

            @block.tensor
            def _(pe):
                def turn_attn(t, h):
                    pe.wait_ge(at_ready, t + 1)
                    wait(pe, a_evac, t - 1)
                    for d in range(DC):
                        mm = nc.tensor.transpose(pa[h][:, d * P:(d + 1) * P], at[h][:, d * P:(d + 1) * P], con["ident"][:, :])
                    mm.then_inc(a_tp, 1)

                def project_out(t, h):
                    pe.wait_ge(a_evac, t + 1)
                    wait(pe, o_evac, t - 1)
                    for d in range(DC):
                        mm = nc.tensor.matmul(po[h][:, 0:D], aT[h][:, d, :], wo[:, d, :], start=(d == 0), stop=(d == DC - 1))
                    mm.then_inc(o_mm, 1)

                pe.wait_ge(wo_in, 32)
                turn_attn(0, 0)
                turn_attn(1, 1)
                project_out(0, 0)
                with pe.Fori(1, TILES // 2) as pair_i:
                    t0 = pair_i * 2
                    turn_attn(t0, 0)
                    project_out(t0 - 1, 1)
                    turn_attn(t0 + 1, 1)
                    project_out(t0, 0)
                project_out(TILES - 1, 1)

                def turn_x(T, xs_count, h):
                    pe.wait_ge(xs_in[h], xs_count)
                    wait(pe, x_evac, T)
                    for d in range(DC):
                        mm = nc.tensor.transpose(px[:, d * P:(d + 1) * P], xs[h][:, d * P:(d + 1) * P], con["ident"][:, :])
                    mm.then_inc(x_tp, 1)

                def hidden(T, h, e, half):
                    if half == 0:
                        pe.wait_ge(x_evac, T + 1)
                    wait(pe, gelu_done, T * 2 + half - 1)
                    for d in range(DC):
                        mm = nc.tensor.matmul(ph[half][:, :], xsT[h][:, d, :], w1[:, e, d, half * 512:(half + 1) * 512],
                                              start=(d == 0), stop=(d == DC - 1))
                    mm.then_inc(h_mm, 1)

                def turn_hidden(T, h, half):
                    pe.wait_ge(gelu_done, T * 2 + (half + 1))
                    wait(pe, hT_evac, T * 2 + half - 1)
                    for k in range(4):
                        j = half * 4 + k
                        mm = nc.tensor.transpose(pt[half][:, k * P:(k + 1) * P], hid[h][:, j * P:(j + 1) * P], con["ident"][:, :])
                    mm.then_inc(h_tp, 1)

                def output(T, h, e):
                    wait(pe, y_evac, T)
                    for j in range(FC):
                        if j % 4 == 0:
                            pe.wait_ge(hT_evac, T * 2 + (j // 4 + 1))
                        mm = nc.tensor.matmul(py[:, 0:D], hT[h][:, j, :], w2[:, e, j, :], start=(j == 0), stop=(j == FC - 1))
                    mm.then_inc(y_mm, 1)

                def expert(T):
                    return pe.value_load(expert_i[0:1, bass.ds(T, 1)], min_val=0, max_val=NE - 1)

                def step(T, h, e, e_before, next_count):
                    for half in range(2):
                        hidden(T, h, e, half)
                        turn_hidden(T - 1, 1 - h, half)
                    if next_count is not None:
                        turn_x(T + 1, next_count, 1 - h)
                    output(T - 1, 1 - h, e_before)

                wait(pe, o_evac, TILES)
                turn_x(0, 16, 0)
                pe.wait_ge(w1_in, 16 * NE)
                e0 = expert(0)
                for half in range(2):
                    hidden(0, 0, e0, half)
                turn_x(1, 16, 1)
                pe.wait_ge(w2_in, 16 * NE)
                step(1, 1, expert(1), e0, 32)
                with pe.Fori(1, LAST // 2) as pair_i:
                    T0 = pair_i * 2
                    e_last, e0, e1 = expert(T0 - 1), expert(T0), expert(T0 + 1)
                    step(T0, 0, e0, e_last, T0 * 8 + 16)
                    step(T0 + 1, 1, e1, e0, T0 * 8 + 32)
                e_last, e0 = expert(LAST - 1), expert(LAST)
                step(LAST, 0, e0, e_last, None)
                for half in range(2):
                    turn_hidden(LAST, 0, half)
                output(LAST, 0, e0)

            @block.scalar
            def _(act):
                def turn_attn(t, h):
                    wait(act, o_mm, t - 1)
                    act.wait_ge(a_tp, t + 1)
                    nc.scalar.activation(aT[h][:, :, :], pa[h][:, 0:D].rearrange("p (c m) -> p c m", c=DC), ACT.Copy).then_inc(a_evac, 1)

                turn_attn(0, 0)
                turn_attn(1, 1)
                with act.Fori(1, TILES // 2) as pair_i:
                    t0 = pair_i * 2
                    turn_attn(t0, 0)
                    turn_attn(t0 + 1, 1)

                def hidden(T, T0, h):
                    for half in range(2):
                        act.wait_ge(h_mm, T0 * 2 + (h * 2 + half + 1))
                        wait(act, h_tp, T * 2 + half - 3)
                        nc.scalar.activation(hid[h][:, half * 512:(half + 1) * 512], ph[half][:, :], ACT.Gelu_apprx_tanh).then_inc(gelu_done, 1)

                hidden(0, 0, 0)
                hidden(1, 0, 1)
                with act.Fori(1, LAST // 2) as pair_i:
                    T0 = pair_i * 2
                    hidden(T0, T0, 0)
                    hidden(T0 + 1, T0, 1)
                hidden(LAST, LAST, 0)

            @block.vector
            def _(dve):
                def gather(t, h):
                    wait(dve, a_tp, t - 1)
                    nc.vector.tensor_copy(heads(at[h][:, :]), token_tile(t)).then_inc(at_ready, 1)

                def add_bias(t, h):
                    dve.wait_ge(o_mm, t + 1)
                    nc.vector.tensor_tensor(token_tile(t), heads(po[h][:, 0:D]), heads(bo[:, :]), ALU.add).then_inc(o_evac, 1)

                dve.wait_ge(wo_in, 32)
                gather(0, 0)
                gather(1, 1)
                with dve.Fori(1, TILES // 2) as pair_i:
                    t0 = pair_i * 2
                    gather(t0, 0)
                    add_bias(t0 - 2, 0)
                    gather(t0 + 1, 1)
                    add_bias(t0 - 1, 1)
                add_bias(TILES - 2, 0)
                add_bias(TILES - 1, 1)

                def turn_x(T, h):
                    dve.wait_ge(x_tp, T + 1)
                    wait(dve, h_mm, T * 2 - 2)
                    nc.vector.tensor_copy(xsT[h][:, :, :], px[:, 0:D].rearrange("p (c m) -> p c m", c=DC)).then_inc(x_evac, 1)

                def turn_hidden(T, h):
                    for half in range(2):
                        dve.wait_ge(h_tp, T * 2 + (half + 1))
                        wait(dve, y_mm, T - 1)
                        nc.vector.tensor_copy(hT[h][:, half * 4:(half + 1) * 4, :], pt[half][:, :].rearrange("p (c m) -> p c m", c=4)).then_inc(hT_evac, 1)

                def output(T, h, out_count):
                    dve.wait_ge(y_mm, T + 1)
                    wait(dve, y_out[h], out_count)
                    nc.vector.tensor_copy(ys[h][:, :], py[:, 0:D]).then_inc(y_evac, 1)

                def step(T, h, out_count, more=True):
                    turn_hidden(T - 1, 1 - h)
                    if more:
                        turn_x(T + 1, 1 - h)
                    output(T - 1, 1 - h, out_count)

                turn_x(0, 0)
                turn_x(1, 1)
                step(1, 1, 0)
                step(2, 0, 0)
                step(3, 1, 16)
                with dve.Fori(2, LAST // 2) as pair_i:
                    T0 = pair_i * 2
                    step(T0, 0, T0 * 8 - 16)
                    step(T0 + 1, 1, T0 * 8)
                step(LAST, 0, LAST * 8 - 16, more=False)
                turn_hidden(LAST, 0)
                output(LAST, 0, LAST * 8)


def finish(nc, io, dram, attn, pos_i, out):
    GROUP = 4
    GROUPS = TILES // GROUP
    with ExitStack() as ctx:
        def sb(name, shape, dt):
            return ctx.enter_context(nc.sbuf_tensor(name, shape, dt))

        def sem(name):
            return ctx.enter_context(nc.semaphore(name))

        x_in = sb("x_in", [P, TILES, D], F32)
        y_all = sb("y_all", [P, TILES, D], F32)

        x_ld = [sem(f"x_ld{g}") for g in range(GROUPS)]
        y_ld = [sem(f"y_ld{g}") for g in range(GROUPS)]
        gate_ready = sem("gate_ready")
        gated = sem("gated")
        res_ready = sem("res_ready")
        stored = sem("stored")
        x_v = io["x"].rearrange("b (t p) d -> p (b t) d", p=P)
        out_v = out.rearrange("b (t p) d -> p (b t) d", p=P)

        def tiles(g):
            return slice(g * GROUP, (g + 1) * GROUP)

        with nc.Block() as block:

            @block.sync
            def _(sp):
                for g in range(GROUPS):
                    sp.dma_start(x_in[:, tiles(g), :], x_v[:, tiles(g), :]).then_inc(x_ld[g], 16)
                for g in range(GROUPS):
                    sp.wait_ge(res_ready, g + 1)
                    sp.dma_start(out_v[:, tiles(g), :], y_all[:, tiles(g), :]).then_inc(stored, 16)
                sp.wait_ge(stored, 16 * GROUPS)

            @block.gpsimd
            def _(pool):
                for t in range(TILES):
                    pool.indirect_dma_start(out=y_all[:, t, :], out_offset=None, in_=dram["ys"][:, :],
                                            in_offset=bass.IndirectOffsetOnAxis(ap=pos_i[:, t:t + 1], axis=0)).then_inc(y_ld[t // GROUP], 16)

            @block.scalar
            def _(act):
                for g in range(GROUPS):
                    act.wait_ge(y_ld[g], 16 * GROUP)
                    nc.scalar.activation(y_all[:, tiles(g), :], y_all[:, tiles(g), :], ACT.Silu).then_inc(gate_ready, 1)

            @block.vector
            def _(dve):
                s_all = attn[:, :, :, :].rearrange("p (h b) i d -> p h (b i) d", b=B)
                for g in range(GROUPS):
                    dve.wait_ge(gate_ready, g + 1)
                    y = y_all[:, tiles(g), :]
                    for k in range(GROUP):
                        t = g * GROUP + k
                        ins = nc.vector.tensor_tensor(y_all[:, t, :].rearrange("p (h d) -> p h d", h=HEADS),
                                                      y_all[:, t, :].rearrange("p (h d) -> p h d", h=HEADS), s_all[:, :, t, :], ALU.mult)
                    ins.then_inc(gated, 1)
                    dve.wait_ge(gated, g + 1)
                    dve.wait_ge(x_ld[g], 16)
                    nc.vector.tensor_tensor(y, y, x_in[:, tiles(g), :], ALU.add).then_inc(res_ready, 1)


def build(nc, io, out):
    def scratch(name, shape, dt):
        return nc.dram_tensor(name, shape, dt, kind="Internal").ap()

    dram = dict(
        q_stack=scratch("q_stack", [HEADS, ROWS, B * S], BF16),
        k_stack=scratch("k_stack", [HEADS, ROWS, B * S], BF16),
        v=scratch("v_pairs", [NBH, P, NB, HD], F32),
        rel=scratch("rel_scores", [2, NB, P, WIN], F32),
        band_p=scratch("band_probs", [2, NB, P, BAND], F32),
        xn=scratch("x_norm", [TILES * P, D], F32),
        xs=scratch("x_sorted", [XT * P, D], F32),
        ys=scratch("y_sorted", [XT * P, D], F32),
    )
    with ExitStack() as ctx:
        def sb(name, shape, dt):
            return ctx.enter_context(nc.sbuf_tensor(name, shape, dt))

        con = dict(ident=sb("ident", [P, P], F32), ident_bf=sb("ident_bf", [P, P], BF16), rel_k=sb("rel_k", [ROWS, RELS], BF16))
        pos_i = sb("pos_i", [P, TILES], I32)
        expert_i = sb("expert_i", [P, XT], I32)
        with ExitStack() as early:
            lg_all = early.enter_context(nc.sbuf_tensor("lg_all", [P, TILES, NE], F32))
            project(nc, io, dram, con, lg_all)
            route(nc, lg_all, pos_i, expert_i)
        attn = sb("attn", [P, NBH, NB, HD], F32)
        attend(nc, io, dram, con, pos_i, attn)
        experts(nc, io, dram, con, attn, expert_i)
        finish(nc, io, dram, attn, pos_i, out)


_INS = ["x", "wqT", "wkT", "wvT", "wg", "bq", "bk", "bv", "bg", "rel_kT", "rel_v", "woT", "bo", "w1", "w2"]


def kernel(**inputs):
    import numpy as _np
    import concourse.bacc as _bacc
    from concourse import mybir as _mybir
    from concourse.bass_utils import run_bass_kernel_spmd as _run

    a = {k: _np.asarray(v) for k, v in inputs.items()}
    host = {
        "x": a["L0_attn_x"], "wqT": a["L0_attn_Wq"].T, "wkT": a["L0_attn_Wk"].T, "wvT": a["L0_attn_Wv"].T, "wg": a["L0_ffn_Wg"],
        "bq": a["L0_attn_bq"].reshape(DC, P).T, "bk": a["L0_attn_bk"].reshape(DC, P).T, "bv": a["L0_attn_bv"], "bg": a["L0_ffn_bg"],
        "rel_kT": a["L0_attn_rel_k"].T, "rel_v": a["L0_attn_rel_v"], "woT": a["L0_attn_Wo"].T, "bo": a["L0_attn_bo"],
        "w1": a["L0_ffn_W1"], "w2": a["L0_ffn_W2"],
    }
    nc = _bacc.Bacc("TRN2", target_bir_lowering=False, num_devices=1)
    nc.disable_value_cache = True
    arrays, io = {}, {}
    for name in _INS:
        arr = _np.ascontiguousarray(host[name])
        arrays[f"in_{name}_dram"] = arr
        io[name] = nc.dram_tensor(f"in_{name}_dram", arr.shape, _mybir.dt.from_np(arr.dtype), kind="ExternalInput").ap()
    out = nc.dram_tensor("out_dram", (B, S, D), F32, kind="ExternalOutput").ap()
    build(nc, io, out)
    r = _run(nc, [arrays], core_ids=[0])
    return r.results[0]["out_dram"]
```
